# Optimizing a Trainium2 kernel written in Bass

```python
import numpy as np
import jax
import jax.numpy as jnp

def _softmax(x, axis=-1):
    return jax.nn.softmax(x, axis=axis)

def _gelu(x):
    return jax.nn.gelu(x, approximate=True)

def _silu(x):
    return jax.nn.silu(x)

def _sigmoid(x):
    return jax.nn.sigmoid(x)

def _layernorm(x, axis=-1, eps=1e-05):
    m = jnp.mean(x, axis=axis, keepdims=True)
    v = jnp.var(x, axis=axis, keepdims=True)
    return (x - m) / jnp.sqrt(v + eps)

def _scatter_add(tgt, idx, src, axis=0):
    return tgt.at[idx].add(src)

def _segment_sum(src, seg, n):
    return jax.ops.segment_sum(src, seg, n)
kernel_name = 'mk_macaron_d1_jaxref_r8_80d7d2'

def setup_inputs(seed: int=0):
    np.random.seed(seed)
    _w = jnp.asarray

    def _L0_attn_setup():
        import jax, jax.numpy as jnp
        import numpy as np
        DIM = 128
        HEADS = 16
        HEAD_DIM = DIM // HEADS
        B, N = (4, 512)
        key = jax.random.key(seed)
        ks = jax.random.split(key, 9)
        s = 1.0 / np.sqrt(DIM)
        return {'x': jax.random.normal(ks[0], (B, N, DIM), dtype=jnp.float32), 'Wq': jax.random.uniform(ks[1], (DIM, DIM), jnp.float32, -s, s), 'bq': jax.random.uniform(ks[2], (DIM,), jnp.float32, -s, s), 'Wk': jax.random.uniform(ks[3], (DIM, DIM), jnp.float32, -s, s), 'bk': jax.random.uniform(ks[4], (DIM,), jnp.float32, -s, s), 'Wv': jax.random.uniform(ks[5], (DIM, DIM), jnp.float32, -s, s), 'bv': jax.random.uniform(ks[6], (DIM,), jnp.float32, -s, s), 'Wp': jax.random.uniform(ks[7], (DIM, DIM), jnp.float32, -s, s), 'bp': jax.random.uniform(ks[8], (DIM,), jnp.float32, -s, s)}
    _L0_attn_in = _L0_attn_setup()

    def _L0_ffn_setup():
        import jax, jax.numpy as jnp
        import numpy as np
        DIM = 128
        INTER = 176
        N_EXPERTS = 16
        TOPK = 2
        N_SHARED = 2
        SHARED_INTER = N_SHARED * INTER
        ROUTE_SCALE = 1.0
        key = jax.random.key(seed)
        ks = jax.random.split(key, 16)
        s = 0.02
        return {'x': jax.random.normal(ks[0], (2, 256, DIM), dtype=jnp.float32), 'gate_w': jax.random.normal(ks[1], (DIM, N_EXPERTS), dtype=jnp.float32) * s, 'gate_b': jnp.zeros((N_EXPERTS,), dtype=jnp.float32), 'w1': jax.random.normal(ks[2], (N_EXPERTS, DIM, INTER), dtype=jnp.float32) * s, 'b1': jnp.zeros((N_EXPERTS, INTER), dtype=jnp.float32), 'w3': jax.random.normal(ks[3], (N_EXPERTS, DIM, INTER), dtype=jnp.float32) * s, 'b3': jnp.zeros((N_EXPERTS, INTER), dtype=jnp.float32), 'w2': jax.random.normal(ks[4], (N_EXPERTS, INTER, DIM), dtype=jnp.float32) * s, 'b2': jnp.zeros((N_EXPERTS, DIM), dtype=jnp.float32), 'sw1': jax.random.normal(ks[5], (DIM, SHARED_INTER), dtype=jnp.float32) * s, 'sb1': jax.random.normal(ks[6], (SHARED_INTER,), dtype=jnp.float32) * s, 'sw3': jax.random.normal(ks[7], (DIM, SHARED_INTER), dtype=jnp.float32) * s, 'sb3': jax.random.normal(ks[8], (SHARED_INTER,), dtype=jnp.float32) * s, 'sw2': jax.random.normal(ks[9], (SHARED_INTER, DIM), dtype=jnp.float32) * s, 'sb2': jax.random.normal(ks[10], (DIM,), dtype=jnp.float32) * s}
    _L0_ffn_in = _L0_ffn_setup()
    _d = {'L0_attn_x': _L0_attn_in['x'], 'L0_attn_Wq': _L0_attn_in['Wq'], 'L0_attn_bq': _L0_attn_in['bq'], 'L0_attn_Wk': _L0_attn_in['Wk'], 'L0_attn_bk': _L0_attn_in['bk'], 'L0_attn_Wv': _L0_attn_in['Wv'], 'L0_attn_bv': _L0_attn_in['bv'], 'L0_attn_Wp': _L0_attn_in['Wp'], 'L0_attn_bp': _L0_attn_in['bp'], 'L0_ffn_gate_w': _L0_ffn_in['gate_w'], 'L0_ffn_gate_b': _L0_ffn_in['gate_b'], 'L0_ffn_w1': _L0_ffn_in['w1'], 'L0_ffn_b1': _L0_ffn_in['b1'], 'L0_ffn_w3': _L0_ffn_in['w3'], 'L0_ffn_b3': _L0_ffn_in['b3'], 'L0_ffn_w2': _L0_ffn_in['w2'], 'L0_ffn_b2': _L0_ffn_in['b2'], 'L0_ffn_sw1': _L0_ffn_in['sw1'], 'L0_ffn_sb1': _L0_ffn_in['sb1'], 'L0_ffn_sw3': _L0_ffn_in['sw3'], 'L0_ffn_sb3': _L0_ffn_in['sb3'], 'L0_ffn_sw2': _L0_ffn_in['sw2'], 'L0_ffn_sb2': _L0_ffn_in['sb2']}
    _x0 = _d['L0_attn_x']
    _d['L0_attn_x'] = jax.random.normal(jax.random.fold_in(jax.random.key(seed), 1), (8, 1024, 128), dtype=_x0.dtype)
    del _x0
    return _d

def reference(L0_attn_x, L0_attn_Wq, L0_attn_bq, L0_attn_Wk, L0_attn_bk, L0_attn_Wv, L0_attn_bv, L0_attn_Wp, L0_attn_bp, L0_ffn_gate_w, L0_ffn_gate_b, L0_ffn_w1, L0_ffn_b1, L0_ffn_w3, L0_ffn_b3, L0_ffn_w2, L0_ffn_b2, L0_ffn_sw1, L0_ffn_sb1, L0_ffn_sw3, L0_ffn_sb3, L0_ffn_sw2, L0_ffn_sb2):

    def _L0_attn_ref(x, Wq, bq, Wk, bk, Wv, bv, Wp, bp):
        import jax, jax.numpy as jnp
        import numpy as np
        DIM = 128
        HEADS = 16
        HEAD_DIM = DIM // HEADS
        B, N = (4, 512)
        b, n, d = x.shape
        q = x @ Wq + bq
        k = x @ Wk + bk
        v = x @ Wv + bv
        split = lambda t: t.reshape(b, n, HEADS, HEAD_DIM).transpose(0, 2, 1, 3)
        q, k, v = (split(q), split(k), split(v))
        q = jax.nn.elu(q) + 1.0
        k = jax.nn.elu(k) + 1.0
        kv = jnp.einsum('bhnd,bhnf->bhdf', k, v)
        out = jnp.einsum('bhnd,bhdf->bhnf', q, kv)
        out = out.transpose(0, 2, 1, 3).reshape(b, n, d)
        return out @ Wp + bp

    def _L0_ffn_ref(x, gate_w, gate_b, w1, b1, w3, b3, w2, b2, sw1, sb1, sw3, sb3, sw2, sb2):
        import jax, jax.numpy as jnp
        import numpy as np
        DIM = 128
        INTER = 176
        N_EXPERTS = 16
        TOPK = 2
        N_SHARED = 2
        SHARED_INTER = N_SHARED * INTER
        ROUTE_SCALE = 1.0
        shape = x.shape
        xf = x.reshape(-1, DIM)
        logits = xf @ gate_w + gate_b
        scores = jax.nn.softmax(logits.astype(jnp.float32), axis=-1)
        top_vals, top_idx = jax.lax.top_k(scores, TOPK)
        weights = (top_vals * ROUTE_SCALE).astype(x.dtype)
        cw = (jax.nn.one_hot(top_idx, N_EXPERTS, dtype=x.dtype) * weights[..., None]).sum(axis=1)
        h = jnp.einsum('td,edh->teh', xf, w1) + b1
        g = jnp.einsum('td,edh->teh', xf, w3) + b3
        a = jax.nn.silu(h) * g
        y = jnp.einsum('teh,ehd,te->td', a, w2, cw) + cw @ b2
        z = jax.nn.silu(xf @ sw1 + sb1) * (xf @ sw3 + sb3) @ sw2 + sb2
        return (y + z).reshape(shape)
    x = L0_attn_x
    x = x + 0.5 * _L0_ffn_ref(_layernorm(x, axis=-1), L0_ffn_gate_w, L0_ffn_gate_b, L0_ffn_w1, L0_ffn_b1, L0_ffn_w3, L0_ffn_b3, L0_ffn_w2, L0_ffn_b2, L0_ffn_sw1, L0_ffn_sb1, L0_ffn_sw3, L0_ffn_sb3, L0_ffn_sw2, L0_ffn_sb2)
    x = x + _L0_attn_ref(_layernorm(x, axis=-1), L0_attn_Wq, L0_attn_bq, L0_attn_Wk, L0_attn_bk, L0_attn_Wv, L0_attn_bv, L0_attn_Wp, L0_attn_bp)
    x = x + 0.5 * _L0_ffn_ref(_layernorm(x, axis=-1), L0_ffn_gate_w, L0_ffn_gate_b, L0_ffn_w1, L0_ffn_b1, L0_ffn_w3, L0_ffn_b3, L0_ffn_w2, L0_ffn_b2, L0_ffn_sw1, L0_ffn_sb1, L0_ffn_sw3, L0_ffn_sb3, L0_ffn_sw2, L0_ffn_sb2)
    return x

_drawn_inputs = setup_inputs


def setup_inputs(seed=0):
    import zlib

    import numpy as np

    out = dict(_drawn_inputs(seed))
    spreads = {'L0_ffn_gate_b': (0.0, 0.469),
     'L0_ffn_b1': (0.0, 0.8),
     'L0_ffn_b3': (0.0, 0.8),
     'L0_ffn_b2': (0.0, 0.349)}
    factors = {'L0_attn_bq': 4.821,
     'L0_attn_bk': 4.215,
     'L0_attn_bp': 200.0,
     'L0_ffn_gate_w': 8.0,
     'L0_ffn_w1': 8.0,
     'L0_ffn_w3': 8.0,
     'L0_ffn_w2': 8.0,
     'L0_ffn_sw1': 8.0,
     'L0_ffn_sb1': 8.0,
     'L0_ffn_sw3': 8.0,
     'L0_ffn_sb3': 8.0,
     'L0_ffn_sw2': 8.0}
    for name, (base, spread) in spreads.items():
        noise = np.random.default_rng([zlib.crc32(name.encode()), seed]).standard_normal(out[name].shape)
        drawn = base * np.exp(spread * noise) if base else spread * noise
        out[name] = jnp.asarray(drawn.astype(out[name].dtype))
    for name, factor in factors.items():
        out[name] = (out[name] * factor).astype(out[name].dtype)
    return out
```

```python
from contextlib import ExitStack, contextmanager

import concourse.bass as bass
from concourse import mybir

F32 = mybir.dt.float32
F32R = mybir.dt.float32r
BF16 = mybir.dt.bfloat16
I32 = mybir.dt.int32
ACT = mybir.ActivationFunctionType
ALU = mybir.AluOpType
AX = mybir.AxisListType.X
ds = bass.ds

P = 128
D = 128
HEAD_DIM = 8
E = 16
INTER = 176
UP = 2 * INTER
SH = 352
GROUPS = 8
GT = 8
TILES = GROUPS * GT
TOKENS = TILES * P
K_TOP = 2
SLOT_TILES = TOKENS * K_TOP // P + E
PAIRS = SLOT_TILES // 2
ROW = D + 2
CHUNK = 4
CHUNKS = TILES // CHUNK
FEAT = [(0, 128), (128, 128), (256, 96)]
A0 = 96
A1 = INTER - A0
EPS = 1e-5
RING = 6
PADS = 2 * RING
MAGIC = float(3 << 22)


@contextmanager
def phase(nc):
    sems = []

    def sem(name):
        sems.append(nc.alloc_semaphore(name=name))
        return sems[-1]
    yield sem
    nc.clear_and_free_semaphores(sems)
    nc.all_engine_barrier()


def wait(eng, sem, value):
    if not (isinstance(value, int) and value <= 0):
        eng.wait_ge(sem, value)


def build(nc, x, wq, bq, wk, bk, wv, bv, wp, bp, gate_w, gate_b, w1, b1, w3, b3, w2, b2,
          sw1, sb1, sw3, sb3, sw2, sb2, out, xs_dram, ys_dram, resid, x3):
    top = ExitStack()
    with top:
        def sb(name, shape, dt=F32, ctx=top):
            return ctx.enter_context(nc.sbuf_tensor(name, shape, dt))

        def ps(name, shape, ctx, dt=F32):
            return ctx.enter_context(nc.psum_tensor(name, shape, dt))

        def sem(name):
            return top.enter_context(nc.semaphore(name))

        class W:
            pass

        k = W()
        k.w13h, k.w13l = sb("w13h", [P, E * UP], F32R), sb("w13l", [P, E * UP], F32R)
        k.w2hl = sb("w2hl", [A0 + 1, 2, E, 2 * D], F32R)
        k.b13 = sb("b13", [33, E * UP], F32R)
        k.sw13h, k.sw13l = sb("sw13h", [P, 2 * SH], F32R), sb("sw13l", [P, 2 * SH], F32R)
        k.sw2hl = sb("sw2hl", [P, 3, 2 * D], F32R)
        k.sb13 = sb("sb13", [P, 2, 3])
        k.wq, k.wkv, k.wp = sb("wq_s", [P, D]), sb("wkv_s", [P, 2 * D]), sb("wp_s", [P, D])
        k.bkvp = sb("bkvp", [33, 3 * D], F32R)
        k.bq = sb("bq_s", [P, 1])
        k.gw, k.gb = sb("gw_s", [P, E]), sb("gb_s", [1, E])
        k.ident = sb("ident", [P, P])
        k.onesr = sb("onesr", [33, P], F32R)
        k.ones1 = sb("ones1", [1, P])
        k.tri, k.onesb = sb("tri", [P, P], BF16), sb("onesb", [P, P], BF16)
        k.blockdiag = sb("blockdiag", [P, P])
        k.iota_e, k.ones_e = sb("iota_e", [P, E]), sb("ones_e", [P, E])
        k.iota_j = sb("iota_j", [1, SLOT_TILES])
        k.carry = sb("carry", [P, E * TILES])
        k.nhalf = sb("nhalf", [P, GT])
        k.tile_expert = sb("tile_expert", [1, SLOT_TILES], I32)
        k.pads = sb("pads", [P, PADS, ROW])
        k.s_fill = [sem("fill0"), sem("fill1")]
        k.xs2 = xs_dram[1]

        setup(nc, k, sb, ps, xs_dram, wq, bq, wk, bk, wv, bv, wp, bp, gate_w, gate_b,
              w1, b1, w3, b3, w2, b2, sw1, sb1, sw3, sb3, sw2, sb2)
        x_v = x.rearrange("b (p i) d -> p b i d", i=GT)
        out_v = out.rearrange("b (p i) d -> p b i d", i=GT)
        resid_v = resid.rearrange("b (p i) d -> p b i d", i=GT)
        x3_v = x3.rearrange("b (p i) d -> p b i d", i=GT)
        ys_v = ys_dram.rearrange("(r c) d -> r (c d)", c=K_TOP)[0:TOKENS, :]
        ys_v = ys_v.rearrange("(b p i) d -> p b i d", i=GT, p=P)
        for n, src in enumerate((x_v, x3_v)):
            with ExitStack() as ctx:
                xrow = sb(f"xrow{n}", [P, TILES, ROW], ctx=ctx)
                logits = sb(f"logits{n}", [P, TILES * E], ctx=ctx)
                norm_and_gate(nc, k, sb, ps, n, src, xrow, logits)
                route_and_share(nc, k, sb, ps, n, src, xrow, logits, xs_dram[n], resid_v)
            experts(nc, k, sb, ps, n, xs_dram[n], ys_dram)
            if n == 0:
                attention(nc, k, sb, ps, resid_v, ys_v, x3_v)
        combine(nc, k, sb, resid_v, ys_v, out_v)


def fill(eng, k, xs, n):
    rows = xs.rearrange("(a j p) c -> a p j c", j=PADS, p=P)
    for a in range(SLOT_TILES // PADS):
        eng.dma_start(rows[a], k.pads[:]).then_inc(k.s_fill[n], 16)


def setup(nc, k, sb, ps, xs_dram, wq, bq, wk, bk, wv, bv, wp, bp, gate_w, gate_b,
          w1, b1, w3, b3, w2, b2, sw1, sb1, sw3, sb3, sw2, sb2):
    with phase(nc) as sem, ExitStack() as ctx:
        raw13 = sb("raw13", [P, E, UP], ctx=ctx)
        raw2 = sb("raw2", [A0 + 1, 2, E, D], ctx=ctx)
        rawb = sb("rawb", [33, E, UP], ctx=ctx)
        raws13 = sb("raws13", [P, 2 * SH], ctx=ctx)
        raws2 = sb("raws2", [P, 3, D], ctx=ctx)
        rawa = sb("rawa", [33, 3 * D], ctx=ctx)
        zeroed, loaded, small = sem("su_zeroed"), sem("su_loaded"), sem("su_small")
        hi, lo, built, base = sem("su_hi"), sem("su_lo"), sem("su_built"), sem("su_base")
        pads_ready = sem("su_pads")
        halves = [
            (raw13[:].rearrange("p e n -> p (e n)"), k.w13h[:], k.w13l[:]),
            (raw2[:, 0], k.w2hl[:, 0, :, 0:D], k.w2hl[:, 0, :, D:2 * D]),
            (raw2[0:A0, 1], k.w2hl[0:A0, 1, :, 0:D], k.w2hl[0:A0, 1, :, D:2 * D]),
            (raws13[:], k.sw13h[:], k.sw13l[:]),
            (raws2[:, 0:2], k.sw2hl[:, 0:2, 0:D], k.sw2hl[:, 0:2, D:2 * D]),
            (raws2[0:97, 2], k.sw2hl[0:97, 2, 0:D], k.sw2hl[0:97, 2, D:2 * D]),
        ]
        bias_hi = [(rawb[:].rearrange("p e n -> p (e n)"), k.b13), (rawa[:], k.bkvp)]
        loads = [
            (raw13[:, :, 0:INTER], w1.rearrange("e d n -> d e n")),
            (raw13[:, :, INTER:UP], w3.rearrange("e d n -> d e n")),
            (raw2[0:A0, 0], w2[:, 0:A0, :].rearrange("e k d -> k e d")),
            (raw2[2 * A0 - INTER:A0, 1], w2[:, A0:INTER, :].rearrange("e k d -> k e d")),
            (raw2[A0:A0 + 1, 0], b2.rearrange("(a e) d -> a e d", a=1)),
            (raws13[:, 0:SH], sw1), (raws13[:, SH:2 * SH], sw3),
            (raws2[:, 0:2], sw2[0:256, :].rearrange("(c p) d -> p c d", p=P)),
            (raws2[0:96, 2], sw2[256:SH, :]),
            (raws2[96:97, 2], sb2.rearrange("(a n) -> a n", a=1)),
        ]
        for r in (0, 32):
            loads += [(rawb[r:r + 1, :, 0:INTER], b1.rearrange("(a e) n -> a e n", a=1)),
                      (rawb[r:r + 1, :, INTER:UP], b3.rearrange("(a e) n -> a e n", a=1))]
            loads += [(rawa[r:r + 1, m * D:(m + 1) * D], b.rearrange("(a n) -> a n", a=1))
                      for m, b in enumerate((bk, bv, bp))]
        smalls = [(k.wq[:], wq), (k.wkv[:, 0:D], wk), (k.wkv[:, D:2 * D], wv), (k.wp[:], wp),
                  (k.bq[:], bq.rearrange("(p a) -> p a", a=1)), (k.gw[:], gate_w),
                  (k.gb[:], gate_b.rearrange("(a n) -> a n", a=1))]
        for m, b in enumerate((sb1, sb3)):
            smalls += [(k.sb13[0:w, m, f:f + 1], b[o:o + w].rearrange("(p a) -> p a", a=1))
                       for f, (o, w) in enumerate(FEAT)]
        with nc.Block() as block:
            @block.sync
            def _(sp):
                sp.wait_ge(zeroed, 3)
                for dst, src in loads:
                    sp.dma_start(dst, src).then_inc(loaded, 16)
                sp.wait_ge(pads_ready, 1)
                fill(sp, k, xs_dram[0], 0)
                sp.wait_ge(k.s_fill[0], 16 * SLOT_TILES // PADS)
                sp.wait_ge(small, 16 * len(smalls))

            @block.gpsimd
            def _(pool):
                pool.memset(k.ident[:], 0.0)
                pool.memset(k.tri[:], 1.0)
                pool.memset(k.blockdiag[:], 1.0)
                pool.memset(k.onesb[:], 1.0)
                pool.memset(k.ones1[:], 1.0)
                pool.memset(k.ones_e[:], 1.0)
                pool.memset(k.nhalf[:], -0.5)
                pool.memset(k.pads[:], 0.0)
                pool.memset(k.carry[:], 1.0).then_inc(base, 1)
                pool.wait_ge(base, 1)
                pool.affine_select(out=k.ident[:], in_=k.ident[:], compare_op=ALU.not_equal,
                                   fill=1.0, base=0, pattern=[[-1, P]], channel_multiplier=1)
                pool.affine_select(out=k.tri[:], in_=k.tri[:], compare_op=ALU.is_ge, fill=0.0,
                                   base=-1, pattern=[[1, P]], channel_multiplier=-1)
                heads = k.blockdiag[:].rearrange("p (a c) -> p a c", c=HEAD_DIM)
                pool.affine_select(out=heads, in_=heads, compare_op=ALU.is_ge, fill=0.0, base=0,
                                   pattern=[[-HEAD_DIM, D // HEAD_DIM], [0, HEAD_DIM]],
                                   channel_multiplier=1).then_inc(base, 1)
                pool.wait_ge(base, 2)
                pool.affine_select(out=heads, in_=heads, compare_op=ALU.is_ge, fill=0.0,
                                   base=HEAD_DIM - 1,
                                   pattern=[[HEAD_DIM, D // HEAD_DIM], [0, HEAD_DIM]],
                                   channel_multiplier=-1)
                pool.memset(k.carry[:].rearrange("p (e t) -> p e t", e=E)[:, :, 0:1], 0.0)
                pool.iota(k.iota_e[:], pattern=[[1, E]], base=0, channel_multiplier=0,
                          allow_small_or_imprecise_dtypes=True)
                pool.iota(k.iota_j[:], pattern=[[1, SLOT_TILES]], base=0, channel_multiplier=0,
                          allow_small_or_imprecise_dtypes=True)
                pool.iota(k.pads[:, :, D:D + 1].bitcast(I32).rearrange("p j a -> p (j a)"),
                          pattern=[[P, PADS]], base=TOKENS * K_TOP,
                          channel_multiplier=1).then_inc(pads_ready, 1)

            @block.vector
            def _(dve):
                dve.memset(k.onesr[:].bitcast(F32), 1.0)
                dve.memset(rawb[:], 0.0).then_inc(zeroed, 1)
                dve.memset(rawa[:], 0.0).then_inc(zeroed, 1)
                dve.memset(raw2[0:32, 1], 0.0).then_inc(zeroed, 1)
                for m, (raw, h, l) in enumerate(halves):
                    dve.wait_ge(hi, m + 1)
                    dve.tensor_tensor(l, raw, h.bitcast(F32), ALU.subtract)
                for m, (raw, b) in enumerate(bias_hi):
                    dve.wait_ge(hi, len(halves) + m + 1)
                    dve.tensor_tensor(raw[32:33], raw[32:33], b[32:33].bitcast(F32),
                                      ALU.subtract).then_inc(lo, 1)
                    dve.wait_ge(lo, m + 1)
                    dve.tensor_copy(b[32:33], raw[32:33])

            @block.scalar
            def _(act):
                for dst, src in smalls:
                    act.dma_start(dst, src).then_inc(small, 16)
                act.wait_ge(loaded, 16 * len(loads))
                for raw, h, _l in halves:
                    act.activation(h, raw, ACT.Copy).then_inc(hi, 1)
                for raw, b in bias_hi:
                    act.activation(b[:], raw, ACT.Copy).then_inc(hi, 1)


def norm_and_gate(nc, k, sb, ps, n, src, xrow, logits):
    with phase(nc) as sem, ExitStack() as ctx:
        xg = [sb(f"a{n}_xg{r}", [P, GT, D], ctx=ctx) for r in range(2)]
        xh = [sb(f"a{n}_xh{r}", [P, GT, D], ctx=ctx) for r in range(2)]
        xt = [sb(f"a{n}_xt{r}", [P, GT * P], ctx=ctx) for r in range(2)]
        st = sb(f"a{n}_st", [P, GT, 6], ctx=ctx)
        mv = [sb(f"a{n}_mv{r}", [P, GT, 2], ctx=ctx) for r in range(2)]
        ve = [sb(f"a{n}_ve{r}", [P, GT], ctx=ctx) for r in range(2)]
        rs = [sb(f"a{n}_rs{r}", [P, GT], ctx=ctx) for r in range(2)]
        pt = [ps(f"a{n}_pt{r}", [P, GT * P], ctx) for r in range(2)]
        pl = [ps(f"a{n}_pl{r}", [P, 512], ctx) for r in range(2)]
        in_ready = [sem(f"a{n}_in{r}") for r in range(2)]
        stats, aggr, var, rstd = (sem(f"a{n}_{s}") for s in ("stats", "aggr", "var", "rstd"))
        passed = sem(f"a{n}_passed")
        xh_ready, kept, xpose = (sem(f"a{n}_{s}") for s in ("xh", "kept", "xpose"))
        xt_ready, gate, lg = (sem(f"a{n}_{s}") for s in ("xt", "gate", "lg"))

        def steps(eng, step):
            step(-1, -1)
            step(0, 0)
            step(1, 1)
            with eng.Fori(0, 2) as i:
                step(2, 2 * i + 2)
                step(3, 2 * i + 3)
            step(6, 6)
            step(7, 7)

        with nc.Block() as block:
            @block.sync
            def _(sp):
                def load(r, g):
                    wait(sp, xh_ready, g - 1)
                    sp.dma_start(xg[r][:], src[:, ds(g, 1)].rearrange("p b i d -> p (b i) d")
                                 ).then_inc(in_ready[r], 16)
                load(0, 0)
                load(1, 1)
                with sp.Fori(1, 4) as i:
                    load(0, 2 * i)
                    load(1, 2 * i + 1)

            @block.vector
            def _(dve):
                def step(s, g):
                    if s < 7:
                        r = (s + 1) % 2
                        dve.wait_ge(in_ready[r], 16 * ((s + 1) // 2 + 1) if isinstance(g, int)
                                    else 8 * (g + 1 - r) + 16)
                        for t in range(GT):
                            last = dve.bn_stats(st[:, t], xg[r][:, t])
                        last.then_inc(stats, 1)
                        dve.wait_ge(stats, g + 2)
                        wait(dve, xh_ready, g)
                        dve.sem_inc(passed, 1)
                        for t in range(GT):
                            last = dve.bn_aggr(mv[r][:, t], st[:, t])
                        last.then_inc(aggr, 1)
                        dve.wait_ge(aggr, g + 2)
                        dve.tensor_scalar(ve[r][:], mv[r][:, :, 1], EPS, None, ALU.add
                                          ).then_inc(var, 1)
                    if s >= 0:
                        r = s % 2
                        dve.wait_ge(rstd, g + 1)
                        wait(dve, xpose, g - 1)
                        wait(dve, kept, g - 1)
                        for t in range(GT):
                            last = dve.tensor_scalar(xh[r][:, t], xg[r][:, t], mv[r][:, t, 0:1],
                                                     rs[r][:, t:t + 1], ALU.subtract, ALU.mult)
                        last.then_inc(xh_ready, 1)
                    if s >= 1:
                        dve.wait_ge(gate, g)
                        dve.tensor_copy(logits[:, ds((g - 1) * (GT * E), GT * E)],
                                        pl[(s - 1) % 2][:, 0:GT * E]).then_inc(lg, 1)
                steps(dve, step)
                dve.wait_ge(gate, 8)
                dve.tensor_copy(logits[:, 7 * GT * E:], pl[1][:, 0:GT * E]).then_inc(lg, 1)

            @block.gpsimd
            def _(pool):
                def step(s, g):
                    if s < 7:
                        r = (s + 1) % 2
                        pool.wait_ge(var, g + 2)
                        wait(pool, xh_ready, g)
                        pool.tensor_tensor(rs[r][:], ve[r][:], k.nhalf[:], ALU.pow
                                           ).then_inc(rstd, 1)
                    if s >= 0:
                        pool.wait_ge(xh_ready, g + 1)
                        pool.tensor_copy(xrow[:, ds(g * GT, GT), 0:D], xh[s % 2][:]
                                         ).then_inc(kept, 1)
                steps(pool, step)

            @block.scalar
            def _(act):
                def step(s, g):
                    if s >= 0:
                        act.wait_ge(xpose, g + 1)
                        wait(act, gate, g - 1)
                        act.activation(xt[s % 2][:], pt[s % 2][:], ACT.Copy).then_inc(xt_ready, 1)
                steps(act, step)

            @block.tensor
            def _(pe):
                def step(s, g):
                    if s < 7:
                        r = (s + 1) % 2
                        pe.wait_ge(xh_ready, g + 2)
                        wait(pe, xt_ready, g)
                        for t in range(GT):
                            last = pe.transpose(pt[r][:, t * P:(t + 1) * P], xh[r][:, t],
                                                k.ident[:])
                        last.then_inc(xpose, 1)
                    if s >= 0:
                        r = s % 2
                        pe.wait_ge(xt_ready, g + 1)
                        wait(pe, lg, g - 1)
                        for t in range(GT):
                            o = pl[r][:, t * E:(t + 1) * E]
                            pe.matmul(o, xt[r][:, t * P:(t + 1) * P], k.gw[:], start=True,
                                      stop=False)
                            last = pe.matmul(o, k.ones1[:], k.gb[:], start=False, stop=True)
                        last.then_inc(gate, 1)
                steps(pe, step)


def route_and_share(nc, k, sb, ps, n, src, xrow, logits, xs, resid):
    N = TILES * E
    with phase(nc) as sem, ExitStack() as ctx:
        def t(name, shape, dt=F32):
            return sb(f"r{n}_{name}", shape, dt, ctx)

        mask = t("mask", [P, N], BF16)
        mx, mx2, ix, ssum, wtop, wsec = (t(s, [P, TILES]) for s in
                                         ("mx", "mx2", "ix", "ssum", "wtop", "wsec"))
        slot = [t(f"slot{q}", [P, TILES], I32) for q in range(K_TOP)]
        need, ends, starts = (t(s, [P, E]) for s in ("need", "ends", "starts"))
        texp = t("texp", [1, SLOT_TILES])
        xs_in = [t(f"xs{r}", [P, CHUNK, D]) for r in range(2)]
        rx = [t(f"rx{r}", [P, CHUNK, D]) for r in range(2)]
        ro = [t(f"ro{r}", [P, CHUNK, D]) for r in range(2)]
        xth = [t(f"xth{r}", [P, 512], F32R) for r in range(2)]
        with ExitStack() as early:
            dev, oh1, oh2, tmp = (sb(f"r{n}_{s}", [P, TILES, E], F32, early)
                                  for s in ("dev", "oh1", "oh2", "tmp"))
            tot, incl = (sb(f"r{n}_{s}", [P, E, TILES], F32, early) for s in ("tot", "incl"))
        xtl = [t(f"xtl{r}", [P, 512], F32R) for r in range(2)]
        sil = [t(f"sil{r}", [P, 512]) for r in range(2)]
        act_f = [t(f"actf{r}", [P, 512]) for r in range(2)]
        ah, al = (t(s, [P, 3, 512], F32R) for s in ("ah", "al"))
        p_route = ps(f"r{n}_proute", [P, 2, 512], ctx)
        p_x = ps(f"r{n}_px", [P, 512], ctx)
        p_hg = [ps(f"r{n}_phg{r}", [P, 2, 512], ctx) for r in range(2)]
        p_z = p_route

        names = ("chain", "dev_ready", "exp_done", "mask_ready", "tot_mm", "tot_done", "pre_mm",
                 "slots_ready", "w_ready", "sent0", "payload", "sent1", "mx2_ready", "expsec")
        (chain, dev_ready, exp_done, mask_ready, tot_mm, tot_done, pre_mm, slots_ready, w_ready,
         sent0, payload, sent1, mx2_ready, expsec) = (sem(f"r{n}_{s}") for s in names)
        names = ("xpose", "hi", "lo", "up", "silu", "aa", "ahi", "alo", "down", "outr", "outh")
        (xpose, hi, lo, up, silu, aa, ahi, alo, down, outr, outh) = (
            sem(f"s{n}_{s}") for s in names)
        in_ready = [sem(f"s{n}_in{r}") for r in range(2)]
        rx_ready = [sem(f"s{n}_rx{r}") for r in range(2)]
        stored = [sem(f"s{n}_st{r}") for r in range(2)]

        def steps(eng, step, first=-1, after=1):
            for c in range(first, 2):
                step(c, c)
            with eng.Fori(0, 6) as i:
                step(2, 2 * i + 2)
                step(3, 2 * i + 3)
            for c in range(14, CHUNKS + after):
                step(c, c)

        def turn(c, cv, r):
            return 16 * (c // 2 + 1) if isinstance(cv, int) else 8 * (cv - r) + 16

        def chunk_of(ap, c, cv):
            b = cv // 2 if isinstance(cv, int) else None
            h = c % 2
            if b is None:
                b = (cv - h) // 2
            return ap[:, ds(b, 1), h * CHUNK:(h + 1) * CHUNK].rearrange("p b i d -> p (b i) d")

        with nc.Block() as block:
            @block.sync
            def _(sp):
                def step(c, cv):
                    r = c % 2
                    if c < CHUNKS:
                        wait(sp, xpose, cv - 1)
                        sp.dma_start(xs_in[r][:], xrow[:, ds(cv * CHUNK, CHUNK), 0:D]
                                     ).then_inc(in_ready[r], 16)
                        wait(sp, outr, cv - 1)
                        sp.dma_start(rx[r][:], chunk_of(src, c, cv)).then_inc(rx_ready[r], 16)
                    if c >= 2:
                        wait(sp, outr, cv - 1)
                        sp.dma_start(chunk_of(resid, c, cv - 2), ro[r][:]
                                     ).then_inc(stored[r], 16)
                steps(sp, step, first=0, after=2)
                for r in range(2):
                    sp.wait_ge(stored[r], 16 * CHUNKS // 2)

            @block.gpsimd
            def _(pool):
                rows = xrow[:, :, D:D + 1].bitcast(I32).rearrange("p (b i) a -> p b (i a)", i=GT)
                pool.iota(rows, pattern=[[2 * GT * P, GROUPS], [2, GT]], base=0,
                          channel_multiplier=2 * GT).then_inc(payload, 1)
                pool.wait_ge(w_ready, 1)
                pool.wait_ge(slots_ready, 1)
                pool.wait_ge(payload, 1)
                for q in range(TILES):
                    pool.indirect_dma_start(xs, bass.IndirectOffsetOnAxis(slot[0][:, q:q + 1], 0),
                                            xrow[:, q, :], None).then_inc(sent0, 16)
                pool.wait_ge(sent0, 16 * TILES)
                pool.iota(rows, pattern=[[2 * GT * P, GROUPS], [2, GT]], base=1,
                          channel_multiplier=2 * GT).then_inc(payload, 1)
                pool.wait_ge(w_ready, 2)
                pool.tensor_copy(xrow[:, :, D + 1:D + 2], wsec[:].unsqueeze(2)
                                 ).then_inc(payload, 1)
                pool.wait_ge(payload, 3)
                for q in range(TILES):
                    pool.indirect_dma_start(xs, bass.IndirectOffsetOnAxis(slot[1][:, q:q + 1], 0),
                                            xrow[:, q, :], None).then_inc(sent1, 16)
                pool.wait_ge(sent1, 16 * TILES)

            @block.vector
            def _(dve):
                links = [0]

                def link(ins):
                    links[0] += 1
                    ins.then_inc(chain, 1)
                    dve.wait_ge(chain, links[0])

                def over_e(a):
                    return a.unsqueeze(2).to_broadcast([P, TILES, E])

                def over_t(a):
                    return a.unsqueeze(1).to_broadcast([P, TILES, E])

                lg = logits[:].rearrange("p (t e) -> p t e", e=E)
                by_te = incl[:].rearrange("p e t -> p t e")
                link(dve.reduce_max(mx[:], lg, AX))
                dve.tensor_tensor(dev[:], lg, over_e(mx[:]), ALU.subtract).then_inc(dev_ready, 1)
                dve.wait_ge(dev_ready, 1)

                def first_of(val, hit, best):
                    if best is None:
                        link(dve.tensor_scalar(hit[:], val[:], 0.0, None, ALU.is_equal))
                    else:
                        link(dve.tensor_tensor(hit[:], val[:], over_e(best[:]), ALU.is_equal))
                    link(dve.scalar_tensor_tensor(hit[:], hit[:], -64.0, over_t(k.iota_e[:]),
                                                  ALU.mult, ALU.add))
                    link(dve.tensor_reduce(ix[:], hit[:], AX, ALU.min))
                    link(dve.tensor_scalar(ix[:], ix[:], 64.0, None, ALU.add))
                    link(dve.tensor_tensor(hit[:], over_t(k.iota_e[:]), over_e(ix[:]),
                                           ALU.is_equal))

                first_of(dev, oh1, None)
                link(dve.scalar_tensor_tensor(tmp[:], oh1[:], -3e38, dev[:], ALU.mult, ALU.add))
                dve.reduce_max(mx2[:], tmp[:], AX).then_inc(mx2_ready, 1)
                dve.wait_ge(mx2_ready, 1)
                first_of(tmp, oh2, mx2)
                dve.tensor_tensor(mask[:].rearrange("p (t e) -> p t e", e=E), oh1[:], oh2[:],
                                  ALU.add).then_inc(mask_ready, 1)
                dve.wait_ge(exp_done, 1)
                link(dve.reduce_sum(ssum[:], dev[:], AX))
                link(dve.reciprocal(ssum[:], ssum[:]))
                dve.tensor_scalar(xrow[:, :, D + 1:D + 2], ssum[:].unsqueeze(2), 0.5, None,
                                  ALU.mult).then_inc(w_ready, 1)
                dve.wait_ge(expsec, 1)
                dve.scalar_tensor_tensor(wsec[:], ssum[:], 0.5, wtop[:], ALU.mult, ALU.mult
                                         ).then_inc(w_ready, 1)
                dve.wait_ge(tot_done, 1)
                link(dve.tensor_tensor_scan(incl[:].rearrange("p e t -> p (e t)"), k.carry[:],
                                            tot[:].rearrange("p e t -> p (e t)"), 0.0,
                                            ALU.mult, ALU.add))
                link(dve.tensor_scalar(need[:], incl[:, :, TILES - 1], 63.5, 1.0 / P, ALU.add,
                                       ALU.mult))
                link(dve.tensor_scalar(need[:], need[:], MAGIC, MAGIC, ALU.add, ALU.subtract))
                link(dve.tensor_tensor_scan(ends[:], k.ones_e[:], need[:], 0.0, ALU.mult,
                                            ALU.add))
                link(dve.tensor_tensor(starts[:], ends[:], need[:], ALU.subtract))
                link(dve.tensor_tensor(incl[:], incl[:], tot[:], ALU.subtract))
                link(dve.scalar_tensor_tensor(
                    incl[:], starts[:].unsqueeze(2).to_broadcast([P, E, TILES]), float(P),
                    incl[:], ALU.mult, ALU.add))
                dve.wait_ge(pre_mm, 1)
                link(dve.tensor_tensor(tmp[:], p_route[:].rearrange("p a (t e) -> p (a t) e", e=E),
                                       by_te, ALU.add))
                link(dve.tensor_tensor(oh1[:], oh1[:], tmp[:], ALU.mult))
                dve.tensor_tensor(oh2[:], oh2[:], tmp[:], ALU.mult)
                link(dve.reduce_sum(mx[:], oh1[:], AX))
                link(dve.reduce_sum(mx2[:], oh2[:], AX))
                dve.tensor_copy(slot[0][:], mx[:])
                dve.tensor_copy(slot[1][:], mx2[:]).then_inc(slots_ready, 1)
                link(dve.memset(texp[:], 0.0))
                for e in range(E):
                    link(dve.scalar_tensor_tensor(texp[:], k.iota_j[:], ends[0:1, e:e + 1],
                                                  texp[:], ALU.is_ge, ALU.add))
                dve.tensor_scalar(k.tile_expert[:], texp[:], float(E - 1), None, ALU.min)
                dve.memset(ah[96:97, 2].bitcast(F32), 1.0)
                dve.memset(al[96:97, 2].bitcast(F32), 0.0)

                def step(c, cv):
                    for f in range(3):
                        m, mv = 3 * c + f, 3 * cv + f
                        if 0 <= c < CHUNKS:
                            w = FEAT[f][1]
                            dve.wait_ge(silu, mv + 1)
                            wait(dve, alo, mv - 1)
                            dve.scalar_tensor_tensor(
                                act_f[m % 2][0:w], p_hg[m % 2][0:w, 1], k.sb13[0:w, 1, f:f + 1],
                                sil[m % 2][0:w], ALU.add, ALU.mult).then_inc(aa, 1)
                        if 1 <= m <= 3 * CHUNKS:
                            g, w = (f - 1) % 3, FEAT[(f - 1) % 3][1]
                            dve.wait_ge(ahi, mv)
                            dve.tensor_tensor(al[0:w, g], act_f[(m - 1) % 2][0:w],
                                              ah[0:w, g].bitcast(F32), ALU.subtract
                                              ).then_inc(alo, 1)
                        if f == 1 and c < CHUNKS - 1:
                            r = (c + 1) % 2
                            dve.wait_ge(hi, cv + 2)
                            dve.tensor_tensor(xtl[r][:], p_x[:], xth[r][:].bitcast(F32),
                                              ALU.subtract).then_inc(lo, 1)
                        if f == 1 and c >= 1:
                            r = (c - 1) % 2
                            z = p_z[:].rearrange("p a (i n) -> p (a i) n", n=2 * D)
                            dve.wait_ge(down, 3 * cv)
                            dve.wait_ge(rx_ready[r], turn(c - 1, cv if isinstance(cv, int)
                                                          else cv - 1, r))
                            if c >= 3:
                                dve.wait_ge(stored[r], turn(c - 1, cv if isinstance(cv, int)
                                                            else cv - 1, r) - 16)
                            dve.scalar_tensor_tensor(rx[r][:], z[:, :, 0:D], 0.5, rx[r][:],
                                                     ALU.mult, ALU.add).then_inc(outh, 1)
                            dve.wait_ge(outh, cv)
                            dve.scalar_tensor_tensor(ro[r][:], z[:, :, D:2 * D], 0.5, rx[r][:],
                                                     ALU.mult, ALU.add).then_inc(outr, 1)
                steps(dve, step)

            @block.scalar
            def _(act):
                act.wait_ge(dev_ready, 1)
                act.wait_ge(mx2_ready, 1)
                act.activation(dev[:], dev[:], ACT.Exp).then_inc(exp_done, 1)
                act.activation(wtop[:], mx2[:], ACT.Exp).then_inc(expsec, 1)
                act.wait_ge(tot_mm, 1)
                act.activation(tot[:].rearrange("p e t -> p t e"),
                               p_route[:].rearrange("p a (t e) -> p (a t) e", e=E), ACT.Copy
                               ).then_inc(tot_done, 1)

                def step(c, cv):
                    for f in range(3):
                        m, mv = 3 * c + f, 3 * cv + f
                        if 0 <= c < CHUNKS:
                            w = FEAT[f][1]
                            act.wait_ge(up, mv + 1)
                            wait(act, aa, mv - 1)
                            act.activation(sil[m % 2][0:w], p_hg[m % 2][0:w, 0], ACT.Silu,
                                           bias=k.sb13[0:w, 0, f:f + 1]).then_inc(silu, 1)
                        if 1 <= m <= 3 * CHUNKS:
                            g, w = (f - 1) % 3, FEAT[(f - 1) % 3][1]
                            act.wait_ge(aa, mv)
                            wait(act, down, mv - 3)
                            act.activation(ah[0:w, g], act_f[(m - 1) % 2][0:w], ACT.Copy
                                           ).then_inc(ahi, 1)
                        if f == 1 and c < CHUNKS - 1:
                            r = (c + 1) % 2
                            act.wait_ge(xpose, cv + 2)
                            wait(act, up, 3 * cv)
                            act.activation(xth[r][:], p_x[:], ACT.Copy).then_inc(hi, 1)
                steps(act, step)

            @block.tensor
            def _(pe):
                def step(c, cv):
                    for f in range(3):
                        m, mv = 3 * c + f, 3 * cv + f
                        if 0 <= c < CHUNKS:
                            r = c % 2
                            o, w = FEAT[f]
                            if f == 0:
                                pe.wait_ge(lo, cv + 1)
                            wait(pe, aa, mv - 1)
                            for g in range(2):
                                cols = slice(g * SH + o, g * SH + o + w)
                                parts = ((k.sw13h, xth), (k.sw13h, xtl), (k.sw13l, xth))
                                for q, (w_, x_) in enumerate(parts):
                                    last = pe.matmul(p_hg[m % 2][0:w, g], w_[:, cols], x_[r][:],
                                                     start=q == 0, stop=q == 2)
                            last.then_inc(up, 1)
                        if f == 0 and c < CHUNKS - 1:
                            r = (c + 1) % 2
                            pe.wait_ge(in_ready[r], turn(c + 1, cv if isinstance(cv, int)
                                                         else cv + 1, r))
                            wait(pe, lo, cv + 1)
                            for q in range(CHUNK):
                                last = pe.transpose(p_x[:, q * P:(q + 1) * P], xs_in[r][:, q],
                                                    k.ident[:])
                            last.then_inc(xpose, 1)
                        if 2 <= m <= 3 * CHUNKS + 1:
                            g = (f - 2) % 3
                            w = 97 if g == 2 else P
                            pe.wait_ge(alo, mv - 1)
                            if g == 0:
                                wait(pe, outr, cv)
                            for q in range(CHUNK):
                                tok = slice(q * P, (q + 1) * P)
                                z, o = p_z[:, q // 2], (q % 2) * 2 * D
                                pe.matmul(z[:, o:o + 2 * D], ah[0:w, g, tok], k.sw2hl[0:w, g],
                                          start=g == 0 and q % 2 == 0, stop=False,
                                          skip_group_check=True)
                                last = pe.matmul(z[:, o:o + D], al[0:w, g, tok],
                                                 k.sw2hl[0:w, g, 0:D], start=False, stop=g == 2,
                                                 skip_group_check=True)
                            last.then_inc(down, 1)

                step(-1, -1)
                pe.wait_ge(mask_ready, 1)
                for h in range(2):
                    last = pe.matmul(p_route[:, h], k.onesb[:], mask[:, h * 512:(h + 1) * 512],
                                     start=True, stop=True)
                last.then_inc(tot_mm, 1)
                pe.wait_ge(tot_done, 1)
                for h in range(2):
                    last = pe.matmul(p_route[:, h], k.tri[:], mask[:, h * 512:(h + 1) * 512],
                                     start=True, stop=True)
                last.then_inc(pre_mm, 1)
                steps(pe, step, first=0)


def experts(nc, k, sb, ps, n, xs, ys):
    with phase(nc) as sem, ExitStack() as ctx:
        xin = [sb(f"e{n}_x{r}", [P, 2, ROW], ctx=ctx) for r in range(RING)]
        y = [sb(f"e{n}_y{r}", [P, 2, D], ctx=ctx) for r in range(RING)]
        xth = [sb(f"e{n}_xth{r}", [P, 2 * P], F32R, ctx) for r in range(2)]
        xtl = [sb(f"e{n}_xtl{r}", [P, 2 * P], F32R, ctx) for r in range(2)]
        sil = [sb(f"e{n}_sil{r}", [P, 2, INTER], ctx=ctx) for r in range(2)]
        a = [sb(f"e{n}_a{r}", [P, 2, INTER], ctx=ctx) for r in range(2)]
        ah = [sb(f"e{n}_ah{r}", [A0 + 1, 512], F32R, ctx) for r in range(2)]
        al = [sb(f"e{n}_al{r}", [A0 + 1, 512], F32R, ctx) for r in range(2)]
        p_x = ps(f"e{n}_px", [P, 512], ctx)
        p_u = [ps(f"e{n}_pu{r}", [P, 2, 512], ctx) for r in range(2)]
        p_a = ps(f"e{n}_pa", [P, 512], ctx)
        p_y = ps(f"e{n}_py", [P, 512], ctx)
        names = ("xpose", "xhi", "xlo", "up", "silu", "aa", "apose", "ahi", "alo", "down", "yhi",
                 "yy", "passed")
        (xpose, xhi, xlo, up, silu, aa, apose, ahi, alo, down, yhi, yy, passed) = (
            sem(f"e{n}_{s}") for s in names)
        x_in = [sem(f"e{n}_in{r}") for r in range(RING)]
        sent = [sem(f"e{n}_sent{r}") for r in range(RING)]
        rows = xs.rearrange("(j t p) c -> p j t c", t=2, p=P)
        LOOPED = (PAIRS - RING) // RING

        def steps(eng, step, last):
            for j in range(-1, 3):
                step(j, j)
            with eng.Fori(0, LOOPED) as i:
                for u in range(RING):
                    step(3 + u, RING * i + (3 + u))
            for j in range(3 + RING * LOOPED, last):
                step(j, j)

        with nc.Block() as block:
            @block.sync
            def _(sp):
                for r in range(RING):
                    sp.dma_start(xin[r][:], rows[:, r]).then_inc(x_in[r], 16)
                with sp.Fori(1, PAIRS // RING) as i:
                    for r in range(RING):
                        sp.wait_ge(sent[r], 32 * i)
                        sp.dma_start(xin[r][:],
                                     rows[:, ds(RING * i + r, 1)].rearrange(
                                         "p j t c -> p (j t) c")).then_inc(x_in[r], 16)
                if n == 0:
                    fill(sp, k, k.xs2, 1)
                    sp.wait_ge(k.s_fill[1], 16 * SLOT_TILES // PADS)

            @block.gpsimd
            def _(pool):
                with pool.Fori(0, PAIRS // RING) as i:
                    for r in range(RING):
                        pool.wait_ge(yy, RING * i + (r + 1))
                        pool.sem_inc(passed, 1)
                        for t in range(2):
                            pool.indirect_dma_start(
                                ys, bass.IndirectOffsetOnAxis(
                                    xin[r][:, t, D:D + 1].bitcast(I32), 0),
                                y[r][:, t, :], None).then_inc(sent[r], 16)
                for r in range(RING):
                    pool.wait_ge(sent[r], 32 * (PAIRS // RING))

            @block.vector
            def _(dve):
                for r in range(2):
                    dve.memset(ah[r][A0:A0 + 1].bitcast(F32), 1.0)
                    dve.memset(al[r][A0:A0 + 1].bitcast(F32), 0.0)

                def step(j, jv):
                    if j < PAIRS - 1:
                        r = (j + 1) % 2
                        dve.wait_ge(xhi, jv + 2)
                        dve.tensor_tensor(xtl[r][:], p_x[:, 0:2 * P], xth[r][:].bitcast(F32),
                                          ALU.subtract).then_inc(xlo, 1)
                    if 0 <= j < PAIRS:
                        r = j % 2
                        dve.wait_ge(silu, jv + 1)
                        wait(dve, apose, jv - 1)
                        dve.tensor_tensor(a[r][:], p_u[r][:, :, INTER:UP], sil[r][:], ALU.mult
                                          ).then_inc(aa, 1)
                    if 1 <= j < PAIRS + 1:
                        r = (j - 1) % 2
                        dve.wait_ge(ahi, jv)
                        dve.tensor_tensor(al[r][0:A0], p_a[0:A0], ah[r][0:A0].bitcast(F32),
                                          ALU.subtract).then_inc(alo, 1)
                    if 2 <= j:
                        s = (j - 2) % RING
                        dve.wait_ge(yhi, jv - 1)
                        for t in range(2):
                            last = dve.scalar_tensor_tensor(
                                y[s][:, t], p_y[:, t * 2 * D + D:(t + 1) * 2 * D],
                                xin[s][:, t, D + 1:D + 2], y[s][:, t], ALU.mult, ALU.add)
                        last.then_inc(yy, 1)
                steps(dve, step, PAIRS + 2)

            @block.scalar
            def _(act):
                def step(j, jv):
                    if j < PAIRS - 1:
                        r = (j + 1) % 2
                        act.wait_ge(xpose, jv + 2)
                        wait(act, up, jv)
                        act.activation(xth[r][:], p_x[:, 0:2 * P], ACT.Copy).then_inc(xhi, 1)
                    if 0 <= j < PAIRS:
                        r = j % 2
                        act.wait_ge(up, jv + 1)
                        wait(act, aa, jv - 1)
                        act.activation(sil[r][:], p_u[r][:, :, 0:INTER], ACT.Silu
                                       ).then_inc(silu, 1)
                    if 1 <= j < PAIRS + 1:
                        r = (j - 1) % 2
                        act.wait_ge(apose, jv)
                        wait(act, down, jv - 2)
                        act.activation(ah[r][0:A0], p_a[0:A0], ACT.Copy).then_inc(ahi, 1)
                    if 2 <= j:
                        s = (j - 2) % RING
                        act.wait_ge(down, jv - 1)
                        for t in range(2):
                            last = act.activation(
                                y[s][:, t], p_y[:, t * 2 * D:t * 2 * D + D], ACT.Copy,
                                scale=xin[s][:, t, D + 1:D + 2])
                        last.then_inc(yhi, 1)
                steps(act, step, PAIRS + 2)

            @block.tensor
            def _(pe):
                expert = {}

                def load_experts(first, pairs):
                    expert.clear()
                    _, got = nc.values_load_multi_w_load_instructions(
                        k.tile_expert[0:1, ds(2 * first, 2 * len(pairs))],
                        engines=[mybir.EngineType.PE], min_val=0, max_val=E - 1,
                        skip_runtime_bounds_check_because="a count of 16 compares, at most 15")
                    for q, j in enumerate(pairs):
                        expert[j] = got[2 * q:2 * q + 2]

                def step(j, jv):
                    if j < PAIRS - 1:
                        s = (j + 1) % RING
                        turns = (16 * ((j + 1) // RING + 1) if isinstance(jv, int)
                                 else 16 * ((jv + (1 - s)) // RING + 1))
                        pe.wait_ge(x_in[s], turns)
                        wait(pe, xlo, jv + 1)
                        for t in range(2):
                            last = pe.transpose(p_x[:, t * P:(t + 1) * P], xin[s][:, t, 0:D],
                                                k.ident[:])
                        last.then_inc(xpose, 1)
                    if 0 <= j < PAIRS:
                        r = j % 2
                        pe.wait_ge(xlo, jv + 1)
                        wait(pe, aa, jv - 1)
                        for t in range(2):
                            cols = ds(expert[j][t] * UP, UP)
                            tok = slice(t * P, (t + 1) * P)
                            o = p_u[r][:, t, 0:UP]
                            pe.matmul(o, k.onesr[:], k.b13[:, cols], start=True, stop=False)
                            pe.matmul(o, xth[r][:, tok], k.w13h[:, cols], start=False, stop=False)
                            pe.matmul(o, xth[r][:, tok], k.w13l[:, cols], start=False, stop=False)
                            last = pe.matmul(o, xtl[r][:, tok], k.w13h[:, cols], start=False,
                                             stop=True)
                        last.then_inc(up, 1)
                    if 1 <= j < PAIRS + 1:
                        r = (j - 1) % 2
                        pe.wait_ge(aa, jv)
                        wait(pe, alo, jv - 1)
                        for t in range(2):
                            for c, o in enumerate((0, A1)):
                                q = 2 * t + c
                                last = pe.transpose(p_a[0:A0, q * P:(q + 1) * P],
                                                    a[r][:, t, o:o + A0], k.ident[:])
                        last.then_inc(apose, 1)
                    if 2 <= j:
                        r = j % 2
                        pe.wait_ge(alo, jv - 1)
                        wait(pe, yy, jv - 2)
                        for t in range(2):
                            for c, rows_ in enumerate((A0 + 1, A0)):
                                q = slice((2 * t + c) * P, (2 * t + c + 1) * P)
                                w2 = k.w2hl[0:rows_, c, ds(expert[j - 2][t], 1)].rearrange(
                                    "p e n -> p (e n)")
                                o = t * 2 * D
                                pe.matmul(p_y[:, o:o + 2 * D], ah[r][0:rows_, q], w2,
                                          start=c == 0, stop=False, skip_group_check=True)
                                last = pe.matmul(p_y[:, o:o + D], al[r][0:rows_, q], w2[:, 0:D],
                                                 start=False, stop=c == 1, skip_group_check=True)
                        last.then_inc(down, 1)

                load_experts(0, [0, 1, 2])
                for j in range(-1, 3):
                    step(j, j)
                with pe.Fori(0, LOOPED) as i:
                    load_experts(RING * i + 1, list(range(1, 3 + RING)))
                    for u in range(RING):
                        step(3 + u, RING * i + (3 + u))
                tail = 3 + RING * LOOPED
                load_experts(tail - 2, list(range(tail - 2, PAIRS)))
                for j in range(tail, PAIRS + 2):
                    step(j, j)


def attention(nc, k, sb, ps, resid, ys, x3):
    with phase(nc) as sem, ExitStack() as ctx:
        def t2(name, shape, dt=F32):
            return [sb(f"t_{name}{r}", shape, dt, ctx) for r in range(2)]

        rs, x2, x3s = t2("rs", [P, GT, D]), t2("x2", [P, GT, D]), t2("x3", [P, GT, D])
        yt = t2("yt", [P, GT, 2 * D])
        xh, xt = sb("t_xh", [P, GT, D], ctx=ctx), t2("xt", [P, GT * P])
        st, mv = sb("t_st", [P, GT, 6], ctx=ctx), sb("t_mv", [P, GT, 2], ctx=ctx)
        ve, rstd = sb("t_ve", [P, GT], ctx=ctx), sb("t_rstd", [P, GT], ctx=ctx)
        mq, eq, rq = (sb(f"t_{s}", [P, GT * P], ctx=ctx) for s in ("mq", "eq", "rq"))
        phq = sb("t_phq", [P, GT * P], ctx=ctx)
        mk, ek = sb("t_mk", [P, 4, D], ctx=ctx), sb("t_ek", [P, 4, D], ctx=ctx)
        phk, v = sb("t_phk", [P, GT, D], ctx=ctx), sb("t_v", [P, GT, D], ctx=ctx)
        kvt, kvp = sb("t_kvt", [P, D], ctx=ctx), sb("t_kvp", [P, D], ctx=ctx)
        p_t, p_q = ps("t_pt", [P, 2, 512], ctx), ps("t_pq", [P, 2, 512], ctx)
        p_kv, p_b = ps("t_pkv", [P, 2, 512], ctx), ps("t_pb", [P, 512], ctx)
        in_ready = [sem(f"t_in{r}") for r in range(2)]
        stored = [sem(f"t_stored{r}") for r in range(2)]
        names = ("ysum", "x2r", "stats", "aggr", "var", "rstds", "xhr", "xpose", "xtr", "qmm",
                 "mqr", "rqr", "eqr", "phqr", "kvmm", "mkr", "ekr", "phkr", "vtk", "kvtr",
                 "kvpmm", "kvpr", "omm", "x3r", "passed")
        s = {m: sem(f"t_{m}") for m in names}

        def steps(eng, step):
            for g in (-1, 0, 1):
                step(g, g)
            with eng.Fori(0, 2) as i:
                step(2, 2 * i + 2)
                step(3, 2 * i + 3)
            step(6, 6)
            step(7, 7)

        def turn(g, gv, r):
            return 16 * (g // 2 + 1) if isinstance(gv, int) else 8 * (gv - r) + 16

        def group(ap, gv):
            return ap[:, ds(gv, 1)].rearrange("p b i d -> p (b i) d")

        with nc.Block() as block:
            @block.sync
            def _(sp):
                def step(g, gv):
                    r = (g + 1) % 2
                    if g < 7:
                        wait(sp, s["x2r"], gv)
                        sp.dma_start(rs[r][:], group(resid, gv + 1)).then_inc(in_ready[r], 16)
                        sp.dma_start(yt[r][:], group(ys, gv + 1)).then_inc(in_ready[r], 16)
                    if g >= 1:
                        sp.wait_ge(s["x3r"], gv)
                        sp.dma_start(group(x3, gv - 1), x3s[(g - 1) % 2][:]
                                     ).then_inc(stored[(g - 1) % 2], 16)
                steps(sp, step)
                sp.wait_ge(s["x3r"], GROUPS)
                sp.dma_start(group(x3, GROUPS - 1), x3s[1][:]).then_inc(stored[1], 16)
                for r in range(2):
                    sp.wait_ge(stored[r], 16 * GROUPS // 2)

            @block.gpsimd
            def _(pool):
                def step(g, gv):
                    if g < 7:
                        r = (g + 1) % 2
                        pool.wait_ge(in_ready[r], 2 * (turn(g + 1, gv if isinstance(gv, int)
                                                            else gv + 1, r)))
                        wait(pool, s["x3r"], gv)
                        pool.tensor_tensor(x2[r][:], yt[r][:, :, 0:D], yt[r][:, :, D:2 * D],
                                           ALU.add).then_inc(s["ysum"], 1)
                        pool.wait_ge(s["var"], gv + 2)
                        pool.tensor_tensor(rstd[:], ve[:], k.nhalf[:], ALU.pow
                                           ).then_inc(s["rstds"], 1)
                steps(pool, step)

            @block.vector
            def _(dve):
                def step(g, gv):
                    if g < 7:
                        r = (g + 1) % 2
                        dve.wait_ge(s["ysum"], gv + 2)
                        dve.tensor_tensor(x2[r][:], x2[r][:], rs[r][:], ALU.add
                                          ).then_inc(s["x2r"], 1)
                        dve.wait_ge(s["x2r"], gv + 2)
                        for q in range(GT):
                            last = dve.bn_stats(st[:, q], x2[r][:, q])
                        last.then_inc(s["stats"], 1)
                        dve.wait_ge(s["stats"], gv + 2)
                        dve.sem_inc(s["passed"], 1)
                        for q in range(GT):
                            last = dve.bn_aggr(mv[:, q], st[:, q])
                        last.then_inc(s["aggr"], 1)
                        dve.wait_ge(s["aggr"], gv + 2)
                        dve.tensor_scalar(ve[:], mv[:, :, 1], EPS, None, ALU.add
                                          ).then_inc(s["var"], 1)
                        dve.wait_ge(s["rstds"], gv + 2)
                        wait(dve, s["xpose"], gv + 1)
                        for q in range(GT):
                            last = dve.tensor_scalar(xh[:, q], x2[r][:, q], mv[:, q, 0:1],
                                                     rstd[:, q:q + 1], ALU.subtract, ALU.mult)
                        last.then_inc(s["xhr"], 1)
                    if g < 0:
                        return
                    r = g % 2
                    dve.wait_ge(s["qmm"], gv + 1)
                    wait(dve, s["eqr"], gv)
                    dve.tensor_scalar(mq[:], p_q[:].rearrange("p a n -> p (a n)"), k.bq[:], 0.0,
                                      ALU.add, ALU.min).then_inc(s["mqr"], 1)
                    for h in range(2):
                        pk = p_kv[:].rearrange("p a (t n) -> p (a t) n", n=2 * D)[:, :, 0:D]
                        dve.wait_ge(s["kvmm"], 2 * gv + h + 1)
                        wait(dve, s["ekr"], 2 * gv + h)
                        dve.tensor_scalar(mk[:], pk, 0.0, None, ALU.min).then_inc(s["mkr"], 1)
                        dve.wait_ge(s["ekr"], 2 * gv + h + 1)
                        if h == 0:
                            wait(dve, s["vtk"], gv)
                        dve.scalar_tensor_tensor(phk[:, 4 * h:4 * h + 4], pk, 0.0, ek[:], ALU.max,
                                                 ALU.add).then_inc(s["phkr"], 1)
                    dve.wait_ge(s["eqr"], gv + 1)
                    dve.wait_ge(s["rqr"], gv + 1)
                    wait(dve, s["omm"], gv)
                    dve.tensor_tensor(phq[:], eq[:], rq[:], ALU.add).then_inc(s["phqr"], 1)
                    dve.wait_ge(s["vtk"], gv + 1)
                    wait(dve, s["kvpmm"], gv)
                    dve.tensor_tensor(kvt[:], p_b[:, 0:D], k.blockdiag[:], ALU.mult
                                      ).then_inc(s["kvtr"], 1)
                    dve.wait_ge(s["omm"], gv + 1)
                    if g >= 2:
                        dve.wait_ge(stored[r], turn(g, gv, r) - 16)
                    dve.tensor_tensor(x3s[r][:], p_kv[:].rearrange("p a (t n) -> p (a t) n", n=D),
                                      x2[r][:], ALU.add).then_inc(s["x3r"], 1)
                steps(dve, step)

            @block.scalar
            def _(act):
                def step(g, gv):
                    if g < 7:
                        r = (g + 1) % 2
                        act.wait_ge(s["xpose"], gv + 2)
                        wait(act, s["kvmm"], 2 * gv)
                        act.activation(xt[r][:], p_t[:].rearrange("p a n -> p (a n)"), ACT.Copy
                                       ).then_inc(s["xtr"], 1)
                    if g < 0:
                        return
                    act.wait_ge(s["mqr"], gv + 1)
                    wait(act, s["phqr"], gv)
                    act.activation(rq[:], p_q[:].rearrange("p a n -> p (a n)"), ACT.Relu,
                                   bias=k.bq[:]).then_inc(s["rqr"], 1)
                    act.activation(eq[:], mq[:], ACT.Exp).then_inc(s["eqr"], 1)
                    for h in range(2):
                        pv = p_kv[:].rearrange("p a (t n) -> p (a t) n", n=2 * D)[:, :, D:2 * D]
                        act.wait_ge(s["mkr"], 2 * gv + h + 1)
                        wait(act, s["phkr"], 2 * gv + h)
                        if h == 0:
                            wait(act, s["vtk"], gv)
                        act.activation(v[:, 4 * h:4 * h + 4], pv, ACT.Copy)
                        act.activation(ek[:], mk[:], ACT.Exp).then_inc(s["ekr"], 1)
                    act.wait_ge(s["kvpmm"], gv + 1)
                    wait(act, s["omm"], gv)
                    act.activation(kvp[:], p_b[:, 0:D], ACT.Copy).then_inc(s["kvpr"], 1)
                steps(act, step)

            @block.tensor
            def _(pe):
                def step(g, gv):
                    if g < 7:
                        pe.wait_ge(s["xhr"], gv + 2)
                        wait(pe, s["xtr"], gv + 1)
                        for q in range(GT):
                            last = pe.transpose(p_t[:, q // 4, (q % 4) * P:(q % 4 + 1) * P],
                                                xh[:, q], k.ident[:])
                        last.then_inc(s["xpose"], 1)
                    if g < 0:
                        return
                    r = g % 2
                    pe.wait_ge(s["xtr"], gv + 1)
                    wait(pe, s["rqr"], gv)
                    for h in range(2):
                        last = pe.matmul(p_q[:, h], k.wq[:], xt[r][:, h * 512:(h + 1) * 512],
                                         start=True, stop=True)
                    last.then_inc(s["qmm"], 1)
                    for h in range(2):
                        if h == 0:
                            wait(pe, s["x3r"], gv)
                        else:
                            pe.wait_ge(s["phkr"], 2 * gv + 1)
                        for q in range(4):
                            o = p_kv[:, q // 2, (q % 2) * 2 * D:(q % 2 + 1) * 2 * D]
                            i = 4 * h + q
                            pe.matmul(o, xt[r][:, i * P:(i + 1) * P], k.wkv[:], start=True,
                                      stop=False)
                            last = pe.matmul(o, k.onesr[:], k.bkvp[:, 0:2 * D], start=False,
                                             stop=True)
                        last.then_inc(s["kvmm"], 1)
                    pe.wait_ge(s["phkr"], 2 * gv + 2)
                    wait(pe, s["kvpr"], gv)
                    for q in range(GT):
                        last = pe.matmul(p_b[:, 0:D], v[:, q], phk[:, q], start=q == 0,
                                         stop=q == GT - 1)
                    last.then_inc(s["vtk"], 1)
                    pe.wait_ge(s["kvtr"], gv + 1)
                    pe.matmul(p_b[:, 0:D], kvt[:], k.wp[:], start=True, stop=True
                              ).then_inc(s["kvpmm"], 1)
                    pe.wait_ge(s["kvpr"], gv + 1)
                    pe.wait_ge(s["phqr"], gv + 1)
                    for q in range(GT):
                        o = p_kv[:, q // 4, (q % 4) * D:(q % 4 + 1) * D]
                        pe.matmul(o, phq[:, q * P:(q + 1) * P], kvp[:], start=True, stop=False)
                        last = pe.matmul(o, k.onesr[:], k.bkvp[:, 2 * D:3 * D], start=False,
                                         stop=True)
                    last.then_inc(s["omm"], 1)
                steps(pe, step)


def combine(nc, k, sb, resid, ys, out):
    with phase(nc) as sem, ExitStack() as ctx:
        rs = [sb(f"c_rs{r}", [P, GT, D], ctx=ctx) for r in range(GROUPS)]
        yt = [sb(f"c_yt{r}", [P, GT, 2 * D], ctx=ctx) for r in range(4)]
        in_ready = [sem(f"c_in{r}") for r in range(GROUPS)]
        half, ysum, stored = sem("c_half"), sem("c_ysum"), sem("c_stored")
        with nc.Block() as block:
            @block.sync
            def _(sp):
                for g in range(GROUPS):
                    sp.dma_start(rs[g][:], resid[:, g]).then_inc(in_ready[g], 16)
                    if g >= 4:
                        sp.wait_ge(ysum, g - 3)
                    sp.dma_start(yt[g % 4][:], ys[:, g]).then_inc(in_ready[g], 16)
                sp.wait_ge(stored, 16 * GROUPS)

            @block.vector
            def _(dve):
                for g in range(GROUPS):
                    dve.wait_ge(in_ready[g], 32)
                    dve.tensor_tensor(rs[g][:], rs[g][:], yt[g % 4][:, :, 0:D], ALU.add
                                      ).then_inc(half, 1)
                    dve.wait_ge(half, g + 1)
                    dve.tensor_tensor(rs[g][:], rs[g][:], yt[g % 4][:, :, D:2 * D], ALU.add
                                      ).then_inc(ysum, 1)

            @block.scalar
            def _(act):
                for g in range(GROUPS):
                    act.wait_ge(ysum, g + 1)
                    act.dma_start(out[:, g], rs[g][:]).then_inc(stored, 16)


INS = ["attn_x", "attn_Wq", "attn_bq", "attn_Wk", "attn_bk", "attn_Wv", "attn_bv", "attn_Wp",
       "attn_bp", "ffn_gate_w", "ffn_gate_b", "ffn_w1", "ffn_b1", "ffn_w3", "ffn_b3", "ffn_w2",
       "ffn_b2", "ffn_sw1", "ffn_sb1", "ffn_sw3", "ffn_sb3", "ffn_sw2", "ffn_sb2"]


def kernel(**inputs):
    import numpy as np
    import concourse.bacc as bacc
    from concourse.bass_utils import run_bass_kernel_spmd

    nc = bacc.Bacc("TRN2", target_bir_lowering=False, num_devices=1)
    arrays, args = {}, []
    for name in INS:
        a = np.ascontiguousarray(inputs["L0_" + name])
        arrays["in_" + name] = a
        args.append(nc.dram_tensor("in_" + name, a.shape, mybir.dt.from_np(a.dtype),
                                   kind="ExternalInput").ap())
    shape = [GROUPS, GT * P, D]
    args.append(nc.dram_tensor("out", shape, F32, kind="ExternalOutput").ap())
    xs = [nc.dram_tensor(f"xs{n}", [SLOT_TILES * P, ROW], F32).ap() for n in range(2)]
    ys = nc.dram_tensor("ys", [TOKENS * K_TOP + PADS * P, D], F32).ap()
    resid = nc.dram_tensor("resid", shape, F32).ap()
    x3 = nc.dram_tensor("x3", shape, F32).ap()
    build(nc, *args, xs, ys, resid, x3)
    r = run_bass_kernel_spmd(nc, [arrays], core_ids=[0])
    return r.results[0]["out"]
```

```python
from contextlib import ExitStack, contextmanager

import concourse.bass as bass
from concourse import mybir

F32 = mybir.dt.float32
F32R = mybir.dt.float32r
BF16 = mybir.dt.bfloat16
I32 = mybir.dt.int32
U32 = mybir.dt.uint32
ACT = mybir.ActivationFunctionType
ALU = mybir.AluOpType
AX = mybir.AxisListType.X
ds = bass.ds

P = 128
D = 128
HEAD_DIM = 8
E = 16
INTER = 176
UP = 2 * INTER
SH = 352
GROUPS = 8
GT = 8
TILES = GROUPS * GT
TOKENS = TILES * P
K_TOP = 2
SLOT_TILES = TOKENS * K_TOP // P + E
PAIRS = SLOT_TILES // 2
ROW = D + 2
CHUNK = 4
CHUNKS = TILES // CHUNK
FEAT = [(0, 128), (128, 128), (256, 96)]
A0 = 96
A1 = INTER - A0
EPS = 1e-5
RING = 8
PADS = 2 * RING
MAGIC = float(3 << 22)


@contextmanager
def phase(nc):
    sems = []

    def sem(name):
        sems.append(nc.alloc_semaphore(name=name))
        return sems[-1]
    yield sem
    nc.clear_and_free_semaphores(sems)
    nc.all_engine_barrier()


def wait(eng, sem, value):
    if not (isinstance(value, int) and value <= 0):
        eng.wait_ge(sem, value)


def build(nc, x, wq, bq, wk, bk, wv, bv, wp, bp, gate_w, gate_b, w1, b1, w3, b3, w2, b2,
          sw1, sb1, sw3, sb3, sw2, sb2, out, xs_dram, ys_dram, resid, x3):
    top = ExitStack()
    with top:
        def sb(name, shape, dt=F32, ctx=top):
            return ctx.enter_context(nc.sbuf_tensor(name, shape, dt))

        def ps(name, shape, ctx, dt=F32):
            return ctx.enter_context(nc.psum_tensor(name, shape, dt))

        def sem(name):
            return top.enter_context(nc.semaphore(name))

        class W:
            pass

        k = W()
        k.w13h, k.w13l = sb("w13h", [P, E * UP], F32R), sb("w13l", [P, E * UP], F32R)
        k.w2hl = sb("w2hl", [A0 + 1, 2, E, 2 * D], F32R)
        k.b13 = sb("b13", [33, E * UP], F32R)
        k.sw13h, k.sw13l = sb("sw13h", [P, 2 * SH], F32R), sb("sw13l", [P, 2 * SH], F32R)
        k.sw2hl = sb("sw2hl", [P, 3, 2 * D], F32R)
        k.sb13 = sb("sb13", [P, 2, 3])
        k.wq, k.wkv, k.wp = sb("wq_s", [P, D]), sb("wkv_s", [P, 2 * D]), sb("wp_s", [P, D])
        k.bkvp = sb("bkvp", [33, 3 * D], F32R)
        k.bq = sb("bq_s", [P, 1])
        k.gw, k.gb = sb("gw_s", [P, E]), sb("gb_s", [P, E])
        k.ident = sb("ident", [P, P])
        k.onesr = sb("onesr", [33, P], F32R)
        k.tri, k.onesb = sb("tri", [P, P], BF16), sb("onesb", [P, P], BF16)
        k.blockdiag = sb("blockdiag", [P, P])
        k.iota_e, k.ones_e = sb("iota_e", [P, E]), sb("ones_e", [P, E])
        k.iota_j = sb("iota_j", [1, SLOT_TILES])
        k.carry = sb("carry", [P, E * TILES])
        k.nhalf = sb("nhalf", [P, GT])
        k.tile_expert = sb("tile_expert", [1, SLOT_TILES], I32)
        k.pads = sb("pads", [P, PADS, ROW])
        k.s_fill = [sem("fill0"), sem("fill1")]
        k.xs = xs_dram

        setup(nc, k, sb, ps, xs_dram, wq, bq, wk, bk, wv, bv, wp, bp, gate_w, gate_b,
              sw1, sb1, sw3, sb3, sw2, sb2)
        x_v = x.rearrange("b (p i) d -> p b i d", i=GT)
        out_v = out.rearrange("b (p i) d -> p b i d", i=GT)
        resid_v = resid.rearrange("b (p i) d -> p b i d", i=GT)
        x3_v = x3.rearrange("b (p i) d -> p b i d", i=GT)
        ys_v = ys_dram.rearrange("(r c) d -> r (c d)", c=K_TOP)[0:TOKENS, :]
        ys_v = ys_v.rearrange("(b p i) d -> p b i d", i=GT, p=P)
        for n, src in enumerate((x_v, x3_v)):
            with ExitStack() as ctx:
                xrow = sb(f"xrow{n}", [P, TILES, ROW], ctx=ctx)
                r_ = W()
                r_.onehot = [sb(f"onehot{n}{q}", [P, TILES, E], BF16, ctx) for q in range(K_TOP)]
                r_.mask = sb(f"mask{n}", [P, TILES, E], BF16, ctx)
                r_.ssum, r_.second = (sb(f"{m}{n}", [P, TILES], ctx=ctx)
                                      for m in ("ssum", "second"))
                norm_and_gate(nc, k, sb, ps, n, src, xrow, r_,
                              (w1, b1, w3, b3, w2, b2) if n == 0 else None)
                route_and_share(nc, k, sb, ps, n, src, xrow, r_, xs_dram[n], resid_v)
            experts(nc, k, sb, ps, n, xs_dram[n], ys_dram)
            if n == 0:
                attention(nc, k, sb, ps, resid_v, ys_v, x3_v)
        combine(nc, k, sb, resid_v, ys_v, out_v)


FILLS = SLOT_TILES // PADS


def fill(eng, k, xs, n, a):
    rows = xs.rearrange("(a j p) c -> p a j c", j=PADS, p=P)
    eng.dma_start(rows[:, ds(a, 1)].rearrange("p a j c -> p (a j) c"), k.pads[:]
                  ).then_inc(k.s_fill[n], 16)


def setup(nc, k, sb, ps, xs_dram, wq, bq, wk, bk, wv, bv, wp, bp, gate_w, gate_b,
          sw1, sb1, sw3, sb3, sw2, sb2):
    with phase(nc) as sem, ExitStack() as ctx:
        raws13 = sb("raws13", [P, 2 * SH], ctx=ctx)
        raws2 = sb("raws2", [P, 3, D], ctx=ctx)
        rawa = sb("rawa", [33, 3 * D], ctx=ctx)
        zeroed, loaded, small = sem("su_zeroed"), sem("su_loaded"), sem("su_small")
        hi, built, base = sem("su_hi"), sem("su_built"), sem("su_base")
        halves = [
            (raws13[:], k.sw13h[:], k.sw13l[:]),
            (raws2[:, 0:2], k.sw2hl[:, 0:2, 0:D], k.sw2hl[:, 0:2, D:2 * D]),
            (raws2[0:97, 2], k.sw2hl[0:97, 2, 0:D], k.sw2hl[0:97, 2, D:2 * D]),
        ]
        loads = [
            (raws13[:, 0:SH], sw1), (raws13[:, SH:2 * SH], sw3),
            (raws2[:, 0:2], sw2[0:256, :].rearrange("(c p) d -> p c d", p=P)),
            (raws2[0:96, 2], sw2[256:SH, :]),
            (raws2[96:97, 2], sb2.rearrange("(a n) -> a n", a=1)),
        ]
        for r in (0, 32):
            loads += [(rawa[r:r + 1, m * D:(m + 1) * D], b.rearrange("(a n) -> a n", a=1))
                      for m, b in enumerate((bk, bv, bp))]
        smalls = [(k.gw[:], gate_w), (k.gb[:], gate_b.partition_broadcast(P)),
                  (k.wq[:], wq), (k.wkv[:, 0:D], wk), (k.wkv[:, D:2 * D], wv), (k.wp[:], wp),
                  (k.bq[:], bq.rearrange("(p a) -> p a", a=1))]
        for m, b in enumerate((sb1, sb3)):
            smalls += [(k.sb13[0:w, m, f:f + 1], b[o:o + w].rearrange("(p a) -> p a", a=1))
                       for f, (o, w) in enumerate(FEAT)]
        with nc.Block() as block:
            @block.sync
            def _(sp):
                sp.wait_ge(zeroed, 1)
                for dst, src in loads:
                    sp.dma_start(dst, src).then_inc(loaded, 16)

            @block.gpsimd
            def _(pool):
                pool.memset(k.ident[:], 0.0)
                pool.memset(k.tri[:], 1.0)
                pool.memset(k.blockdiag[:], 1.0)
                pool.memset(k.onesb[:], 1.0)
                pool.memset(k.ones_e[:], 1.0)
                pool.memset(k.nhalf[:], -0.5)
                pool.memset(k.pads[:], 0.0)
                pool.memset(k.carry[:], 1.0).then_inc(base, 1)
                pool.wait_ge(base, 1)
                pool.affine_select(out=k.ident[:], in_=k.ident[:], compare_op=ALU.not_equal,
                                   fill=1.0, base=0, pattern=[[-1, P]], channel_multiplier=1)
                pool.affine_select(out=k.tri[:], in_=k.tri[:], compare_op=ALU.is_ge, fill=0.0,
                                   base=-1, pattern=[[1, P]], channel_multiplier=-1)
                heads = k.blockdiag[:].rearrange("p (a c) -> p a c", c=HEAD_DIM)
                pool.affine_select(out=heads, in_=heads, compare_op=ALU.is_ge, fill=0.0, base=0,
                                   pattern=[[-HEAD_DIM, D // HEAD_DIM], [0, HEAD_DIM]],
                                   channel_multiplier=1).then_inc(base, 1)
                pool.wait_ge(base, 2)
                pool.affine_select(out=heads, in_=heads, compare_op=ALU.is_ge, fill=0.0,
                                   base=HEAD_DIM - 1,
                                   pattern=[[HEAD_DIM, D // HEAD_DIM], [0, HEAD_DIM]],
                                   channel_multiplier=-1)
                pool.memset(k.carry[:].rearrange("p (e t) -> p e t", e=E)[:, :, 0:1], 0.0)
                pool.iota(k.iota_e[:], pattern=[[1, E]], base=0, channel_multiplier=0,
                          allow_small_or_imprecise_dtypes=True)
                pool.iota(k.iota_j[:], pattern=[[1, SLOT_TILES]], base=0, channel_multiplier=0,
                          allow_small_or_imprecise_dtypes=True)
                pool.iota(k.pads[:, :, D:D + 1].bitcast(I32).rearrange("p j a -> p (j a)"),
                          pattern=[[P, PADS]], base=TOKENS * K_TOP, channel_multiplier=1)

            @block.vector
            def _(dve):
                dve.memset(rawa[:], 0.0).then_inc(zeroed, 1)
                dve.memset(k.onesr[:].bitcast(F32), 1.0)
                for m, (raw, h, l) in enumerate(halves):
                    dve.wait_ge(hi, m + 1)
                    dve.tensor_tensor(l, raw, h.bitcast(F32), ALU.subtract)
                dve.wait_ge(hi, len(halves) + 1)
                dve.tensor_tensor(k.bkvp[32:33], rawa[32:33], k.bkvp[32:33].bitcast(F32),
                                  ALU.subtract)

            @block.scalar
            def _(act):
                for dst, src in smalls:
                    act.dma_start(dst, src).then_inc(small, 16)
                act.wait_ge(loaded, 16 * len(loads))
                for raw, h, _l in halves:
                    act.activation(h, raw, ACT.Copy).then_inc(hi, 1)
                act.activation(k.bkvp[:], rawa[:], ACT.Copy).then_inc(hi, 1)
                act.wait_ge(small, 16 * len(smalls))


def norm_and_gate(nc, k, sb, ps, n, src, xrow, r_, weights):
    with phase(nc) as sem, ExitStack() as ctx:
        xh = [sb(f"a{n}_xh{r}", [P, GT, D], ctx=ctx) for r in range(2)]
        xt = [sb(f"a{n}_xt{r}", [P, GT * P], ctx=ctx) for r in range(2)]
        st = sb(f"a{n}_st", [P, GT, 6], ctx=ctx)
        mv, ve = sb(f"a{n}_mv", [P, GT, 2], ctx=ctx), sb(f"a{n}_ve", [P, GT], ctx=ctx)
        rs = [sb(f"a{n}_rs{r}", [P, GT], ctx=ctx) for r in range(2)]
        nm = [sb(f"a{n}_nm{r}", [P, GT], ctx=ctx) for r in range(2)]
        lgt, dev, ex = (sb(f"a{n}_{m}", [P, GT, E], ctx=ctx) for m in ("lgt", "dev", "ex"))
        m8, i8 = sb(f"a{n}_m8", [P, GT, 8], ctx=ctx), sb(f"a{n}_i8", [P, GT, 8], U32, ctx)
        idx = sb(f"a{n}_idx", [P, GT, 2], ctx=ctx)
        pt = [ps(f"a{n}_pt{r}", [P, GT * P], ctx) for r in range(2)]
        pl = [ps(f"a{n}_pl{r}", [P, 512], ctx) for r in range(2)]
        if weights:
            w1, b1, w3, b3, w2, b2 = weights
            raw13 = [sb(f"raw13{r}", [P, 2, UP], ctx=ctx) for r in range(2)]
            raw2 = [sb(f"raw2{r}", [A0 + 1, 2, 2, D], ctx=ctx) for r in range(2)]
            rawb = [sb(f"rawb{r}", [33, 2, UP], ctx=ctx) for r in range(2)]
        in_ready = [sem(f"a{n}_in{r}") for r in range(2)]
        kept = [sem(f"a{n}_kept{r}") for r in range(2)]
        w_in = [sem(f"a{n}_win{r}") for r in range(2)]
        names = ("stats", "aggr", "var", "rstd", "nmr", "passed", "xh", "xpose", "xt", "gate",
                 "lgr", "maxed", "found", "idxr", "onehots", "devr", "exr", "summed", "whi",
                 "wlo", "blo", "zeroed")
        (stats, aggr, var, rstd, nmr, passed, xh_ready, xpose, xt_ready, gate, lg_ready, maxed,
         found, idx_ready, onehots, dev_ready, ex_ready, summed, whi, wlo, blo, zeroed) = (
            sem(f"a{n}_{s}") for s in names)

        def steps(eng, step):
            for g in (-1, 0, 1):
                step(g, g)
            with eng.Fori(0, 2) as i:
                step(2, 2 * i + 2)
                step(3, 2 * i + 3)
            for g in (6, 7, 8):
                step(g, g)

        def turn(s, g, r):
            return 16 * (s // 2 + 1) if isinstance(g, int) else 8 * (g - r) + 16

        def wslices(r, g):
            es = ds(2 * g, 2)
            w13h, w13l = (w[:, ds(2 * g * UP, 2 * UP)] for w in (k.w13h, k.w13l))
            out = [(raw13[r][:].rearrange("p e n -> p (e n)"), w13h, w13l)]
            for c, rows in ((0, A0 + 1), (1, A0)):
                out.append((raw2[r][0:rows, c], k.w2hl[0:rows, c, es, 0:D],
                            k.w2hl[0:rows, c, es, D:2 * D]))
            return out

        with nc.Block() as block:
            @block.sync
            def _(sp):
                def load_weights(s, g):
                    r, es = s % 2, ds(2 * g, 2)
                    wait(sp, wlo, g - 1)
                    wait(sp, blo, g - 1)
                    parts = [
                        (raw13[r][:, :, 0:INTER], w1[es].rearrange("e d n -> d e n")),
                        (raw13[r][:, :, INTER:UP], w3[es].rearrange("e d n -> d e n")),
                        (raw2[r][0:A0, 0], w2[es, 0:A0, :].rearrange("e k d -> k e d")),
                        (raw2[r][2 * A0 - INTER:A0, 1],
                         w2[es, A0:INTER, :].rearrange("e k d -> k e d")),
                        (raw2[r][A0:A0 + 1, 0], b2[es].rearrange("(a e) d -> a e d", a=1))]
                    for row in (0, 32):
                        parts += [
                            (rawb[r][row:row + 1, :, 0:INTER],
                             b1[es].rearrange("(a e) n -> a e n", a=1)),
                            (rawb[r][row:row + 1, :, INTER:UP],
                             b3[es].rearrange("(a e) n -> a e n", a=1))]
                    for dst, part in parts:
                        sp.dma_start(dst, part).then_inc(w_in[r], 16)

                def step(s, g):
                    if s < 0:
                        if weights:
                            sp.wait_ge(zeroed, 1)
                            load_weights(0, 0)
                            load_weights(1, 1)
                    elif s < 8:
                        sp.wait_ge(xh_ready, g + 1)
                        sp.dma_start(xrow[:, ds(g * GT, GT), 0:D], xh[s % 2][:]
                                     ).then_inc(kept[s % 2], 16)
                        if weights and 1 <= s < 7:
                            load_weights(s + 1, g + 1)
                    if weights and s >= 0:
                        fill(sp, k, k.xs[0], 0, g)
                steps(sp, step)
                for r in range(2):
                    sp.wait_ge(kept[r], 16 * GROUPS // 2)

            @block.vector
            def _(dve):
                if weights:
                    for r in range(2):
                        dve.memset(rawb[r][:], 0.0)
                        last = dve.memset(raw2[r][0:32, 1], 0.0)
                    last.then_inc(zeroed, 1)

                def step(s, g):
                    if s < 7:
                        r = (s + 1) % 2
                        dve.wait_ge(in_ready[r], turn(s + 1, g if isinstance(g, int) else g + 1,
                                                      r))
                        dve.sem_inc(passed, 1)
                        xg = xrow[:, ds((g + 1) * GT, GT), 0:D]
                        for t in range(GT):
                            last = dve.bn_stats(st[:, t], xg[:, t])
                        last.then_inc(stats, 1)
                        dve.wait_ge(stats, g + 2)
                        dve.sem_inc(passed, 1)
                        for t in range(GT):
                            last = dve.bn_aggr(mv[:, t], st[:, t])
                        last.then_inc(aggr, 1)
                        dve.wait_ge(aggr, g + 2)
                        dve.tensor_scalar(ve[:], mv[:, :, 1], EPS, None, ALU.add
                                          ).then_inc(var, 1)
                    if s >= 1:
                        h = ds((g - 1) * GT, GT)
                        dve.wait_ge(gate, g)
                        dve.tensor_tensor(
                            lgt[:], pl[(s - 1) % 2][:, 0:GT * E].rearrange("p (t e) -> p t e",
                                                                           e=E),
                            k.gb[:].unsqueeze(1).to_broadcast([P, GT, E]), ALU.add
                            ).then_inc(lg_ready, 1)
                        dve.wait_ge(lg_ready, g)
                        dve.sem_inc(passed, 1)
                        for t in range(GT):
                            last = dve.max(m8[:, t], lgt[:, t])
                        last.then_inc(maxed, 1)
                        dve.wait_ge(maxed, g)
                        dve.sem_inc(passed, 1)
                        for t in range(GT):
                            last = dve.max_index(i8[:, t], m8[:, t], lgt[:, t])
                        last.then_inc(found, 1)
                        wait(dve, ex_ready, g - 1)
                        dve.tensor_tensor(dev[:], lgt[:],
                                          m8[:, :, 0:1].to_broadcast([P, GT, E]), ALU.subtract
                                          ).then_inc(dev_ready, 1)
                        dve.tensor_tensor(r_.second[:, h], m8[:, :, 1], m8[:, :, 0],
                                          ALU.subtract)
                        dve.wait_ge(found, g)
                        dve.tensor_copy(idx[:], i8[:, :, 0:2]).then_inc(idx_ready, 1)
                    if s < 7:
                        dve.wait_ge(rstd, g + 2)
                        dve.scalar_tensor_tensor(nm[(s + 1) % 2][:], mv[:, :, 0], -1.0,
                                                 rs[(s + 1) % 2][:], ALU.mult, ALU.mult
                                                 ).then_inc(nmr, 1)
                    if s >= 1:
                        h = ds((g - 1) * GT, GT)
                        iota = k.iota_e[:].unsqueeze(1).to_broadcast([P, GT, E])
                        dve.wait_ge(idx_ready, g)
                        for q, oh in enumerate(r_.onehot):
                            last = dve.tensor_tensor(
                                oh[:, h], iota, idx[:, :, q:q + 1].to_broadcast([P, GT, E]),
                                ALU.is_equal)
                        last.then_inc(onehots, 1)
                        dve.wait_ge(onehots, g)
                        dve.tensor_tensor(r_.mask[:, h], r_.onehot[0][:, h], r_.onehot[1][:, h],
                                          ALU.add)
                        dve.wait_ge(ex_ready, g)
                        dve.reduce_sum(r_.ssum[:, h], ex[:], AX).then_inc(summed, 1)
                    if weights and s >= 1:
                        dve.wait_ge(whi, g)
                        b = k.b13[32:33, ds((g - 1) * 2 * UP, 2 * UP)]
                        dve.tensor_tensor(b, rawb[(s - 1) % 2][32:33].rearrange("p e n -> p (e n)"),
                                          b.bitcast(F32), ALU.subtract).then_inc(blo, 1)
                steps(dve, step)

            @block.gpsimd
            def _(pool):
                def step(s, g):
                    if s < 7:
                        r = (s + 1) % 2
                        pool.wait_ge(var, g + 2)
                        wait(pool, xh_ready, g)
                        pool.tensor_tensor(rs[r][:], ve[:], k.nhalf[:], ALU.pow
                                           ).then_inc(rstd, 1)
                    if weights and s >= 1:
                        pool.wait_ge(whi, g)
                        for raw, h, l in wslices((s - 1) % 2, g - 1):
                            last = pool.tensor_tensor(l, raw, h.bitcast(F32), ALU.subtract)
                        last.then_inc(wlo, 1)
                steps(pool, step)

            @block.scalar
            def _(act):
                def load(s, g):
                    act.dma_start(xrow[:, ds(g * GT, GT), 0:D],
                                  src[:, ds(g, 1)].rearrange("p b i d -> p (b i) d")
                                  ).then_inc(in_ready[s % 2], 16)

                load(0, 0)
                load(1, 1)

                def step(s, g):
                    if 0 <= s < 6:
                        load(s + 2, g + 2)
                    if 0 <= s < 8:
                        act.wait_ge(xpose, g + 1)
                        wait(act, gate, g - 1)
                        act.activation(xt[s % 2][:], pt[s % 2][:], ACT.Copy).then_inc(xt_ready, 1)
                    if s >= 1:
                        act.wait_ge(dev_ready, g)
                        wait(act, summed, g - 1)
                        act.activation(ex[:], dev[:], ACT.Exp).then_inc(ex_ready, 1)
                    if s < 7:
                        r = (s + 1) % 2
                        act.wait_ge(nmr, g + 2)
                        wait(act, xpose, g)
                        if s >= 1:
                            act.wait_ge(kept[r], turn(s + 1, g if isinstance(g, int) else g + 1,
                                                      r) - 16)
                        act.sem_inc(passed, 1)
                        xg = xrow[:, ds((g + 1) * GT, GT), 0:D]
                        for t in range(GT):
                            last = act.activation(xh[r][:, t], xg[:, t], ACT.Identity,
                                                  bias=nm[r][:, t:t + 1], scale=rs[r][:, t:t + 1])
                        last.then_inc(xh_ready, 1)
                    if weights and 0 <= s < 8:
                        r = s % 2
                        act.wait_ge(w_in[r], 9 * turn(s, g, r))
                        act.sem_inc(passed, 1)
                        for raw, h, _l in wslices(r, g):
                            act.activation(h, raw, ACT.Copy)
                        act.activation(k.b13[:, ds(2 * g * UP, 2 * UP)],
                                       rawb[r][:].rearrange("p e n -> p (e n)"), ACT.Copy
                                       ).then_inc(whi, 1)
                steps(act, step)

            @block.tensor
            def _(pe):
                def step(s, g):
                    if 0 <= s < 8:
                        r = s % 2
                        pe.wait_ge(xt_ready, g + 1)
                        wait(pe, lg_ready, g - 1)
                        for t in range(GT):
                            last = pe.matmul(pl[r][:, t * E:(t + 1) * E],
                                             xt[r][:, t * P:(t + 1) * P], k.gw[:], start=True,
                                             stop=True)
                        last.then_inc(gate, 1)
                    if s < 7:
                        r = (s + 1) % 2
                        pe.wait_ge(xh_ready, g + 2)
                        wait(pe, xt_ready, g)
                        for t in range(GT):
                            last = pe.transpose(pt[r][:, t * P:(t + 1) * P], xh[r][:, t],
                                                k.ident[:])
                        last.then_inc(xpose, 1)
                steps(pe, step)


def route_and_share(nc, k, sb, ps, n, src, xrow, r_, xs, resid):
    N = TILES * E
    with phase(nc) as sem, ExitStack() as ctx:
        def t(name, shape, dt=F32):
            return sb(f"r{n}_{name}", shape, dt, ctx)

        mask = r_.mask[:].rearrange("p t e -> p (t e)")
        rec, wtop, wsec = (t(s, [P, TILES]) for s in ("rec", "wtop", "wsec"))
        mx = [t(f"mx{q}", [P, TILES]) for q in range(K_TOP)]
        slot = [t(f"slot{q}", [P, TILES], I32) for q in range(K_TOP)]
        need, ends, starts = (t(s, [P, E]) for s in ("need", "ends", "starts"))
        texp = t("texp", [1, SLOT_TILES])
        xs_in = [t(f"xs{r}", [P, CHUNK, D]) for r in range(2)]
        rx = [t(f"rx{r}", [P, CHUNK, D]) for r in range(2)]
        ro = [t(f"ro{r}", [P, CHUNK, D]) for r in range(2)]
        xth = [t(f"xth{r}", [P, 512], F32R) for r in range(2)]
        with ExitStack() as early:
            tmp, prod = (sb(f"r{n}_{s}", [P, TILES, E], F32, early) for s in ("tmp", "prod"))
            tot, incl = (sb(f"r{n}_{s}", [P, E, TILES], F32, early) for s in ("tot", "incl"))
        xtl = [t(f"xtl{r}", [P, 512], F32R) for r in range(2)]
        sil = [t(f"sil{r}", [P, 512]) for r in range(2)]
        act_f = [t(f"actf{r}", [P, 512]) for r in range(2)]
        ah, al = (t(s, [P, 3, 512], F32R) for s in ("ah", "al"))
        p_x = ps(f"r{n}_px", [P, 512], ctx)
        p_hg = [ps(f"r{n}_phg{r}", [P, 512], ctx) for r in range(3)]
        p_z = [ps(f"r{n}_pz{r}", [P, 2, 512], ctx) for r in range(2)]
        p_tot, p_pre = p_z

        names = ("chain", "tot_mm", "tot_done", "pre_mm", "pre_used", "slots_ready", "w_ready",
                 "sent0", "payload", "sent1", "exp2")
        (chain, tot_mm, tot_done, pre_mm, pre_used, slots_ready, w_ready, sent0, payload, sent1,
         exp2) = (sem(f"r{n}_{s}") for s in names)
        names = ("xpose", "hi", "lo", "up_h", "up", "silu", "aa", "ahi", "alo", "down", "outr", "outh")
        (xpose, hi, lo, up_h, up, silu, aa, ahi, alo, down, outr, outh) = (
            sem(f"s{n}_{s}") for s in names)
        in_ready = [sem(f"s{n}_in{r}") for r in range(2)]
        rx_ready = [sem(f"s{n}_rx{r}") for r in range(2)]
        stored = [sem(f"s{n}_st{r}") for r in range(2)]

        def steps(eng, step, first=-1, after=1):
            for c in range(first, 2):
                step(c, c)
            with eng.Fori(0, 6) as i:
                step(2, 2 * i + 2)
                step(3, 2 * i + 3)
            for c in range(14, CHUNKS + after):
                step(c, c)

        def turn(c, cv, r):
            return 16 * (c // 2 + 1) if isinstance(cv, int) else 8 * (cv - r) + 16

        def chunk_of(ap, c, cv):
            b = cv // 2 if isinstance(cv, int) else None
            h = c % 2
            if b is None:
                b = (cv - h) // 2
            return ap[:, ds(b, 1), h * CHUNK:(h + 1) * CHUNK].rearrange("p b i d -> p (b i) d")

        with nc.Block() as block:
            @block.sync
            def _(sp):
                def load_x(c, cv):
                    sp.dma_start(xs_in[c % 2][:], xrow[:, ds(cv * CHUNK, CHUNK), 0:D]
                                 ).then_inc(in_ready[c % 2], 16)

                def step(c, cv):
                    r = c % 2
                    if c < CHUNKS - 1:
                        wait(sp, xpose, cv)
                        load_x(c + 1, cv + 1)
                    if c < CHUNKS:
                        wait(sp, outr, cv - 1)
                        sp.dma_start(rx[r][:], chunk_of(src, c, cv)).then_inc(rx_ready[r], 16)
                    if c >= 2:
                        wait(sp, outr, cv - 1)
                        sp.dma_start(chunk_of(resid, c, cv - 2), ro[r][:]
                                     ).then_inc(stored[r], 16)
                load_x(0, 0)
                steps(sp, step, first=0, after=2)
                for r in range(2):
                    sp.wait_ge(stored[r], 16 * CHUNKS // 2)

            @block.gpsimd
            def _(pool):
                rows = xrow[:, :, D:D + 1].bitcast(I32).rearrange("p (b i) a -> p b (i a)", i=GT)
                pool.iota(rows, pattern=[[2 * GT * P, GROUPS], [2, GT]], base=0,
                          channel_multiplier=2 * GT).then_inc(payload, 1)
                pool.wait_ge(w_ready, 1)
                pool.wait_ge(k.s_fill[n], 16 * FILLS)
                pool.wait_ge(slots_ready, 1)
                pool.wait_ge(payload, 1)
                for q in range(TILES):
                    pool.indirect_dma_start(xs, bass.IndirectOffsetOnAxis(slot[0][:, q:q + 1], 0),
                                            xrow[:, q, :], None).then_inc(sent0, 16)
                pool.wait_ge(sent0, 16 * TILES)
                pool.iota(rows, pattern=[[2 * GT * P, GROUPS], [2, GT]], base=1,
                          channel_multiplier=2 * GT).then_inc(payload, 1)
                pool.wait_ge(w_ready, 2)
                pool.wait_ge(slots_ready, 2)
                pool.tensor_copy(xrow[:, :, D + 1:D + 2], wsec[:].unsqueeze(2)
                                 ).then_inc(payload, 1)
                pool.wait_ge(payload, 3)
                for q in range(TILES):
                    pool.indirect_dma_start(xs, bass.IndirectOffsetOnAxis(slot[1][:, q:q + 1], 0),
                                            xrow[:, q, :], None).then_inc(sent1, 16)
                pool.wait_ge(sent1, 16 * TILES)

            @block.vector
            def _(dve):
                links = [0]

                def link(ins):
                    links[0] += 1
                    ins.then_inc(chain, 1)
                    dve.wait_ge(chain, links[0])

                by_te = incl[:].rearrange("p e t -> p t e")
                dve.memset(ah[96:97, 2].bitcast(F32), 1.0)
                dve.memset(al[96:97, 2].bitcast(F32), 0.0)
                link(dve.reciprocal(rec[:], r_.ssum[:]))
                dve.tensor_scalar(xrow[:, :, D + 1:D + 2], rec[:].unsqueeze(2), 0.5, None,
                                  ALU.mult).then_inc(w_ready, 1)
                dve.wait_ge(exp2, 1)
                dve.scalar_tensor_tensor(wsec[:], rec[:], 0.5, wtop[:], ALU.mult, ALU.mult
                                         ).then_inc(w_ready, 1)
                dve.wait_ge(tot_done, 1)
                link(dve.tensor_tensor_scan(incl[:].rearrange("p e t -> p (e t)"), k.carry[:],
                                            tot[:].rearrange("p e t -> p (e t)"), 0.0,
                                            ALU.mult, ALU.add))
                link(dve.tensor_scalar(need[:], incl[:, :, TILES - 1], 63.5, 1.0 / P, ALU.add,
                                       ALU.mult))
                link(dve.tensor_scalar(need[:], need[:], MAGIC, MAGIC, ALU.add, ALU.subtract))
                link(dve.tensor_tensor_scan(ends[:], k.ones_e[:], need[:], 0.0, ALU.mult,
                                            ALU.add))
                link(dve.tensor_tensor(starts[:], ends[:], need[:], ALU.subtract))
                link(dve.tensor_tensor(incl[:], incl[:], tot[:], ALU.subtract))
                link(dve.scalar_tensor_tensor(
                    incl[:], starts[:].unsqueeze(2).to_broadcast([P, E, TILES]), float(P),
                    incl[:], ALU.mult, ALU.add))
                dve.wait_ge(pre_mm, 1)
                dve.tensor_tensor(tmp[:], p_pre[:].rearrange("p a (t e) -> p (a t) e", e=E),
                                  by_te, ALU.add).then_inc(pre_used, 1)
                dve.wait_ge(pre_used, 1)
                for q in range(K_TOP):
                    link(dve.tensor_tensor(prod[:], r_.onehot[q][:], tmp[:], ALU.mult))
                    link(dve.reduce_sum(mx[q][:], prod[:], AX))
                    dve.tensor_copy(slot[q][:], mx[q][:]).then_inc(slots_ready, 1)

                def step(c, cv):
                    for f in range(3):
                        m, mv = 3 * c + f, 3 * cv + f
                        if 0 <= c < CHUNKS:
                            w = FEAT[f][1]
                            dve.wait_ge(silu, mv + 1)
                            dve.wait_ge(up, mv + 1)
                            wait(dve, alo, mv - 1)
                            dve.scalar_tensor_tensor(
                                act_f[m % 2][0:w], p_hg[(2 * m + 1) % 3][0:w], k.sb13[0:w, 1, f:f + 1],
                                sil[m % 2][0:w], ALU.add, ALU.mult).then_inc(aa, 1)
                        if 1 <= m <= 3 * CHUNKS:
                            g, w = (f - 1) % 3, FEAT[(f - 1) % 3][1]
                            dve.wait_ge(ahi, mv)
                            dve.tensor_tensor(al[0:w, g], act_f[(m - 1) % 2][0:w],
                                              ah[0:w, g].bitcast(F32), ALU.subtract
                                              ).then_inc(alo, 1)
                        if f == 1 and c < CHUNKS - 1:
                            r = (c + 1) % 2
                            dve.wait_ge(hi, cv + 2)
                            dve.tensor_tensor(xtl[r][:], p_x[:], xth[r][:].bitcast(F32),
                                              ALU.subtract).then_inc(lo, 1)
                        if f == 1 and c >= 1:
                            r = (c - 1) % 2
                            z = p_z[r][:].rearrange("p a (i n) -> p (a i) n", n=2 * D)
                            dve.wait_ge(down, 3 * cv)
                            dve.wait_ge(rx_ready[r], turn(c - 1, cv if isinstance(cv, int)
                                                          else cv - 1, r))
                            if c >= 3:
                                dve.wait_ge(stored[r], turn(c - 1, cv if isinstance(cv, int)
                                                            else cv - 1, r) - 16)
                            dve.scalar_tensor_tensor(rx[r][:], z[:, :, 0:D], 0.5, rx[r][:],
                                                     ALU.mult, ALU.add).then_inc(outh, 1)
                            dve.wait_ge(outh, cv)
                            dve.scalar_tensor_tensor(ro[r][:], z[:, :, D:2 * D], 0.5, rx[r][:],
                                                     ALU.mult, ALU.add).then_inc(outr, 1)
                steps(dve, step)
                link(dve.memset(texp[:], 0.0))
                for e in range(E):
                    link(dve.scalar_tensor_tensor(texp[:], k.iota_j[:], ends[0:1, e:e + 1],
                                                  texp[:], ALU.is_ge, ALU.add))
                dve.tensor_scalar(k.tile_expert[:], texp[:], float(E - 1), None, ALU.min)

            @block.scalar
            def _(act):
                act.activation(wtop[:], r_.second[:], ACT.Exp).then_inc(exp2, 1)
                act.wait_ge(tot_mm, 1)
                act.activation(tot[:].rearrange("p e t -> p t e"),
                               p_tot[:].rearrange("p a (t e) -> p (a t) e", e=E), ACT.Copy
                               ).then_inc(tot_done, 1)

                def step(c, cv):
                    for f in range(3):
                        m, mv = 3 * c + f, 3 * cv + f
                        if 0 <= c < CHUNKS:
                            w = FEAT[f][1]
                            act.wait_ge(up_h, mv + 1)
                            wait(act, aa, mv - 1)
                            act.activation(sil[m % 2][0:w], p_hg[2 * m % 3][0:w], ACT.Silu,
                                           bias=k.sb13[0:w, 0, f:f + 1]).then_inc(silu, 1)
                        if 1 <= m <= 3 * CHUNKS:
                            g, w = (f - 1) % 3, FEAT[(f - 1) % 3][1]
                            act.wait_ge(aa, mv)
                            wait(act, down, mv - 3)
                            act.activation(ah[0:w, g], act_f[(m - 1) % 2][0:w], ACT.Copy
                                           ).then_inc(ahi, 1)
                        if f == 1 and c < CHUNKS - 1:
                            r = (c + 1) % 2
                            act.wait_ge(xpose, cv + 2)
                            wait(act, up, 3 * cv)
                            act.activation(xth[r][:], p_x[:], ACT.Copy).then_inc(hi, 1)
                steps(act, step)

            @block.tensor
            def _(pe):
                def step(c, cv):
                    for f in range(3):
                        m, mv = 3 * c + f, 3 * cv + f
                        if 0 <= c < CHUNKS:
                            r = c % 2
                            o, w = FEAT[f]
                            if f == 0:
                                pe.wait_ge(lo, cv + 1)
                            for g in range(2):
                                if g == 0:
                                    wait(pe, aa, mv - 1)
                                else:
                                    wait(pe, silu, mv)
                                cols = slice(g * SH + o, g * SH + o + w)
                                parts = ((k.sw13h, xth), (k.sw13h, xtl), (k.sw13l, xth))
                                for q, (w_, x_) in enumerate(parts):
                                    last = pe.matmul(p_hg[(2 * m + g) % 3][0:w], w_[:, cols],
                                                     x_[r][:], start=q == 0, stop=q == 2)
                                last.then_inc((up_h, up)[g], 1)
                        if f == 0 and c < CHUNKS - 1:
                            r = (c + 1) % 2
                            pe.wait_ge(in_ready[r], turn(c + 1, cv if isinstance(cv, int)
                                                         else cv + 1, r))
                            wait(pe, lo, cv + 1)
                            for q in range(CHUNK):
                                last = pe.transpose(p_x[:, q * P:(q + 1) * P], xs_in[r][:, q],
                                                    k.ident[:])
                            last.then_inc(xpose, 1)
                        if 2 <= m <= 3 * CHUNKS + 1:
                            g = (f - 2) % 3
                            w = 97 if g == 2 else P
                            pe.wait_ge(alo, mv - 1)
                            if g == 0:
                                wait(pe, outr, cv - 1)
                            for q in range(CHUNK):
                                tok = slice(q * P, (q + 1) * P)
                                z, o = p_z[(m - 2) // 3 % 2][:, q // 2], (q % 2) * 2 * D
                                pe.matmul(z[:, o:o + 2 * D], ah[0:w, g, tok], k.sw2hl[0:w, g],
                                          start=g == 0 and q % 2 == 0, stop=False,
                                          skip_group_check=True)
                                last = pe.matmul(z[:, o:o + D], al[0:w, g, tok],
                                                 k.sw2hl[0:w, g, 0:D], start=False, stop=g == 2,
                                                 skip_group_check=True)
                            last.then_inc(down, 1)

                for h in range(2):
                    last = pe.matmul(p_tot[:, h], k.onesb[:], mask[:, h * 512:(h + 1) * 512],
                                     start=True, stop=True)
                last.then_inc(tot_mm, 1)
                for h in range(2):
                    last = pe.matmul(p_pre[:, h], k.tri[:], mask[:, h * 512:(h + 1) * 512],
                                     start=True, stop=True)
                last.then_inc(pre_mm, 1)
                step(-1, -1)
                pe.wait_ge(tot_done, 1)
                pe.wait_ge(pre_used, 1)
                steps(pe, step, first=0)


def experts(nc, k, sb, ps, n, xs, ys):
    with phase(nc) as sem, ExitStack() as ctx:
        xin = [sb(f"e{n}_x{r}", [P, 2, ROW], ctx=ctx) for r in range(RING)]
        y = [sb(f"e{n}_y{r}", [P, 2, D], ctx=ctx) for r in range(RING)]
        xth = [sb(f"e{n}_xth{r}", [P, 2 * P], F32R, ctx) for r in range(2)]
        xtl = [sb(f"e{n}_xtl{r}", [P, 2 * P], F32R, ctx) for r in range(2)]
        sil = [sb(f"e{n}_sil{r}", [P, 2, INTER], ctx=ctx) for r in range(2)]
        a = [sb(f"e{n}_a{r}", [P, 2, INTER], ctx=ctx) for r in range(2)]
        ah = [sb(f"e{n}_ah{r}", [A0 + 1, 512], F32R, ctx) for r in range(2)]
        al = [sb(f"e{n}_al{r}", [A0 + 1, 512], F32R, ctx) for r in range(2)]
        p_x = ps(f"e{n}_px", [P, 512], ctx)
        p_u = [ps(f"e{n}_pu{r}", [P, 2, 512], ctx) for r in range(2)]
        p_a = ps(f"e{n}_pa", [P, 512], ctx)
        p_y = ps(f"e{n}_py", [P, 512], ctx)
        names = ("xpose", "xhi", "xlo", "up", "silu", "aa", "apose", "ahi", "alo", "down", "yhi",
                 "yy", "passed")
        (xpose, xhi, xlo, up, silu, aa, apose, ahi, alo, down, yhi, yy, passed) = (
            sem(f"e{n}_{s}") for s in names)
        x_in = [sem(f"e{n}_in{r}") for r in range(RING)]
        sent = [sem(f"e{n}_sent{r}") for r in range(RING)]
        rows = xs.rearrange("(j t p) c -> p j t c", t=2, p=P)
        LOOPED = (PAIRS - RING) // RING

        def steps(eng, step, last):
            for j in range(-1, 3):
                step(j, j)
            with eng.Fori(0, LOOPED) as i:
                for u in range(RING):
                    step(3 + u, RING * i + (3 + u))
            for j in range(3 + RING * LOOPED, last):
                step(j, j)

        with nc.Block() as block:
            @block.sync
            def _(sp):
                for r in range(RING):
                    sp.dma_start(xin[r][:], rows[:, r]).then_inc(x_in[r], 16)
                with sp.Fori(1, PAIRS // RING) as i:
                    for r in range(RING):
                        sp.wait_ge(sent[r], 32 * i)
                        sp.dma_start(xin[r][:],
                                     rows[:, ds(RING * i + r, 1)].rearrange(
                                         "p j t c -> p (j t) c")).then_inc(x_in[r], 16)
                if n == 0:
                    for a in range(FILLS):
                        fill(sp, k, k.xs[1], 1, a)
                    sp.wait_ge(k.s_fill[1], 16 * FILLS)

            @block.gpsimd
            def _(pool):
                with pool.Fori(0, PAIRS // RING) as i:
                    for r in range(RING):
                        pool.wait_ge(yy, RING * i + (r + 1))
                        pool.sem_inc(passed, 1)
                        for t in range(2):
                            pool.indirect_dma_start(
                                ys, bass.IndirectOffsetOnAxis(
                                    xin[r][:, t, D:D + 1].bitcast(I32), 0),
                                y[r][:, t, :], None).then_inc(sent[r], 16)
                for r in range(RING):
                    pool.wait_ge(sent[r], 32 * (PAIRS // RING))

            @block.vector
            def _(dve):
                for r in range(2):
                    dve.memset(ah[r][A0:A0 + 1].bitcast(F32), 1.0)
                    dve.memset(al[r][A0:A0 + 1].bitcast(F32), 0.0)

                def step(j, jv):
                    if j < PAIRS - 1:
                        r = (j + 1) % 2
                        dve.wait_ge(xhi, jv + 2)
                        dve.tensor_tensor(xtl[r][:], p_x[:, 0:2 * P], xth[r][:].bitcast(F32),
                                          ALU.subtract).then_inc(xlo, 1)
                    if 0 <= j < PAIRS:
                        r = j % 2
                        dve.wait_ge(silu, jv + 1)
                        wait(dve, apose, jv - 1)
                        dve.tensor_tensor(a[r][:], p_u[r][:, :, INTER:UP], sil[r][:], ALU.mult
                                          ).then_inc(aa, 1)
                    if 1 <= j < PAIRS + 1:
                        r = (j - 1) % 2
                        dve.wait_ge(ahi, jv)
                        dve.tensor_tensor(al[r][0:A0], p_a[0:A0], ah[r][0:A0].bitcast(F32),
                                          ALU.subtract).then_inc(alo, 1)
                    if 2 <= j:
                        s = (j - 2) % RING
                        dve.wait_ge(yhi, jv - 1)
                        for t in range(2):
                            last = dve.scalar_tensor_tensor(
                                y[s][:, t], p_y[:, t * 2 * D + D:(t + 1) * 2 * D],
                                xin[s][:, t, D + 1:D + 2], y[s][:, t], ALU.mult, ALU.add)
                        last.then_inc(yy, 1)
                steps(dve, step, PAIRS + 2)

            @block.scalar
            def _(act):
                def step(j, jv):
                    if j < PAIRS - 1:
                        r = (j + 1) % 2
                        act.wait_ge(xpose, jv + 2)
                        wait(act, up, jv)
                        act.activation(xth[r][:], p_x[:, 0:2 * P], ACT.Copy).then_inc(xhi, 1)
                    if 0 <= j < PAIRS:
                        r = j % 2
                        act.wait_ge(up, jv + 1)
                        wait(act, aa, jv - 1)
                        act.activation(sil[r][:], p_u[r][:, :, 0:INTER], ACT.Silu
                                       ).then_inc(silu, 1)
                    if 1 <= j < PAIRS + 1:
                        r = (j - 1) % 2
                        act.wait_ge(apose, jv)
                        wait(act, down, jv - 2)
                        act.activation(ah[r][0:A0], p_a[0:A0], ACT.Copy).then_inc(ahi, 1)
                    if 2 <= j:
                        s = (j - 2) % RING
                        act.wait_ge(down, jv - 1)
                        for t in range(2):
                            last = act.activation(
                                y[s][:, t], p_y[:, t * 2 * D:t * 2 * D + D], ACT.Copy,
                                scale=xin[s][:, t, D + 1:D + 2])
                        last.then_inc(yhi, 1)
                steps(act, step, PAIRS + 2)

            @block.tensor
            def _(pe):
                expert = {}

                def load_experts(first, pairs):
                    expert.clear()
                    _, got = nc.values_load_multi_w_load_instructions(
                        k.tile_expert[0:1, ds(2 * first, 2 * len(pairs))],
                        engines=[mybir.EngineType.PE], min_val=0, max_val=E - 1,
                        skip_runtime_bounds_check_because="a count of 16 compares, at most 15")
                    for q, j in enumerate(pairs):
                        expert[j] = got[2 * q:2 * q + 2]

                def step(j, jv):
                    if j < PAIRS - 1:
                        s = (j + 1) % RING
                        turns = (16 * ((j + 1) // RING + 1) if isinstance(jv, int)
                                 else 16 * ((jv + (1 - s)) // RING + 1))
                        pe.wait_ge(x_in[s], turns)
                        wait(pe, xlo, jv + 1)
                        for t in range(2):
                            last = pe.transpose(p_x[:, t * P:(t + 1) * P], xin[s][:, t, 0:D],
                                                k.ident[:])
                        last.then_inc(xpose, 1)
                    if 0 <= j < PAIRS:
                        r = j % 2
                        pe.wait_ge(xlo, jv + 1)
                        wait(pe, aa, jv - 1)
                        for t in range(2):
                            cols = ds(expert[j][t] * UP, UP)
                            tok = slice(t * P, (t + 1) * P)
                            o = p_u[r][:, t, 0:UP]
                            pe.matmul(o, k.onesr[:], k.b13[:, cols], start=True, stop=False)
                            pe.matmul(o, xth[r][:, tok], k.w13h[:, cols], start=False, stop=False)
                            pe.matmul(o, xth[r][:, tok], k.w13l[:, cols], start=False, stop=False)
                            last = pe.matmul(o, xtl[r][:, tok], k.w13h[:, cols], start=False,
                                             stop=True)
                        last.then_inc(up, 1)
                    if 1 <= j < PAIRS + 1:
                        r = (j - 1) % 2
                        pe.wait_ge(aa, jv)
                        wait(pe, alo, jv - 1)
                        for t in range(2):
                            for c, o in enumerate((0, A1)):
                                q = 2 * t + c
                                last = pe.transpose(p_a[0:A0, q * P:(q + 1) * P],
                                                    a[r][:, t, o:o + A0], k.ident[:])
                        last.then_inc(apose, 1)
                    if 2 <= j:
                        r = j % 2
                        pe.wait_ge(alo, jv - 1)
                        wait(pe, yy, jv - 2)
                        for t in range(2):
                            for c, rows_ in enumerate((A0 + 1, A0)):
                                q = slice((2 * t + c) * P, (2 * t + c + 1) * P)
                                w2 = k.w2hl[0:rows_, c, ds(expert[j - 2][t], 1)].rearrange(
                                    "p e n -> p (e n)")
                                o = t * 2 * D
                                pe.matmul(p_y[:, o:o + 2 * D], ah[r][0:rows_, q], w2,
                                          start=c == 0, stop=False, skip_group_check=True)
                                last = pe.matmul(p_y[:, o:o + D], al[r][0:rows_, q], w2[:, 0:D],
                                                 start=False, stop=c == 1, skip_group_check=True)
                        last.then_inc(down, 1)

                load_experts(0, [0, 1, 2])
                for j in range(-1, 3):
                    step(j, j)
                with pe.Fori(0, LOOPED) as i:
                    load_experts(RING * i + 1, list(range(1, 3 + RING)))
                    for u in range(RING):
                        step(3 + u, RING * i + (3 + u))
                tail = 3 + RING * LOOPED
                load_experts(tail - 2, list(range(tail - 2, PAIRS)))
                for j in range(tail, PAIRS + 2):
                    step(j, j)


def attention(nc, k, sb, ps, resid, ys, x3):
    with phase(nc) as sem, ExitStack() as ctx:
        def t2(name, shape, dt=F32):
            return [sb(f"t_{name}{r}", shape, dt, ctx) for r in range(2)]

        xa = sb("t_xa", [P, TILES, D], ctx=ctx)
        yt, xt = t2("yt", [P, GT, 2 * D]), t2("xt", [P, GT * P])
        xh = sb("t_xh", [P, GT, D], ctx=ctx)
        rs, nm = t2("rs", [P, GT]), t2("nm", [P, GT])
        st, mv = sb("t_st", [P, GT, 6], ctx=ctx), sb("t_mv", [P, GT, 2], ctx=ctx)
        ve = sb("t_ve", [P, GT], ctx=ctx)
        phq, rq = (sb(f"t_{s}", [P, GT * P], ctx=ctx) for s in ("phq", "rq"))
        ek = sb("t_ek", [P, 4, D], ctx=ctx)
        phk, v = sb("t_phk", [P, GT, D], ctx=ctx), sb("t_v", [P, GT, D], ctx=ctx)
        kvt, kvp = sb("t_kvt", [P, D], ctx=ctx), sb("t_kvp", [P, D], ctx=ctx)
        p_t, p_q = ps("t_pt", [P, 2, 512], ctx), ps("t_pq", [P, 2, 512], ctx)
        p_kv = ps("t_pkv", [P, 2, 512], ctx)
        p_b, p_c = ps("t_pb", [P, 512], ctx), ps("t_pc", [P, 512], ctx)
        in_ready = [sem(f"t_in{r}") for r in range(2)]
        names = ("ysum", "x2r", "stats", "aggr", "var", "rstds", "nmr", "xhr", "xpose", "xtr",
                 "qmm", "mqr", "rqr", "eqr", "phqr", "kvmm", "mkr", "ekr", "phkr", "vtk", "kvtr",
                 "kvpmm", "kvpr", "omm", "x3r", "passed", "stored")
        s = {m: sem(f"t_{m}") for m in names}

        def steps(eng, step):
            for g in (-2, -1, 0, 1):
                step(g, g)
            with eng.Fori(0, 2) as i:
                step(2, 2 * i + 2)
                step(3, 2 * i + 3)
            for g in (6, 7, 8):
                step(g, g)

        def group(ap, gv):
            return ap[:, ds(gv, 1)].rearrange("p b i d -> p (b i) d")

        def tiles(gv):
            return xa[:, ds(gv * GT, GT)]

        k_of = p_kv[:].rearrange("p a (t n) -> p (a t) n", n=2 * D)[:, :, 0:D]
        v_of = p_kv[:].rearrange("p a (t n) -> p (a t) n", n=2 * D)[:, :, D:2 * D]
        q_of = p_q[:].rearrange("p a n -> p (a n)")

        with nc.Block() as block:
            @block.sync
            def _(sp):
                def load(g, gv):
                    sp.dma_start(tiles(gv), group(resid, gv)).then_inc(in_ready[g % 2], 16)
                    sp.dma_start(yt[g % 2][:], group(ys, gv)).then_inc(in_ready[g % 2], 16)

                def store(gv):
                    sp.wait_ge(s["x3r"], gv + 1)
                    sp.dma_start(group(x3, gv), tiles(gv)).then_inc(s["stored"], 16)

                def step(g, gv):
                    if g < 6:
                        wait(sp, s["x2r"], gv + 1)
                        load(g + 2, gv + 2)
                    if g >= 2:
                        store(gv - 2)
                steps(sp, step)
                store(GROUPS - 1)
                sp.wait_ge(s["stored"], 16 * GROUPS)

            @block.gpsimd
            def _(pool):
                def step(g, gv):
                    r = g % 2
                    if g < 6:
                        turns = 32 * ((g + 2) // 2 + 1) if isinstance(gv, int) else (
                            16 * (gv + 2 - r) + 32)
                        pool.wait_ge(in_ready[r], turns)
                        pool.tensor_tensor(yt[r][:, :, 0:D], yt[r][:, :, 0:D],
                                           yt[r][:, :, D:2 * D], ALU.add).then_inc(s["ysum"], 1)
                    if g >= 1:
                        pool.wait_ge(s["eqr"], gv)
                        pool.tensor_tensor(phq[:], phq[:], rq[:], ALU.add).then_inc(s["phqr"], 1)
                    if g < 6:
                        pool.wait_ge(s["var"], gv + 3)
                        wait(pool, s["xhr"], gv + 1)
                        pool.tensor_tensor(rs[r][:], ve[:], k.nhalf[:], ALU.pow
                                           ).then_inc(s["rstds"], 1)
                steps(pool, step)

            @block.vector
            def _(dve):
                def step(g, gv):
                    r = g % 2
                    if g >= 1:
                        dve.wait_ge(s["qmm"], gv)
                        wait(dve, s["omm"], gv - 1)
                        dve.tensor_scalar(phq[:], q_of, k.bq[:], 0.0, ALU.add, ALU.min
                                          ).then_inc(s["mqr"], 1)
                        dve.wait_ge(s["vtk"], gv)
                        wait(dve, s["kvpmm"], gv - 1)
                        dve.tensor_tensor(kvt[:], p_b[:, 0:D], k.blockdiag[:], ALU.mult
                                          ).then_inc(s["kvtr"], 1)
                    if g < 6:
                        x2 = tiles(gv + 2)
                        dve.wait_ge(s["ysum"], gv + 3)
                        dve.tensor_tensor(x2, x2, yt[r][:, :, 0:D], ALU.add
                                          ).then_inc(s["x2r"], 1)
                        dve.wait_ge(s["x2r"], gv + 3)
                        dve.sem_inc(s["passed"], 1)
                        for q in range(GT):
                            last = dve.bn_stats(st[:, q], x2[:, q])
                        last.then_inc(s["stats"], 1)
                    if 0 <= g < 8:
                        dve.wait_ge(s["kvmm"], 2 * gv + 1)
                        dve.tensor_scalar(ek[:], k_of, 0.0, None, ALU.min).then_inc(s["mkr"], 1)
                    if g < 6:
                        dve.wait_ge(s["stats"], gv + 3)
                        dve.sem_inc(s["passed"], 1)
                        for q in range(GT):
                            last = dve.bn_aggr(mv[:, q], st[:, q])
                        last.then_inc(s["aggr"], 1)
                        dve.wait_ge(s["aggr"], gv + 3)
                        dve.tensor_scalar(ve[:], mv[:, :, 1], EPS, None, ALU.add
                                          ).then_inc(s["var"], 1)
                    if 0 <= g < 8:
                        dve.wait_ge(s["ekr"], 2 * gv + 1)
                        wait(dve, s["vtk"], gv)
                        dve.scalar_tensor_tensor(phk[:, 0:4], k_of, 0.0, ek[:], ALU.max, ALU.add
                                                 ).then_inc(s["phkr"], 1)
                        dve.wait_ge(s["kvmm"], 2 * gv + 2)
                        dve.wait_ge(s["phkr"], 2 * gv + 1)
                        dve.tensor_scalar(ek[:], k_of, 0.0, None, ALU.min).then_inc(s["mkr"], 1)
                    if g < 6:
                        dve.wait_ge(s["rstds"], gv + 3)
                        dve.scalar_tensor_tensor(nm[r][:], mv[:, :, 0], -1.0, rs[r][:], ALU.mult,
                                                 ALU.mult).then_inc(s["nmr"], 1)
                    if g >= 1:
                        dve.wait_ge(s["omm"], gv)
                        x3_ = tiles(gv - 1)
                        dve.tensor_tensor(x3_, p_q[:].rearrange("p a (t n) -> p (a t) n", n=D),
                                          x3_, ALU.add).then_inc(s["x3r"], 1)
                    if 0 <= g < 8:
                        dve.wait_ge(s["ekr"], 2 * gv + 2)
                        dve.scalar_tensor_tensor(phk[:, 4:8], k_of, 0.0, ek[:], ALU.max, ALU.add
                                                 ).then_inc(s["phkr"], 1)
                steps(dve, step)

            @block.scalar
            def _(act):
                def step(g, gv):
                    r = g % 2
                    if g >= 1:
                        act.wait_ge(s["mqr"], gv)
                        wait(act, s["phqr"], gv - 1)
                        act.activation(rq[:], q_of, ACT.Relu, bias=k.bq[:]
                                       ).then_inc(s["rqr"], 1)
                        act.activation(phq[:], phq[:], ACT.Exp).then_inc(s["eqr"], 1)
                        act.wait_ge(s["kvpmm"], gv)
                        wait(act, s["omm"], gv - 1)
                        act.activation(kvp[:], p_c[:, 0:D], ACT.Copy).then_inc(s["kvpr"], 1)

                    def v_and_exp(h):
                        act.wait_ge(s["mkr"], 2 * gv + h + 1)
                        if h == 0:
                            wait(act, s["vtk"], gv)
                        act.activation(v[:, 4 * h:4 * h + 4], v_of, ACT.Copy)
                        act.activation(ek[:], ek[:], ACT.Exp).then_inc(s["ekr"], 1)
                    if 0 <= g < 8:
                        v_and_exp(0)
                    if -1 <= g < 7:
                        act.wait_ge(s["xpose"], gv + 2)
                        act.activation(xt[(g + 1) % 2][:], p_t[:].rearrange("p a n -> p (a n)"),
                                       ACT.Copy).then_inc(s["xtr"], 1)
                    if 0 <= g < 8:
                        v_and_exp(1)
                    if g < 6:
                        act.wait_ge(s["nmr"], gv + 3)
                        wait(act, s["xpose"], gv + 2)
                        x2 = tiles(gv + 2)
                        for q in range(GT):
                            last = act.activation(xh[:, q], x2[:, q], ACT.Identity,
                                                  bias=nm[r][:, q:q + 1],
                                                  scale=rs[r][:, q:q + 1])
                        last.then_inc(s["xhr"], 1)
                steps(act, step)

            @block.tensor
            def _(pe):
                def step(g, gv):
                    r = g % 2

                    def kv(h):
                        for q in range(4):
                            o = p_kv[:, q // 2, (q % 2) * 2 * D:(q % 2 + 1) * 2 * D]
                            i = 4 * h + q
                            pe.matmul(o, xt[r][:, i * P:(i + 1) * P], k.wkv[:], start=True,
                                      stop=False)
                            last = pe.matmul(o, k.onesr[:], k.bkvp[:, 0:2 * D], start=False,
                                             stop=True)
                        last.then_inc(s["kvmm"], 1)
                    if 0 <= g < 8:
                        pe.wait_ge(s["xtr"], gv + 1)
                        wait(pe, s["phkr"], 2 * gv)
                        kv(0)
                    if g >= 1:
                        pe.wait_ge(s["kvtr"], gv)
                        wait(pe, s["kvpr"], gv - 1)
                        pe.matmul(p_c[:, 0:D], kvt[:], k.wp[:], start=True, stop=True
                                  ).then_inc(s["kvpmm"], 1)
                    if -1 <= g < 7:
                        pe.wait_ge(s["xhr"], gv + 2)
                        wait(pe, s["xtr"], gv + 1)
                        for q in range(GT):
                            last = pe.transpose(p_t[:, q // 4, (q % 4) * P:(q % 4 + 1) * P],
                                                xh[:, q], k.ident[:])
                        last.then_inc(s["xpose"], 1)
                    if g >= 1:
                        pe.wait_ge(s["kvpr"], gv)
                        pe.wait_ge(s["rqr"], gv)
                        pe.wait_ge(s["phqr"], gv)
                        for q in range(GT):
                            o = p_q[:, q // 4, (q % 4) * D:(q % 4 + 1) * D]
                            pe.matmul(o, phq[:, q * P:(q + 1) * P], kvp[:], start=True,
                                      stop=False)
                            last = pe.matmul(o, k.onesr[:], k.bkvp[:, 2 * D:3 * D], start=False,
                                             stop=True)
                        last.then_inc(s["omm"], 1)
                    if 0 <= g < 8:
                        pe.wait_ge(s["phkr"], 2 * gv + 1)
                        kv(1)
                        wait(pe, s["x3r"], gv)
                        for h in range(2):
                            last = pe.matmul(p_q[:, h], k.wq[:], xt[r][:, h * 512:(h + 1) * 512],
                                             start=True, stop=True)
                        last.then_inc(s["qmm"], 1)
                        pe.wait_ge(s["phkr"], 2 * gv + 2)
                        wait(pe, s["kvtr"], gv)
                        for q in range(GT):
                            last = pe.matmul(p_b[:, 0:D], v[:, q], phk[:, q], start=q == 0,
                                             stop=q == GT - 1)
                        last.then_inc(s["vtk"], 1)
                steps(pe, step)


def combine(nc, k, sb, resid, ys, out):
    with phase(nc) as sem, ExitStack() as ctx:
        rs = [sb(f"c_rs{r}", [P, GT, D], ctx=ctx) for r in range(GROUPS)]
        yt = [sb(f"c_yt{r}", [P, GT, 2 * D], ctx=ctx) for r in range(4)]
        in_ready = [sem(f"c_in{r}") for r in range(GROUPS)]
        half, ysum, stored = sem("c_half"), sem("c_ysum"), sem("c_stored")
        with nc.Block() as block:
            @block.sync
            def _(sp):
                for g in range(GROUPS):
                    sp.dma_start(rs[g][:], resid[:, g]).then_inc(in_ready[g], 16)
                    if g >= 4:
                        sp.wait_ge(ysum, g - 3)
                    sp.dma_start(yt[g % 4][:], ys[:, g]).then_inc(in_ready[g], 16)
                sp.wait_ge(stored, 16 * GROUPS)

            @block.vector
            def _(dve):
                for g in range(GROUPS):
                    dve.wait_ge(in_ready[g], 32)
                    dve.tensor_tensor(rs[g][:], rs[g][:], yt[g % 4][:, :, 0:D], ALU.add
                                      ).then_inc(half, 1)
                    dve.wait_ge(half, g + 1)
                    dve.tensor_tensor(rs[g][:], rs[g][:], yt[g % 4][:, :, D:2 * D], ALU.add
                                      ).then_inc(ysum, 1)

            @block.scalar
            def _(act):
                for g in range(GROUPS):
                    act.wait_ge(ysum, g + 1)
                    act.dma_start(out[:, g], rs[g][:]).then_inc(stored, 16)


INS = ["attn_x", "attn_Wq", "attn_bq", "attn_Wk", "attn_bk", "attn_Wv", "attn_bv", "attn_Wp",
       "attn_bp", "ffn_gate_w", "ffn_gate_b", "ffn_w1", "ffn_b1", "ffn_w3", "ffn_b3", "ffn_w2",
       "ffn_b2", "ffn_sw1", "ffn_sb1", "ffn_sw3", "ffn_sb3", "ffn_sw2", "ffn_sb2"]


def kernel(**inputs):
    import numpy as np
    import concourse.bacc as bacc
    from concourse.bass_utils import run_bass_kernel_spmd

    nc = bacc.Bacc("TRN2", target_bir_lowering=False, num_devices=1)
    arrays, args = {}, []
    for name in INS:
        a = np.ascontiguousarray(inputs["L0_" + name])
        arrays["in_" + name] = a
        args.append(nc.dram_tensor("in_" + name, a.shape, mybir.dt.from_np(a.dtype),
                                   kind="ExternalInput").ap())
    shape = [GROUPS, GT * P, D]
    args.append(nc.dram_tensor("out", shape, F32, kind="ExternalOutput").ap())
    xs = [nc.dram_tensor(f"xs{n}", [SLOT_TILES * P, ROW], F32).ap() for n in range(2)]
    ys = nc.dram_tensor("ys", [TOKENS * K_TOP + PADS * P, D], F32).ap()
    resid = nc.dram_tensor("resid", shape, F32).ap()
    x3 = nc.dram_tensor("x3", shape, F32).ap()
    build(nc, *args, xs, ys, resid, x3)
    r = run_bass_kernel_spmd(nc, [arrays], core_ids=[0])
    return r.results[0]["out"]
```

```python
from contextlib import ExitStack, contextmanager

import concourse.bass as bass
from concourse import mybir

F32 = mybir.dt.float32
F32R = mybir.dt.float32r
BF16 = mybir.dt.bfloat16
I32 = mybir.dt.int32
U32 = mybir.dt.uint32
ACT = mybir.ActivationFunctionType
ALU = mybir.AluOpType
AX = mybir.AxisListType.X
ds = bass.ds

P = 128
D = 128
HEAD_DIM = 8
E = 16
INTER = 176
UP = 2 * INTER
SH = 352
GROUPS = 8
GT = 8
TILES = GROUPS * GT
TOKENS = TILES * P
K_TOP = 2
SLOT_TILES = TOKENS * K_TOP // P + E
PAIRS = SLOT_TILES // 2
ROW = D + 2
CHUNK = 4
CHUNKS = TILES // CHUNK
FEAT = [(0, 128), (128, 128), (256, 96)]
A0 = 96
A1 = INTER - A0
EPS = 1e-5
RING = 8
SENT_EARLY = GT // 2
REGION = TOKENS + P
RTILES = REGION // P
PADS = 2 * E
XS_ROWS = E * REGION + PADS * P
MAGIC = float(3 << 22)


@contextmanager
def phase(nc):
    sems = []

    def sem(name):
        sems.append(nc.alloc_semaphore(name=name))
        return sems[-1]
    yield sem
    nc.clear_and_free_semaphores(sems)
    nc.all_engine_barrier()


def wait(eng, sem, value):
    if not (isinstance(value, int) and value <= 0):
        eng.wait_ge(sem, value)


def build(nc, x, wq, bq, wk, bk, wv, bv, wp, bp, gate_w, gate_b, w1, b1, w3, b3, w2, b2,
          sw1, sb1, sw3, sb3, sw2, sb2, out, xs_dram, ys_dram, resid, x3):
    top = ExitStack()
    with top:
        def sb(name, shape, dt=F32, ctx=top):
            return ctx.enter_context(nc.sbuf_tensor(name, shape, dt))

        def ps(name, shape, ctx, dt=F32):
            return ctx.enter_context(nc.psum_tensor(name, shape, dt))

        def sem(name):
            return top.enter_context(nc.semaphore(name))

        class W:
            pass

        k = W()
        k.w13h, k.w13l = sb("w13h", [P, E * UP], F32R), sb("w13l", [P, E * UP], F32R)
        k.w2hl = sb("w2hl", [A0 + 1, 2, E, 2 * D], F32R)
        k.b13 = sb("b13", [33, E * UP], F32R)
        k.sw13h, k.sw13l = sb("sw13h", [P, 2 * SH], F32R), sb("sw13l", [P, 2 * SH], F32R)
        k.sw2hl = sb("sw2hl", [P, 3, 2 * D], F32R)
        k.sb13 = sb("sb13", [P, 2, 3])
        k.wq, k.wkv, k.wp = sb("wq_s", [P, D]), sb("wkv_s", [P, 2 * D]), sb("wp_s", [P, D])
        k.bkvp = sb("bkvp", [33, 6 * D], F32R)
        k.bq = sb("bq_s", [P, 1])
        k.gw, k.gb = sb("gw_s", [P, E]), sb("gb_s", [P, E])
        k.ident = sb("ident", [P, P])
        k.onesr = sb("onesr", [33, P], F32R)
        k.tri, k.onesb = sb("tri", [P, P], BF16), sb("onesb", [P, P], BF16)
        k.blockdiag = sb("blockdiag", [P, P])
        k.iota_e, k.ones_e = sb("iota_e", [P, E]), sb("ones_e", [P, E])
        k.iota_j = sb("iota_j", [P, 2])
        k.region = sb("region", [P, E])
        k.nhalf = sb("nhalf", [P, GT])
        k.tile_expert = sb("tile_expert", [1, SLOT_TILES], I32)
        k.tile_at = sb("tile_at", [1, SLOT_TILES], I32)
        k.pad_at = sb("pad_at", [1, E], I32)

        k.zero, k.pad_tail = sb("zero", [P, D]), sb("pad_tail", [P, PADS, 2])
        k.first_in = [sem("first_in0"), sem("first_in1")]
        k.gate_in, k.smalls_in, k.padded = sem("gate_in"), sem("smalls_in"), sem("padded")
        x_v = x.rearrange("b (p i) d -> p b i d", i=GT)
        out_v = out.rearrange("b (p i) d -> p b i d", i=GT)
        resid_v = resid.rearrange("b (p i) d -> p b i d", i=GT)
        x3_v = x3.rearrange("b (p i) d -> p b i d", i=GT)
        ys_v = ys_dram.rearrange("(r c) d -> r (c d)", c=K_TOP)[0:TOKENS, :]
        ys_v = ys_v.rearrange("(b p i) d -> p b i d", i=GT, p=P)
        for n, src in enumerate((x_v, x3_v)):
            with ExitStack() as ctx:
                xrow = sb(f"xrow{n}", [P, TILES, ROW], ctx=ctx)
                r_ = W()
                r_.onehot = [sb(f"onehot{n}{q}", [P, TILES, E], BF16, ctx) for q in range(K_TOP)]
                r_.mask = sb(f"mask{n}", [P, TILES, E], BF16, ctx)
                r_.rec, r_.second = (sb(f"{m}{n}", [P, TILES], ctx=ctx)
                                     for m in ("rec", "second"))
                r_.slot = [sb(f"slot{n}{q}", [P, TILES], I32, ctx) for q in range(K_TOP)]
                r_.base = [sb(f"base{n}{q}", [P, E], ctx=ctx) for q in range(2)]
                with ExitStack() as staging:
                    if n == 0:
                        stage_weights(k, sb, staging, bk, bv, bp, sw1, sw3, sw2, sb2)
                        setup(nc, k, xs_dram, src, xrow, wq, bq, wk, wv, wp, gate_w, gate_b,
                              sb1, sb3)
                    norm_and_gate(nc, k, sb, ps, n, src, xrow, r_, xs_dram,
                                  (w1, b1, w3, b3, w2, b2) if n == 0 else None)
                share(nc, k, sb, ps, n, src, xrow, r_, xs_dram, resid_v)
            if n == 0:
                experts(nc, k, sb, ps, n, xs_dram, ys_dram)
                attention(nc, k, sb, ps, resid_v, ys_v, x3_v)
        rs = sb("rs", [P, GROUPS, GT, D])
        experts(nc, k, sb, ps, 1, xs_dram, ys_dram, (rs, resid_v))
        combine(nc, k, sb, rs, ys_v, out_v)


def load_group(eng, src, xrow, g, done):
    eng.dma_start(xrow[:, ds(g * GT, GT), 0:D],
                  src[:, ds(g, 1)].rearrange("p b i d -> p (b i) d")).then_inc(done, 16)


def stage_weights(k, sb, ctx, bk, bv, bp, sw1, sw3, sw2, sb2):
    raws13 = sb("raws13", [P, 2 * SH], ctx=ctx)
    raws2 = sb("raws2", [P, 3, D], ctx=ctx)
    k.rawa = sb("rawa", [33, 6 * D], ctx=ctx)
    k.halves = [
        (raws13[:], k.sw13h[:], k.sw13l[:]),
        (raws2[:, 0:2], k.sw2hl[:, 0:2, 0:D], k.sw2hl[:, 0:2, D:2 * D]),
        (raws2[0:97, 2], k.sw2hl[0:97, 2, 0:D], k.sw2hl[0:97, 2, D:2 * D]),
    ]
    k.staged = [
        (raws13[:, 0:SH], sw1), (raws13[:, SH:2 * SH], sw3),
        (raws2[:, 0:2], sw2[0:256, :].rearrange("(c p) d -> p c d", p=P)),
        (raws2[0:96, 2], sw2[256:SH, :]),
        (raws2[96:97, 2], sb2.rearrange("(a n) -> a n", a=1)),
    ]
    for r in (0, 32):
        k.staged += [(k.rawa[r:r + 1, m * D:(m + 1) * D], b.rearrange("(a n) -> a n", a=1))
                     for m, b in enumerate((bk, bv))]
        k.staged.append((k.rawa[r:r + 1, 2 * D:].rearrange("a (t n) -> a t n", t=4),
                         bp.rearrange("(a t n) -> a t n", a=1, t=1).to_broadcast([1, 4, D])))


def setup(nc, k, xs_dram, src, xrow, wq, bq, wk, wv, wp, gate_w, gate_b, sb1, sb3):
    with phase(nc) as sem:
        built, base = sem("su_built"), sem("su_base")
        smalls = [(k.wq[:], wq), (k.wkv[:, 0:D], wk), (k.wkv[:, D:2 * D], wv), (k.wp[:], wp),
                  (k.bq[:], bq.rearrange("(p a) -> p a", a=1))]
        for m, b in enumerate((sb1, sb3)):
            smalls += [(k.sb13[0:w, m, f:f + 1], b[o:o + w].rearrange("(p a) -> p a", a=1))
                       for f, (o, w) in enumerate(FEAT)]
        k.smalls = len(smalls)
        with nc.Block() as block:
            @block.gpsimd
            def _(pool):
                pool.memset(k.zero[:], 0.0)
                pool.memset(k.pad_tail[:], 0.0).then_inc(base, 1)
                pool.wait_ge(base, 1)
                pool.iota(k.pad_tail[:, :, 0:1].bitcast(I32).rearrange("p j a -> p (j a)"),
                          pattern=[[P, PADS]], base=TOKENS * K_TOP, channel_multiplier=1
                          ).then_inc(built, 1)
                pool.memset(k.ident[:], 0.0)
                pool.memset(k.tri[:], 1.0)
                pool.memset(k.blockdiag[:], 1.0)
                pool.memset(k.onesb[:], 1.0)
                pool.memset(k.ones_e[:], 1.0)
                pool.memset(k.nhalf[:], -0.5).then_inc(base, 1)
                pool.wait_ge(base, 2)
                pool.affine_select(out=k.ident[:], in_=k.ident[:], compare_op=ALU.not_equal,
                                   fill=1.0, base=0, pattern=[[-1, P]], channel_multiplier=1)
                pool.affine_select(out=k.tri[:], in_=k.tri[:], compare_op=ALU.is_ge, fill=0.0,
                                   base=-1, pattern=[[1, P]], channel_multiplier=-1)
                heads = k.blockdiag[:].rearrange("p (a c) -> p a c", c=HEAD_DIM)
                pool.affine_select(out=heads, in_=heads, compare_op=ALU.is_ge, fill=0.0, base=0,
                                   pattern=[[-HEAD_DIM, D // HEAD_DIM], [0, HEAD_DIM]],
                                   channel_multiplier=1).then_inc(base, 1)
                pool.wait_ge(base, 3)
                pool.affine_select(out=heads, in_=heads, compare_op=ALU.is_ge, fill=0.0,
                                   base=HEAD_DIM - 1,
                                   pattern=[[HEAD_DIM, D // HEAD_DIM], [0, HEAD_DIM]],
                                   channel_multiplier=-1)
                pool.iota(k.iota_e[:], pattern=[[1, E]], base=0, channel_multiplier=0,
                          allow_small_or_imprecise_dtypes=True)
                pool.iota(k.iota_j[:], pattern=[[P, 2]], base=0, channel_multiplier=1,
                          allow_small_or_imprecise_dtypes=True)
                pool.iota(k.region[:], pattern=[[REGION, E]], base=0, channel_multiplier=0,
                          allow_small_or_imprecise_dtypes=True)

            @block.vector
            def _(dve):
                dve.memset(k.rawa[:], 0.0)
                dve.memset(k.onesr[:].bitcast(F32), 1.0)

            @block.scalar
            def _(act):
                for g in range(2):
                    load_group(act, src, xrow, g, k.first_in[g])
                act.dma_start(k.gw[:], gate_w).then_inc(k.gate_in, 16)
                act.dma_start(k.gb[:], gate_b.partition_broadcast(P)).then_inc(k.gate_in, 16)
                for dst, part in smalls:
                    act.dma_start(dst, part).then_inc(k.smalls_in, 16)

            @block.sync
            def _(sp):
                rows = xs_dram[E * REGION:, :].rearrange("(j p) c -> p j c", p=P)
                sp.wait_ge(built, 1)
                sp.dma_start(rows[:, :, 0:D], k.zero[:].unsqueeze(1).to_broadcast([P, PADS, D])
                             ).then_inc(k.padded, 16)
                sp.dma_start(rows[:, :, D:ROW], k.pad_tail[:]).then_inc(k.padded, 16)


def norm_and_gate(nc, k, sb, ps, n, src, xrow, r_, xs, weights):
    with phase(nc) as sem, ExitStack() as ctx:
        xh = [sb(f"a{n}_xh{r}", [P, GT, D], ctx=ctx) for r in range(2)]
        xt = [sb(f"a{n}_xt{r}", [P, GT * P], ctx=ctx) for r in range(2)]
        st = sb(f"a{n}_st", [P, GT, 6], ctx=ctx)
        mv, ve = sb(f"a{n}_mv", [P, GT, 2], ctx=ctx), sb(f"a{n}_ve", [P, GT], ctx=ctx)
        rs = [sb(f"a{n}_rs{r}", [P, GT], ctx=ctx) for r in range(2)]
        nm = [sb(f"a{n}_nm{r}", [P, GT], ctx=ctx) for r in range(2)]
        lgt, dev, ex = (sb(f"a{n}_{m}", [P, GT, E], ctx=ctx) for m in ("lgt", "dev", "ex"))
        m8, i8 = sb(f"a{n}_m8", [P, GT, 8], ctx=ctx), sb(f"a{n}_i8", [P, GT, 8], U32, ctx)
        idx = sb(f"a{n}_idx", [P, GT, 2], ctx=ctx)
        pt = [ps(f"a{n}_pt{r}", [P, GT * P], ctx) for r in range(2)]
        pl = [ps(f"a{n}_pl{r}", [P, 512], ctx) for r in range(2)]
        pc = [ps(f"a{n}_pc{r}", [P, 512], ctx) for r in range(2)]
        ssum = sb(f"a{n}_ssum", [P, GT], ctx=ctx)
        place = sb(f"a{n}_place", [P, GT, E], ctx=ctx)
        prod = [sb(f"a{n}_prod{q}", [P, GT, E], ctx=ctx) for q in range(K_TOP)]
        at = sb(f"a{n}_at", [P, K_TOP, GT], ctx=ctx)
        if weights:
            w1, b1, w3, b3, w2, b2 = weights
            raw13 = [sb(f"raw13{r}", [P, 2, UP], ctx=ctx) for r in range(2)]
            raw2 = [sb(f"raw2{r}", [A0 + 1, 2, 2, D], ctx=ctx) for r in range(2)]
            rawb = [sb(f"rawb{r}", [33, 2, UP], ctx=ctx) for r in range(2)]
        in_ready = k.first_in if n == 0 else [sem(f"a{n}_in{r}") for r in range(2)]
        kept = [sem(f"a{n}_kept{r}") for r in range(2)]
        w_in = [sem(f"a{n}_win{r}") for r in range(2)]
        names = ("stats", "aggr", "var", "rstd", "nmr", "passed", "xh", "xpose", "xt", "gate",
                 "lgr", "maxed", "found", "idxr", "onehots", "devr", "exr", "summed", "whi",
                 "blo", "wlo", "zeroed", "masked", "staged", "shi", "counted", "placed", "picked", "at",
                 "slots", "recd", "weighted", "payload", "sent")
        (stats, aggr, var, rstd, nmr, passed, xh_ready, xpose, xt_ready, gate, lg_ready, maxed,
         found, idx_ready, onehots, dev_ready, ex_ready, summed, whi, blo, wlo, zeroed, masked, staged, shi, counted, placed, picked, at_ready, slots, recd, weighted, payload,
         sent) = (
            sem(f"a{n}_{s}") for s in names)

        def steps(eng, step):
            for g in (-1, 0, 1):
                step(g, g)
            with eng.Fori(0, 2) as i:
                step(2, 2 * i + 2)
                step(3, 2 * i + 3)
            for g in (6, 7, 8, 9):
                step(g, g)

        def turn(s, g, r):
            return 16 * (s // 2 + 1) if isinstance(g, int) else 8 * (g - r) + 16

        def wslices(r, g):
            es = ds(2 * g, 2)
            w13h, w13l = (w[:, ds(2 * g * UP, 2 * UP)] for w in (k.w13h, k.w13l))
            out = [(raw13[r][:].rearrange("p e n -> p (e n)"), w13h, w13l)]
            for c, rows in ((0, A0 + 1), (1, A0)):
                out.append((raw2[r][0:rows, c], k.w2hl[0:rows, c, es, 0:D],
                            k.w2hl[0:rows, c, es, D:2 * D]))
            return out

        with nc.Block() as block:
            @block.sync
            def _(sp):
                def load_weights(s, g):
                    r, es = s % 2, ds(2 * g, 2)
                    wait(sp, blo, g - 1)
                    wait(sp, wlo, g - 1)
                    parts = [
                        (raw13[r][:, :, 0:INTER], w1[es].rearrange("e d n -> d e n")),
                        (raw13[r][:, :, INTER:UP], w3[es].rearrange("e d n -> d e n")),
                        (raw2[r][0:A0, 0], w2[es, 0:A0, :].rearrange("e k d -> k e d")),
                        (raw2[r][2 * A0 - INTER:A0, 1],
                         w2[es, A0:INTER, :].rearrange("e k d -> k e d")),
                        (raw2[r][A0:A0 + 1, 0], b2[es].rearrange("(a e) d -> a e d", a=1))]
                    for row in (0, 32):
                        parts += [
                            (rawb[r][row:row + 1, :, 0:INTER],
                             b1[es].rearrange("(a e) n -> a e n", a=1)),
                            (rawb[r][row:row + 1, :, INTER:UP],
                             b3[es].rearrange("(a e) n -> a e n", a=1))]
                    for dst, part in parts:
                        sp.dma_start(dst, part).then_inc(w_in[r], 16)

                def step(s, g):
                    if s < 0:
                        if weights:
                            sp.wait_ge(zeroed, 1)
                            load_weights(0, 0)
                            for dst, part in k.staged:
                                sp.dma_start(dst, part).then_inc(staged, 16)
                            load_weights(1, 1)
                    elif s < 8:
                        sp.wait_ge(xh_ready, g + 1)
                        sp.dma_start(xrow[:, ds(g * GT, GT), 0:D], xh[s % 2][:]
                                     ).then_inc(kept[s % 2], 16)
                        if weights and 1 <= s < 7:
                            load_weights(s + 1, g + 1)
                steps(sp, step)
                for r in range(2):
                    sp.wait_ge(kept[r], 16 * GROUPS // 2)

            @block.vector
            def _(dve):
                if weights:
                    for r in range(2):
                        dve.memset(rawb[r][:], 0.0)
                        last = dve.memset(raw2[r][0:32, 1], 0.0)
                    last.then_inc(zeroed, 1)
                dve.tensor_copy(r_.base[0][:], k.region[:])

                def step(s, g):
                    r = (s + 1) % 2
                    front, top2, place_ = s < 7, 1 <= s < 9, s >= 2
                    h1, h2 = ds((g - 1) * GT, GT), ds((g - 2) * GT, GT)
                    if front:
                        dve.wait_ge(in_ready[r], turn(s + 1, g if isinstance(g, int) else g + 1,
                                                      r))
                        dve.sem_inc(passed, 1)
                        xg = xrow[:, ds((g + 1) * GT, GT), 0:D]
                        for t in range(GT):
                            last = dve.bn_stats(st[:, t], xg[:, t])
                        last.then_inc(stats, 1)
                    if place_:
                        base = r_.base[s % 2]
                        dve.wait_ge(counted, g - 1)
                        dve.tensor_tensor(
                            place[:], pc[s % 2][:, 0:GT * E].rearrange("p (t e) -> p t e", e=E),
                            base[:].unsqueeze(1).to_broadcast([P, GT, E]), ALU.add
                            ).then_inc(placed, 1)
                        dve.tensor_tensor(r_.base[(s + 1) % 2][:], base[:],
                                          pc[s % 2][:, GT * E:(GT + 1) * E], ALU.add)
                        dve.wait_ge(summed, g - 1)
                        dve.reciprocal(r_.rec[:, h2], ssum[:]).then_inc(recd, 1)
                    if front:
                        dve.wait_ge(stats, g + 2)
                        dve.sem_inc(passed, 1)
                        for t in range(GT):
                            last = dve.bn_aggr(mv[:, t], st[:, t])
                        last.then_inc(aggr, 1)
                    if place_:
                        dve.wait_ge(placed, g - 1)
                        for q in range(K_TOP):
                            last = dve.tensor_tensor(prod[q][:], r_.onehot[q][:, h2], place[:],
                                                     ALU.mult)
                        last.then_inc(picked, 1)
                    if front:
                        dve.wait_ge(aggr, g + 2)
                        dve.tensor_scalar(ve[:], mv[:, :, 1], EPS, None, ALU.add
                                          ).then_inc(var, 1)
                    if top2:
                        if s == 1:
                            dve.wait_ge(k.gate_in, 32)
                        dve.wait_ge(gate, g)
                        dve.tensor_tensor(
                            lgt[:], pl[(s - 1) % 2][:, 0:GT * E].rearrange("p (t e) -> p t e",
                                                                           e=E),
                            k.gb[:].unsqueeze(1).to_broadcast([P, GT, E]), ALU.add
                            ).then_inc(lg_ready, 1)
                    if place_:
                        dve.wait_ge(picked, g - 1)
                        for q in range(K_TOP):
                            last = dve.reduce_sum(at[:, q], prod[q][:], AX)
                        last.then_inc(at_ready, 1)
                        dve.wait_ge(recd, g - 1)
                        dve.tensor_scalar(xrow[:, h2, D + 1:D + 2], r_.rec[:, h2].unsqueeze(2),
                                          0.5, None, ALU.mult).then_inc(weighted, 1)
                    if top2:
                        dve.wait_ge(lg_ready, g)
                        dve.sem_inc(passed, 1)
                        for t in range(GT):
                            last = dve.max(m8[:, t], lgt[:, t])
                        last.then_inc(maxed, 1)
                    if place_:
                        dve.wait_ge(at_ready, g - 1)
                        for q in range(K_TOP):
                            last = dve.tensor_copy(r_.slot[q][:, h2], at[:, q])
                        last.then_inc(slots, 1)
                    if top2:
                        dve.wait_ge(maxed, g)
                        dve.sem_inc(passed, 1)
                        for t in range(GT):
                            last = dve.max_index(i8[:, t], m8[:, t], lgt[:, t])
                        last.then_inc(found, 1)
                        wait(dve, ex_ready, g - 1)
                        dve.tensor_tensor(dev[:], lgt[:],
                                          m8[:, :, 0:1].to_broadcast([P, GT, E]), ALU.subtract
                                          ).then_inc(dev_ready, 1)
                        dve.tensor_tensor(r_.second[:, h1], m8[:, :, 1], m8[:, :, 0],
                                          ALU.subtract)
                        dve.wait_ge(found, g)
                        dve.tensor_copy(idx[:], i8[:, :, 0:2]).then_inc(idx_ready, 1)
                    if front:
                        dve.wait_ge(rstd, g + 2)
                        dve.scalar_tensor_tensor(nm[r][:], mv[:, :, 0], -1.0, rs[r][:],
                                                 ALU.mult, ALU.mult).then_inc(nmr, 1)
                    if top2:
                        iota = k.iota_e[:].unsqueeze(1).to_broadcast([P, GT, E])
                        dve.wait_ge(idx_ready, g)
                        for q, oh in enumerate(r_.onehot):
                            last = dve.tensor_tensor(
                                oh[:, h1], iota, idx[:, :, q:q + 1].to_broadcast([P, GT, E]),
                                ALU.is_equal)
                        last.then_inc(onehots, 1)
                    if weights and top2:
                        dve.wait_ge(whi, g)
                        b = k.b13[32:33, ds((g - 1) * 2 * UP, 2 * UP)]
                        dve.tensor_tensor(b, rawb[(s - 1) % 2][32:33].rearrange(
                            "p e n -> p (e n)"), b.bitcast(F32), ALU.subtract).then_inc(blo, 1)
                    if top2:
                        dve.wait_ge(onehots, g)
                        dve.tensor_tensor(r_.mask[:, h1], r_.onehot[0][:, h1],
                                          r_.onehot[1][:, h1], ALU.add).then_inc(masked, 1)
                        dve.wait_ge(ex_ready, g)
                        dve.reduce_sum(ssum[:], ex[:], AX).then_inc(summed, 1)
                    if weights and s == 9:
                        for m, (raw, h, l) in enumerate(k.halves):
                            dve.wait_ge(shi, m + 1)
                            dve.tensor_tensor(l, raw, h.bitcast(F32), ALU.subtract)
                        dve.wait_ge(shi, len(k.halves) + 1)
                        dve.tensor_tensor(k.bkvp[32:33], k.rawa[32:33],
                                          k.bkvp[32:33].bitcast(F32), ALU.subtract)
                steps(dve, step)

            @block.gpsimd
            def _(pool):
                pool.iota(xrow[:, :, D:D + 1].bitcast(I32).rearrange("p (b i) a -> p b (i a)",
                                                                     i=GT),
                          pattern=[[2 * GT * P, GROUPS], [2, GT]], base=0,
                          channel_multiplier=2 * GT).then_inc(payload, 1)
                pool.wait_ge(payload, 1)
                for g in range(-1, 10):
                    if g < 7:
                        pool.wait_ge(var, g + 2)
                        wait(pool, xh_ready, g)
                        pool.tensor_tensor(rs[(g + 1) % 2][:], ve[:], k.nhalf[:], ALU.pow
                                           ).then_inc(rstd, 1)
                    if weights and 1 <= g < 9:
                        pool.wait_ge(whi, g)
                        for raw, h, l in wslices((g - 1) % 2, g - 1):
                            last = pool.tensor_tensor(l, raw, h.bitcast(F32), ALU.subtract)
                        last.then_inc(wlo, 1)
                    if 2 <= g < 9:
                        pool.wait_ge(slots, g - 1)
                        pool.wait_ge(weighted, g - 1)
                        pool.wait_ge(kept[g % 2], 16 * (g // 2))
                        for q in range((g - 2) * GT, (g - 2) * GT + SENT_EARLY):
                            pool.indirect_dma_start(
                                xs, bass.IndirectOffsetOnAxis(r_.slot[0][:, q:q + 1], 0),
                                xrow[:, q, :], None).then_inc(sent, 16)
                pool.wait_ge(sent, 16 * SENT_EARLY * (GROUPS - 1))

            @block.scalar
            def _(act):
                if n == 1:
                    for g in range(2):
                        load_group(act, src, xrow, g, in_ready[g])

                def step(s, g):
                    if 0 <= s < 6:
                        load_group(act, src, xrow, g + 2, in_ready[s % 2])
                    if 0 <= s < 8:
                        act.wait_ge(xpose, g + 1)
                        wait(act, gate, g - 1)
                        act.activation(xt[s % 2][:], pt[s % 2][:], ACT.Copy).then_inc(xt_ready, 1)
                    if 1 <= s < 9:
                        act.wait_ge(dev_ready, g)
                        wait(act, summed, g - 1)
                        act.activation(ex[:], dev[:], ACT.Exp).then_inc(ex_ready, 1)
                    if s < 7:
                        r = (s + 1) % 2
                        act.wait_ge(nmr, g + 2)
                        wait(act, xpose, g)
                        if s >= 1:
                            act.wait_ge(kept[r], turn(s + 1, g if isinstance(g, int) else g + 1,
                                                      r) - 16)
                        act.sem_inc(passed, 1)
                        xg = xrow[:, ds((g + 1) * GT, GT), 0:D]
                        for t in range(GT):
                            last = act.activation(xh[r][:, t], xg[:, t], ACT.Identity,
                                                  bias=nm[r][:, t:t + 1], scale=rs[r][:, t:t + 1])
                        last.then_inc(xh_ready, 1)
                    if weights and 0 <= s < 8:
                        r = s % 2
                        act.wait_ge(w_in[r], 9 * turn(s, g, r))
                        act.sem_inc(passed, 1)
                        for raw, h, _l in wslices(r, g):
                            act.activation(h, raw, ACT.Copy)
                        act.activation(k.b13[:, ds(2 * g * UP, 2 * UP)],
                                       rawb[r][:].rearrange("p e n -> p (e n)"), ACT.Copy
                                       ).then_inc(whi, 1)
                    if weights and s == 9:
                        act.wait_ge(staged, 16 * len(k.staged))
                        for raw, h, _l in k.halves:
                            act.activation(h, raw, ACT.Copy).then_inc(shi, 1)
                        act.activation(k.bkvp[:], k.rawa[:], ACT.Copy).then_inc(shi, 1)
                        act.wait_ge(k.smalls_in, 16 * k.smalls)
                steps(act, step)

            @block.tensor
            def _(pe):
                def step(s, g):
                    if 0 <= s < 8:
                        r = s % 2
                        if s == 0:
                            pe.wait_ge(k.gate_in, 32)
                        pe.wait_ge(xt_ready, g + 1)
                        wait(pe, lg_ready, g - 1)
                        for t in range(GT):
                            last = pe.matmul(pl[r][:, t * E:(t + 1) * E],
                                             xt[r][:, t * P:(t + 1) * P], k.gw[:], start=True,
                                             stop=True)
                        last.then_inc(gate, 1)
                    if 1 <= s < 9:
                        r = (s - 1) % 2
                        pe.wait_ge(masked, g)
                        m = r_.mask[:, ds((g - 1) * GT, GT)].rearrange("p t e -> p (t e)")
                        pe.matmul(pc[r][:, 0:GT * E], k.tri[:], m, start=True, stop=False,
                                  skip_group_check=True)
                        for v in range(1, GT + 1):
                            last = pe.matmul(pc[r][:, v * E:(GT + 1) * E], k.onesb[:],
                                             m[:, 0:(GT + 1 - v) * E], start=False, stop=v == GT,
                                             skip_group_check=True)
                        last.then_inc(counted, 1)
                    if s < 7:
                        r = (s + 1) % 2
                        pe.wait_ge(xh_ready, g + 2)
                        wait(pe, xt_ready, g)
                        for t in range(GT):
                            last = pe.transpose(pt[r][:, t * P:(t + 1) * P], xh[r][:, t],
                                                k.ident[:])
                        last.then_inc(xpose, 1)
                steps(pe, step)


def share(nc, k, sb, ps, n, src, xrow, r_, xs, resid):
    with phase(nc) as sem, ExitStack() as ctx:
        def t(name, shape, dt=F32):
            return sb(f"r{n}_{name}", shape, dt, ctx)

        wtop, wsec = (t(s, [P, TILES]) for s in ("wtop", "wsec"))
        need, ends, starts = (t(s, [P, E]) for s in ("need", "ends", "starts"))
        past, passed_ = t("past", [P, 2, E]), t("passed", [P, 2, E])
        which, at = t("which", [P, 2]), t("at", [P, 2])
        xs_in = [t(f"xs{r}", [P, CHUNK, D]) for r in range(2)]
        rx = [t(f"rx{r}", [P, CHUNK, D]) for r in range(2)]
        ro = [t(f"ro{r}", [P, CHUNK, D]) for r in range(2)]
        xth = [t(f"xth{r}", [P, 512], F32R) for r in range(2)]
        xtl = [t(f"xtl{r}", [P, 512], F32R) for r in range(2)]
        sil = [t(f"sil{r}", [P, 512]) for r in range(2)]
        act_f = [t(f"actf{r}", [P, 512]) for r in range(2)]
        ah, al = (t(s, [P, 3, 512], F32R) for s in ("ah", "al"))
        p_x = ps(f"r{n}_px", [P, 512], ctx)
        p_hg = [ps(f"r{n}_phg{r}", [P, 512], ctx) for r in range(3)]
        p_z = [ps(f"r{n}_pz{r}", [P, 2, 512], ctx) for r in range(2)]
        p_tab = p_z[1]

        names = ("chain", "w_ready", "payload", "sent0", "sent1", "exp2", "tab_in", "tab_mm", "tab_done",
                 "padded")
        (chain, w_ready, payload, sent0, sent1, exp2, tab_in, tab_mm, tab_done, padded) = (
            sem(f"r{n}_{s}") for s in names)
        names = ("xpose", "hi", "lo", "up_h", "up", "silu", "aa", "ahi", "alo", "down", "outr", "outh")
        (xpose, hi, lo, up_h, up, silu, aa, ahi, alo, down, outr, outh) = (
            sem(f"s{n}_{s}") for s in names)
        in_ready = [sem(f"s{n}_in{r}") for r in range(2)]
        rx_ready = [sem(f"s{n}_rx{r}") for r in range(2)]
        stored = [sem(f"s{n}_st{r}") for r in range(2)]

        def steps(eng, step, first=-1, after=1):
            for c in range(first, 2):
                step(c, c)
            with eng.Fori(0, 6) as i:
                step(2, 2 * i + 2)
                step(3, 2 * i + 3)
            for c in range(14, CHUNKS + after):
                step(c, c)

        def turn(c, cv, r):
            return 16 * (c // 2 + 1) if isinstance(cv, int) else 8 * (cv - r) + 16

        def chunk_of(ap, c, cv):
            b = cv // 2 if isinstance(cv, int) else None
            h = c % 2
            if b is None:
                b = (cv - h) // 2
            return ap[:, ds(b, 1), h * CHUNK:(h + 1) * CHUNK].rearrange("p b i d -> p (b i) d")

        with nc.Block() as block:
            @block.sync
            def _(sp):
                def load_x(c, cv):
                    sp.dma_start(xs_in[c % 2][:], xrow[:, ds(cv * CHUNK, CHUNK), 0:D]
                                 ).then_inc(in_ready[c % 2], 16)

                def step(c, cv):
                    r = c % 2
                    if c < CHUNKS - 1:
                        wait(sp, xpose, cv)
                        load_x(c + 1, cv + 1)
                    if c < CHUNKS:
                        wait(sp, outr, cv - 1)
                        sp.dma_start(rx[r][:], chunk_of(src, c, cv)).then_inc(rx_ready[r], 16)
                    if c >= 2:
                        wait(sp, outr, cv - 1)
                        sp.dma_start(chunk_of(resid, c, cv - 2), ro[r][:]
                                     ).then_inc(stored[r], 16)
                load_x(0, 0)
                for c in (0, 1):
                    step(c, c)
                sp.wait_ge(k.padded, 32)
                sp.wait_ge(tab_done, 1)
                _, at_ = nc.values_load_multi_w_load_instructions(
                    k.pad_at[0:1, :], engines=[mybir.EngineType.SP], min_val=0,
                    max_val=(E - 1) * REGION + TOKENS,
                    skip_runtime_bounds_check_because="a region's start plus at most its tokens")
                for e in range(E):
                    pad = E * REGION + (E + e) * P
                    sp.dma_start(xs[ds(at_[e], P), :], xs[pad:pad + P, :]).then_inc(padded, 16)
                with sp.Fori(0, 6) as i:
                    step(2, 2 * i + 2)
                    step(3, 2 * i + 3)
                for c in range(14, CHUNKS + 2):
                    step(c, c)
                sp.wait_ge(padded, 16 * E)
                for r in range(2):
                    sp.wait_ge(stored[r], 16 * CHUNKS // 2)

            @block.gpsimd
            def _(pool):
                for g in range(GROUPS):
                    early = SENT_EARLY if g < GROUPS - 1 else 0
                    for q in range(g * GT + early, (g + 1) * GT):
                        pool.indirect_dma_start(xs,
                                                bass.IndirectOffsetOnAxis(
                                                    r_.slot[0][:, q:q + 1], 0),
                                                xrow[:, q, :], None).then_inc(sent0, 16)
                pool.wait_ge(sent0, 16 * (TILES - SENT_EARLY * (GROUPS - 1)))
                pool.iota(xrow[:, :, D:D + 1].bitcast(I32).rearrange("p (b i) a -> p b (i a)",
                                                                     i=GT),
                          pattern=[[2 * GT * P, GROUPS], [2, GT]], base=1,
                          channel_multiplier=2 * GT).then_inc(payload, 1)
                pool.wait_ge(w_ready, 1)
                pool.tensor_copy(xrow[:, :, D + 1:D + 2], wsec[:].unsqueeze(2)
                                 ).then_inc(payload, 1)
                pool.wait_ge(payload, 2)
                for q in range(TILES):
                    pool.indirect_dma_start(xs,
                                            bass.IndirectOffsetOnAxis(r_.slot[1][:, q:q + 1], 0),
                                            xrow[:, q, :], None).then_inc(sent1, 16)
                pool.wait_ge(sent1, 16 * TILES)

            @block.vector
            def _(dve):
                links = [0]

                def link(ins):
                    links[0] += 1
                    ins.then_inc(chain, 1)
                    dve.wait_ge(chain, links[0])

                dve.wait_ge(exp2, 1)
                dve.scalar_tensor_tensor(wsec[:], r_.rec[:], 0.5, wtop[:], ALU.mult, ALU.mult
                                         ).then_inc(w_ready, 1)
                dve.memset(ah[96:97, 2].bitcast(F32), 1.0)
                dve.memset(al[96:97, 2].bitcast(F32), 0.0)
                full = r_.base[GROUPS % 2]
                dve.tensor_copy(k.pad_at[:], full[0:1, :])
                link(dve.tensor_tensor(need[:], full[:], k.region[:], ALU.subtract))
                link(dve.tensor_scalar(need[:], need[:], 63.5, 1.0 / P, ALU.add, ALU.mult))
                link(dve.tensor_scalar(need[:], need[:], MAGIC, MAGIC, ALU.add, ALU.subtract))
                link(dve.tensor_tensor_scan(ends[:], k.ones_e[:], need[:], 0.0, ALU.mult,
                                            ALU.add))
                for c in range(2):
                    last = dve.tensor_scalar(past[:, c], ends[:], k.iota_j[:, c:c + 1], None,
                                             ALU.is_le)
                link(last)
                link(dve.tensor_tensor(passed_[:], past[:],
                                       need[:].unsqueeze(1).to_broadcast([P, 2, E]), ALU.mult))
                dve.reduce_sum(which[:], past[:], AX)
                link(dve.reduce_sum(at[:], passed_[:], AX))
                link(dve.tensor_tensor(at[:], k.iota_j[:], at[:], ALU.subtract))
                dve.scalar_tensor_tensor(at[:], which[:], float(RTILES), at[:], ALU.mult, ALU.add
                                         ).then_inc(tab_in, 1)
                dve.wait_ge(tab_mm, 1)
                dve.tensor_scalar(k.tile_expert[:], p_tab[0:1, 0, 0:SLOT_TILES], float(E - 1),
                                  None, ALU.min)
                dve.tensor_copy(k.tile_at[:], p_tab[0:1, 1, 0:SLOT_TILES]).then_inc(tab_done, 1)

                def step(c, cv):
                    for f in range(3):
                        m, mv = 3 * c + f, 3 * cv + f
                        if 0 <= c < CHUNKS:
                            w = FEAT[f][1]
                            dve.wait_ge(silu, mv + 1)
                            dve.wait_ge(up, mv + 1)
                            wait(dve, alo, mv - 1)
                            dve.scalar_tensor_tensor(
                                act_f[m % 2][0:w], p_hg[(2 * m + 1) % 3][0:w], k.sb13[0:w, 1, f:f + 1],
                                sil[m % 2][0:w], ALU.add, ALU.mult).then_inc(aa, 1)
                        if 1 <= m <= 3 * CHUNKS:
                            g, w = (f - 1) % 3, FEAT[(f - 1) % 3][1]
                            dve.wait_ge(ahi, mv)
                            dve.tensor_tensor(al[0:w, g], act_f[(m - 1) % 2][0:w],
                                              ah[0:w, g].bitcast(F32), ALU.subtract
                                              ).then_inc(alo, 1)
                        if f == 1 and c < CHUNKS - 1:
                            r = (c + 1) % 2
                            dve.wait_ge(hi, cv + 2)
                            dve.tensor_tensor(xtl[r][:], p_x[:], xth[r][:].bitcast(F32),
                                              ALU.subtract).then_inc(lo, 1)
                        if f == 1 and c >= 1:
                            r = (c - 1) % 2
                            z = p_z[r][:].rearrange("p a (i n) -> p (a i) n", n=2 * D)
                            dve.wait_ge(down, 3 * cv)
                            dve.wait_ge(rx_ready[r], turn(c - 1, cv if isinstance(cv, int)
                                                          else cv - 1, r))
                            if c >= 3:
                                dve.wait_ge(stored[r], turn(c - 1, cv if isinstance(cv, int)
                                                            else cv - 1, r) - 16)
                            dve.scalar_tensor_tensor(rx[r][:], z[:, :, 0:D], 0.5, rx[r][:],
                                                     ALU.mult, ALU.add).then_inc(outh, 1)
                            dve.wait_ge(outh, cv)
                            dve.scalar_tensor_tensor(ro[r][:], z[:, :, D:2 * D], 0.5, rx[r][:],
                                                     ALU.mult, ALU.add).then_inc(outr, 1)
                steps(dve, step)

            @block.scalar
            def _(act):
                act.activation(wtop[:], r_.second[:], ACT.Exp).then_inc(exp2, 1)

                def step(c, cv):
                    for f in range(3):
                        m, mv = 3 * c + f, 3 * cv + f
                        if 0 <= c < CHUNKS:
                            w = FEAT[f][1]
                            act.wait_ge(up_h, mv + 1)
                            wait(act, aa, mv - 1)
                            act.activation(sil[m % 2][0:w], p_hg[2 * m % 3][0:w], ACT.Silu,
                                           bias=k.sb13[0:w, 0, f:f + 1]).then_inc(silu, 1)
                        if 1 <= m <= 3 * CHUNKS:
                            g, w = (f - 1) % 3, FEAT[(f - 1) % 3][1]
                            act.wait_ge(aa, mv)
                            wait(act, down, mv - 3)
                            act.activation(ah[0:w, g], act_f[(m - 1) % 2][0:w], ACT.Copy
                                           ).then_inc(ahi, 1)
                        if f == 1 and c < CHUNKS - 1:
                            r = (c + 1) % 2
                            act.wait_ge(xpose, cv + 2)
                            wait(act, up, 3 * cv)
                            act.activation(xth[r][:], p_x[:], ACT.Copy).then_inc(hi, 1)
                steps(act, step)

            @block.tensor
            def _(pe):
                def step(c, cv):
                    for f in range(3):
                        m, mv = 3 * c + f, 3 * cv + f
                        if 0 <= c < CHUNKS:
                            r = c % 2
                            o, w = FEAT[f]
                            if f == 0:
                                pe.wait_ge(lo, cv + 1)
                            for g in range(2):
                                if g == 0:
                                    wait(pe, aa, mv - 1)
                                else:
                                    wait(pe, silu, mv)
                                cols = slice(g * SH + o, g * SH + o + w)
                                parts = ((k.sw13h, xth), (k.sw13h, xtl), (k.sw13l, xth))
                                for q, (w_, x_) in enumerate(parts):
                                    last = pe.matmul(p_hg[(2 * m + g) % 3][0:w], w_[:, cols],
                                                     x_[r][:], start=q == 0, stop=q == 2)
                                last.then_inc((up_h, up)[g], 1)
                        if f == 0 and c < CHUNKS - 1:
                            r = (c + 1) % 2
                            pe.wait_ge(in_ready[r], turn(c + 1, cv if isinstance(cv, int)
                                                         else cv + 1, r))
                            wait(pe, lo, cv + 1)
                            for q in range(CHUNK):
                                last = pe.transpose(p_x[:, q * P:(q + 1) * P], xs_in[r][:, q],
                                                    k.ident[:])
                            last.then_inc(xpose, 1)
                        if 2 <= m <= 3 * CHUNKS + 1:
                            g = (f - 2) % 3
                            w = 97 if g == 2 else P
                            pe.wait_ge(alo, mv - 1)
                            if g == 0:
                                wait(pe, outr, cv - 1)
                            for q in range(CHUNK):
                                tok = slice(q * P, (q + 1) * P)
                                z, o = p_z[(m - 2) // 3 % 2][:, q // 2], (q % 2) * 2 * D
                                pe.matmul(z[:, o:o + 2 * D], ah[0:w, g, tok], k.sw2hl[0:w, g],
                                          start=g == 0 and q % 2 == 0, stop=False,
                                          skip_group_check=True)
                                last = pe.matmul(z[:, o:o + D], al[0:w, g, tok],
                                                 k.sw2hl[0:w, g, 0:D], start=False, stop=g == 2,
                                                 skip_group_check=True)
                            last.then_inc(down, 1)

                step(-1, -1)
                pe.wait_ge(tab_in, 1)
                for m, col in enumerate((which, at)):
                    pe.matmul(p_tab[0:1, m, 0:P], col[:, 0:1], k.ident[:], start=True, stop=True)
                    last = pe.matmul(p_tab[0:1, m, P:SLOT_TILES], col[:, 1:2],
                                     k.ident[:, 0:SLOT_TILES - P], start=True, stop=True)
                last.then_inc(tab_mm, 1)
                pe.wait_ge(tab_done, 1)
                steps(pe, step, first=0)


def experts(nc, k, sb, ps, n, xs, ys, beside=None):
    with phase(nc) as sem, ExitStack() as ctx:
        xin = [sb(f"e{n}_x{r}", [P, 2, ROW], ctx=ctx) for r in range(RING)]
        y = [sb(f"e{n}_y{r}", [P, 2, D], ctx=ctx) for r in range(RING)]
        xth = [sb(f"e{n}_xth{r}", [P, 2 * P], F32R, ctx) for r in range(2)]
        xtl = [sb(f"e{n}_xtl{r}", [P, 2 * P], F32R, ctx) for r in range(2)]
        sil = [sb(f"e{n}_sil{r}", [P, 2, INTER], ctx=ctx) for r in range(2)]
        a = [sb(f"e{n}_a{r}", [P, 2, INTER], ctx=ctx) for r in range(2)]
        ah = [sb(f"e{n}_ah{r}", [A0 + 1, 512], F32R, ctx) for r in range(2)]
        al = [sb(f"e{n}_al{r}", [A0 + 1, 512], F32R, ctx) for r in range(2)]
        p_x = ps(f"e{n}_px", [P, 512], ctx)
        p_u = [ps(f"e{n}_pu{r}", [P, 2, 512], ctx) for r in range(2)]
        p_a = ps(f"e{n}_pa", [P, 512], ctx)
        p_y = ps(f"e{n}_py", [P, 512], ctx)
        names = ("xpose", "xhi", "xlo", "up", "silu", "aa", "apose", "ahi", "alo", "down", "yhi",
                 "yy", "passed")
        (xpose, xhi, xlo, up, silu, aa, apose, ahi, alo, down, yhi, yy, passed) = (
            sem(f"e{n}_{s}") for s in names)
        brought = sem(f"e{n}_brought")
        x_in = [sem(f"e{n}_in{r}") for r in range(RING)]
        sent = [sem(f"e{n}_sent{r}") for r in range(RING)]
        rows = xs.rearrange("(j p) c -> p j c", p=P)
        LOOPED = (PAIRS - RING) // RING

        def steps(eng, step, last):
            for j in range(-1, 3):
                step(j, j)
            with eng.Fori(0, LOOPED) as i:
                for u in range(RING):
                    step(3 + u, RING * i + (3 + u))
            for j in range(3 + RING * LOOPED, last):
                step(j, j)

        with nc.Block() as block:
            @block.sync
            def _(sp):
                def load(first, free):
                    _, at = nc.values_load_multi_w_load_instructions(
                        k.tile_at[0:1, ds(first, 2 * RING)], engines=[mybir.EngineType.SP],
                        min_val=0, max_val=E * RTILES + E - 1,
                        skip_runtime_bounds_check_because="a tile of a region, or of the first "
                        "padding tiles: fewer than 16 tiles are left over")
                    for r in range(RING):
                        if free is not None:
                            sp.wait_ge(sent[r], free)
                        for t in range(2):
                            sp.dma_start(xin[r][:, t], rows[:, ds(at[2 * r + t], 1)].rearrange(
                                "p j c -> p (j c)")).then_inc(x_in[r], 16)
                load(0, None)
                if beside:
                    sp.dma_start(beside[0][:], beside[1]).then_inc(brought, 16)
                with sp.Fori(1, PAIRS // RING) as i:
                    load(2 * RING * i, 32 * i)
                if beside:
                    sp.wait_ge(brought, 16)

            @block.gpsimd
            def _(pool):
                with pool.Fori(0, PAIRS // RING) as i:
                    for r in range(RING):
                        pool.wait_ge(yy, RING * i + (r + 1))
                        pool.sem_inc(passed, 1)
                        for t in range(2):
                            pool.indirect_dma_start(
                                ys, bass.IndirectOffsetOnAxis(
                                    xin[r][:, t, D:D + 1].bitcast(I32), 0),
                                y[r][:, t, :], None).then_inc(sent[r], 16)
                for r in range(RING):
                    pool.wait_ge(sent[r], 32 * (PAIRS // RING))

            @block.vector
            def _(dve):
                for r in range(2):
                    dve.memset(ah[r][A0:A0 + 1].bitcast(F32), 1.0)
                    dve.memset(al[r][A0:A0 + 1].bitcast(F32), 0.0)

                def step(j, jv):
                    if j < PAIRS - 1:
                        r = (j + 1) % 2
                        dve.wait_ge(xhi, jv + 2)
                        dve.tensor_tensor(xtl[r][:], p_x[:, 0:2 * P], xth[r][:].bitcast(F32),
                                          ALU.subtract).then_inc(xlo, 1)
                    if 0 <= j < PAIRS:
                        r = j % 2
                        dve.wait_ge(silu, jv + 1)
                        wait(dve, apose, jv - 1)
                        dve.tensor_tensor(a[r][:], p_u[r][:, :, INTER:UP], sil[r][:], ALU.mult
                                          ).then_inc(aa, 1)
                    if 1 <= j < PAIRS + 1:
                        r = (j - 1) % 2
                        dve.wait_ge(ahi, jv)
                        dve.tensor_tensor(al[r][0:A0], p_a[0:A0], ah[r][0:A0].bitcast(F32),
                                          ALU.subtract).then_inc(alo, 1)
                    if 2 <= j:
                        s = (j - 2) % RING
                        dve.wait_ge(yhi, jv - 1)
                        for t in range(2):
                            last = dve.scalar_tensor_tensor(
                                y[s][:, t], p_y[:, t * 2 * D + D:(t + 1) * 2 * D],
                                xin[s][:, t, D + 1:D + 2], y[s][:, t], ALU.mult, ALU.add)
                        last.then_inc(yy, 1)
                steps(dve, step, PAIRS + 2)

            @block.scalar
            def _(act):
                def step(j, jv):
                    if j < PAIRS - 1:
                        r = (j + 1) % 2
                        act.wait_ge(xpose, jv + 2)
                        wait(act, up, jv)
                        act.activation(xth[r][:], p_x[:, 0:2 * P], ACT.Copy).then_inc(xhi, 1)
                    if 0 <= j < PAIRS:
                        r = j % 2
                        act.wait_ge(up, jv + 1)
                        wait(act, aa, jv - 1)
                        act.activation(sil[r][:], p_u[r][:, :, 0:INTER], ACT.Silu
                                       ).then_inc(silu, 1)
                    if 1 <= j < PAIRS + 1:
                        r = (j - 1) % 2
                        act.wait_ge(apose, jv)
                        wait(act, down, jv - 2)
                        act.activation(ah[r][0:A0], p_a[0:A0], ACT.Copy).then_inc(ahi, 1)
                    if 2 <= j:
                        s = (j - 2) % RING
                        act.wait_ge(down, jv - 1)
                        for t in range(2):
                            last = act.activation(
                                y[s][:, t], p_y[:, t * 2 * D:t * 2 * D + D], ACT.Copy,
                                scale=xin[s][:, t, D + 1:D + 2])
                        last.then_inc(yhi, 1)
                steps(act, step, PAIRS + 2)

            @block.tensor
            def _(pe):
                expert = {}

                def load_experts(first, pairs):
                    expert.clear()
                    _, got = nc.values_load_multi_w_load_instructions(
                        k.tile_expert[0:1, ds(2 * first, 2 * len(pairs))],
                        engines=[mybir.EngineType.PE], min_val=0, max_val=E - 1,
                        skip_runtime_bounds_check_because="a count of 16 compares, at most 15")
                    for q, j in enumerate(pairs):
                        expert[j] = got[2 * q:2 * q + 2]

                def step(j, jv):
                    if j < PAIRS - 1:
                        s = (j + 1) % RING
                        turns = (32 * ((j + 1) // RING + 1) if isinstance(jv, int)
                                 else 32 * ((jv + (1 - s)) // RING + 1))
                        pe.wait_ge(x_in[s], turns)
                        wait(pe, xlo, jv + 1)
                        for t in range(2):
                            last = pe.transpose(p_x[:, t * P:(t + 1) * P], xin[s][:, t, 0:D],
                                                k.ident[:])
                        last.then_inc(xpose, 1)
                    if 0 <= j < PAIRS:
                        r = j % 2
                        pe.wait_ge(xlo, jv + 1)
                        wait(pe, aa, jv - 1)
                        for t in range(2):
                            cols = ds(expert[j][t] * UP, UP)
                            tok = slice(t * P, (t + 1) * P)
                            o = p_u[r][:, t, 0:UP]
                            pe.matmul(o, k.onesr[:], k.b13[:, cols], start=True, stop=False)
                            pe.matmul(o, xth[r][:, tok], k.w13h[:, cols], start=False, stop=False)
                            pe.matmul(o, xth[r][:, tok], k.w13l[:, cols], start=False, stop=False)
                            last = pe.matmul(o, xtl[r][:, tok], k.w13h[:, cols], start=False,
                                             stop=True)
                        last.then_inc(up, 1)
                    if 1 <= j < PAIRS + 1:
                        r = (j - 1) % 2
                        pe.wait_ge(aa, jv)
                        wait(pe, alo, jv - 1)
                        for t in range(2):
                            for c, o in enumerate((0, A1)):
                                q = 2 * t + c
                                last = pe.transpose(p_a[0:A0, q * P:(q + 1) * P],
                                                    a[r][:, t, o:o + A0], k.ident[:])
                        last.then_inc(apose, 1)
                    if 2 <= j:
                        r = j % 2
                        pe.wait_ge(alo, jv - 1)
                        wait(pe, yy, jv - 2)
                        for t in range(2):
                            for c, rows_ in enumerate((A0 + 1, A0)):
                                q = slice((2 * t + c) * P, (2 * t + c + 1) * P)
                                w2 = k.w2hl[0:rows_, c, ds(expert[j - 2][t], 1)].rearrange(
                                    "p e n -> p (e n)")
                                o = t * 2 * D
                                pe.matmul(p_y[:, o:o + 2 * D], ah[r][0:rows_, q], w2,
                                          start=c == 0, stop=False, skip_group_check=True)
                                last = pe.matmul(p_y[:, o:o + D], al[r][0:rows_, q], w2[:, 0:D],
                                                 start=False, stop=c == 1, skip_group_check=True)
                        last.then_inc(down, 1)

                load_experts(0, [0, 1, 2])
                for j in range(-1, 3):
                    step(j, j)
                with pe.Fori(0, LOOPED) as i:
                    load_experts(RING * i + 1, list(range(1, 3 + RING)))
                    for u in range(RING):
                        step(3 + u, RING * i + (3 + u))
                tail = 3 + RING * LOOPED
                load_experts(tail - 2, list(range(tail - 2, PAIRS)))
                for j in range(tail, PAIRS + 2):
                    step(j, j)


def attention(nc, k, sb, ps, resid, ys, x3):
    with phase(nc) as sem, ExitStack() as ctx:
        def t2(name, shape, dt=F32):
            return [sb(f"t_{name}{r}", shape, dt, ctx) for r in range(2)]

        xa = sb("t_xa", [P, TILES, D], ctx=ctx)
        yt, xt = t2("yt", [P, GT, 2 * D]), t2("xt", [P, GT * P])
        xh = sb("t_xh", [P, GT, D], ctx=ctx)
        rs, nm = t2("rs", [P, GT]), t2("nm", [P, GT])
        st, mv = sb("t_st", [P, GT, 6], ctx=ctx), sb("t_mv", [P, GT, 2], ctx=ctx)
        ve = sb("t_ve", [P, GT], ctx=ctx)
        phq, rq = (sb(f"t_{s}", [P, GT * P], ctx=ctx) for s in ("phq", "rq"))
        ek = sb("t_ek", [P, 4, D], ctx=ctx)
        phk, v = t2("phk", [P, GT, D]), t2("v", [P, GT, D])
        kvt, kvp = sb("t_kvt", [P, D], ctx=ctx), sb("t_kvp", [P, D], ctx=ctx)
        p_t, p_q = ps("t_pt", [P, 2, 512], ctx), ps("t_pq", [P, 2, 512], ctx)
        p_kv = ps("t_pkv", [P, 2, 512], ctx)
        p_b, p_c = ps("t_pb", [P, 512], ctx), ps("t_pc", [P, 512], ctx)
        in_ready = [sem(f"t_in{r}") for r in range(2)]
        names = ("ysum", "x2r", "stats", "aggr", "var", "rstds", "nmr", "xhr", "xpose", "xtr",
                 "qmm", "mqr", "rqr", "eqr", "phqr", "kvmm", "mkr", "ekr", "phkr", "vtk", "kvtr",
                 "kvpmm", "kvpr", "omm", "x3r", "passed", "stored")
        s = {m: sem(f"t_{m}") for m in names}

        def steps(eng, step):
            for g in (-2, -1, 0, 1):
                step(g, g)
            with eng.Fori(0, 2) as i:
                step(2, 2 * i + 2)
                step(3, 2 * i + 3)
            for g in (6, 7, 8):
                step(g, g)

        def group(ap, gv):
            return ap[:, ds(gv, 1)].rearrange("p b i d -> p (b i) d")

        def tiles(gv):
            return xa[:, ds(gv * GT, GT)]

        k_of = p_kv[:].rearrange("p a (t n) -> p (a t) n", n=2 * D)[:, :, 0:D]
        v_of = p_kv[:].rearrange("p a (t n) -> p (a t) n", n=2 * D)[:, :, D:2 * D]
        q_of = p_q[:].rearrange("p a n -> p (a n)")

        with nc.Block() as block:
            @block.sync
            def _(sp):
                def load(g, gv):
                    sp.dma_start(tiles(gv), group(resid, gv)).then_inc(in_ready[g % 2], 16)
                    sp.dma_start(yt[g % 2][:], group(ys, gv)).then_inc(in_ready[g % 2], 16)

                def store(gv):
                    sp.wait_ge(s["x3r"], gv + 1)
                    sp.dma_start(group(x3, gv), tiles(gv)).then_inc(s["stored"], 16)

                def step(g, gv):
                    if g < 6:
                        wait(sp, s["x2r"], gv + 1)
                        load(g + 2, gv + 2)
                    if g >= 2:
                        store(gv - 2)
                steps(sp, step)
                store(GROUPS - 1)
                sp.wait_ge(s["stored"], 16 * GROUPS)

            @block.gpsimd
            def _(pool):
                def step(g, gv):
                    r = g % 2
                    if g < 6:
                        turns = 32 * ((g + 2) // 2 + 1) if isinstance(gv, int) else (
                            16 * (gv + 2 - r) + 32)
                        pool.wait_ge(in_ready[r], turns)
                        pool.tensor_tensor(yt[r][:, :, 0:D], yt[r][:, :, 0:D],
                                           yt[r][:, :, D:2 * D], ALU.add).then_inc(s["ysum"], 1)
                    if g < 6:
                        pool.wait_ge(s["var"], gv + 3)
                        wait(pool, s["xhr"], gv + 1)
                        pool.tensor_tensor(rs[r][:], ve[:], k.nhalf[:], ALU.pow
                                           ).then_inc(s["rstds"], 1)
                steps(pool, step)

            @block.vector
            def _(dve):
                def step(g, gv):
                    r = g % 2
                    if 0 <= g < 8:
                        dve.wait_ge(s["kvmm"], 2 * gv + 1)
                        dve.tensor_scalar(ek[:], k_of, 0.0, None, ALU.min).then_inc(s["mkr"], 1)
                    if g < 6:
                        x2 = tiles(gv + 2)
                        dve.wait_ge(s["ysum"], gv + 3)
                        dve.tensor_tensor(x2, x2, yt[r][:, :, 0:D], ALU.add
                                          ).then_inc(s["x2r"], 1)
                    if g >= 1:
                        dve.wait_ge(s["qmm"], gv)
                        wait(dve, s["omm"], gv - 1)
                        dve.tensor_scalar(phq[:], q_of, k.bq[:], 0.0, ALU.add, ALU.min
                                          ).then_inc(s["mqr"], 1)
                    if 0 <= g < 8:
                        dve.wait_ge(s["ekr"], 2 * gv + 1)
                        wait(dve, s["vtk"], gv - 1)
                        dve.scalar_tensor_tensor(phk[r][:, 0:4], k_of, 0.0, ek[:], ALU.max, ALU.add
                                                 ).then_inc(s["phkr"], 1)
                    if g >= 1:
                        dve.wait_ge(s["vtk"], gv)
                        wait(dve, s["kvpmm"], gv - 1)
                        dve.tensor_tensor(kvt[:], p_b[:, 0:D], k.blockdiag[:], ALU.mult
                                          ).then_inc(s["kvtr"], 1)
                    if g < 6:
                        dve.wait_ge(s["x2r"], gv + 3)
                        dve.sem_inc(s["passed"], 1)
                        for q in range(GT):
                            last = dve.bn_stats(st[:, q], x2[:, q])
                        last.then_inc(s["stats"], 1)
                    if g >= 1:
                        dve.wait_ge(s["eqr"], gv)
                        dve.tensor_tensor(phq[:], phq[:], rq[:], ALU.add).then_inc(s["phqr"], 1)
                    if 0 <= g < 8:
                        dve.wait_ge(s["kvmm"], 2 * gv + 2)
                        dve.wait_ge(s["phkr"], 2 * gv + 1)
                        dve.tensor_scalar(ek[:], k_of, 0.0, None, ALU.min).then_inc(s["mkr"], 1)
                    if g < 6:
                        dve.wait_ge(s["stats"], gv + 3)
                        dve.sem_inc(s["passed"], 1)
                        for q in range(GT):
                            last = dve.bn_aggr(mv[:, q], st[:, q])
                        last.then_inc(s["aggr"], 1)
                        dve.wait_ge(s["aggr"], gv + 3)
                        dve.tensor_scalar(ve[:], mv[:, :, 1], EPS, None, ALU.add
                                          ).then_inc(s["var"], 1)
                    if 0 <= g < 8:
                        dve.wait_ge(s["ekr"], 2 * gv + 2)
                        dve.scalar_tensor_tensor(phk[r][:, 4:8], k_of, 0.0, ek[:], ALU.max, ALU.add
                                                 ).then_inc(s["phkr"], 1)
                    if g >= 1:
                        dve.wait_ge(s["omm"], gv)
                        x3_ = tiles(gv - 1)
                        dve.tensor_tensor(x3_, p_q[:].rearrange("p a (t n) -> p (a t) n", n=D),
                                          x3_, ALU.add).then_inc(s["x3r"], 1)
                    if g < 6:
                        dve.wait_ge(s["rstds"], gv + 3)
                        dve.scalar_tensor_tensor(nm[r][:], mv[:, :, 0], -1.0, rs[r][:], ALU.mult,
                                                 ALU.mult).then_inc(s["nmr"], 1)
                steps(dve, step)

            @block.scalar
            def _(act):
                def step(g, gv):
                    r = g % 2

                    def v_and_exp(h):
                        act.wait_ge(s["mkr"], 2 * gv + h + 1)
                        if h == 0:
                            wait(act, s["vtk"], gv - 1)
                        act.activation(v[r][:, 4 * h:4 * h + 4], v_of, ACT.Copy)
                        act.activation(ek[:], ek[:], ACT.Exp).then_inc(s["ekr"], 1)
                    if 0 <= g < 8:
                        v_and_exp(0)
                    if g >= 1:
                        act.wait_ge(s["mqr"], gv)
                        wait(act, s["phqr"], gv - 1)
                        act.activation(rq[:], q_of, ACT.Relu, bias=k.bq[:]
                                       ).then_inc(s["rqr"], 1)
                        act.activation(phq[:], phq[:], ACT.Exp).then_inc(s["eqr"], 1)
                        act.wait_ge(s["kvpmm"], gv)
                        wait(act, s["omm"], gv - 1)
                        act.activation(kvp[:], p_c[:, 0:D], ACT.Copy).then_inc(s["kvpr"], 1)
                    if -1 <= g < 7:
                        act.wait_ge(s["xpose"], gv + 2)
                        act.activation(xt[(g + 1) % 2][:], p_t[:].rearrange("p a n -> p (a n)"),
                                       ACT.Copy).then_inc(s["xtr"], 1)
                    if 0 <= g < 8:
                        v_and_exp(1)
                    if g < 6:
                        act.wait_ge(s["nmr"], gv + 3)
                        wait(act, s["xpose"], gv + 2)
                        x2 = tiles(gv + 2)
                        for q in range(GT):
                            last = act.activation(xh[:, q], x2[:, q], ACT.Identity,
                                                  bias=nm[r][:, q:q + 1],
                                                  scale=rs[r][:, q:q + 1])
                        last.then_inc(s["xhr"], 1)
                steps(act, step)

            @block.tensor
            def _(pe):
                def step(g, gv):
                    r = g % 2

                    def kv(h):
                        for q in range(4):
                            o = p_kv[:, q // 2, (q % 2) * 2 * D:(q % 2 + 1) * 2 * D]
                            i = 4 * h + q
                            pe.matmul(o, xt[r][:, i * P:(i + 1) * P], k.wkv[:], start=True,
                                      stop=False)
                            last = pe.matmul(o, k.onesr[:], k.bkvp[:, 0:2 * D], start=False,
                                             stop=True)
                        last.then_inc(s["kvmm"], 1)
                    if 0 <= g < 8:
                        pe.wait_ge(s["xtr"], gv + 1)
                        wait(pe, s["phkr"], 2 * gv)
                        kv(0)
                    if g >= 1:
                        wait(pe, s["x3r"], gv - 1)
                        for h in range(2):
                            last = pe.matmul(p_q[:, h], k.wq[:],
                                             xt[(g - 1) % 2][:, h * 512:(h + 1) * 512],
                                             start=True, stop=True)
                        last.then_inc(s["qmm"], 1)
                    if g >= 1:
                        pe.wait_ge(s["phkr"], 2 * gv)
                        wait(pe, s["kvtr"], gv - 1)
                        for q in range(GT):
                            last = pe.matmul(p_b[:, 0:D], v[(g - 1) % 2][:, q],
                                             phk[(g - 1) % 2][:, q], start=q == 0,
                                             stop=q == GT - 1)
                        last.then_inc(s["vtk"], 1)
                    if -1 <= g < 7:
                        pe.wait_ge(s["xhr"], gv + 2)
                        wait(pe, s["xtr"], gv + 1)
                        for q in range(GT):
                            last = pe.transpose(p_t[:, q // 4, (q % 4) * P:(q % 4 + 1) * P],
                                                xh[:, q], k.ident[:])
                        last.then_inc(s["xpose"], 1)
                    if g >= 1:
                        pe.wait_ge(s["kvtr"], gv)
                        wait(pe, s["kvpr"], gv - 1)
                        pe.matmul(p_c[:, 0:D], kvt[:], k.wp[:], start=True, stop=True
                                  ).then_inc(s["kvpmm"], 1)
                    if 0 <= g < 8:
                        pe.wait_ge(s["phkr"], 2 * gv + 1)
                        kv(1)
                    if g >= 1:
                        pe.wait_ge(s["kvpr"], gv)
                        pe.wait_ge(s["rqr"], gv)
                        pe.wait_ge(s["phqr"], gv)
                        for h in range(2):
                            pe.matmul(p_q[:, h], k.onesr[:], k.bkvp[:, 2 * D:6 * D], start=True,
                                      stop=False, skip_group_check=True)
                            for q in range(4):
                                i = 4 * h + q
                                last = pe.matmul(p_q[:, h, q * D:(q + 1) * D],
                                                 phq[:, i * P:(i + 1) * P], kvp[:], start=False,
                                                 stop=True, skip_group_check=True)
                        last.then_inc(s["omm"], 1)
                steps(pe, step)


def combine(nc, k, sb, rs, ys, out):
    with phase(nc) as sem, ExitStack() as ctx:
        yt = [sb(f"c_yt{r}", [P, GT, 2 * D], ctx=ctx) for r in range(4)]
        in_ready = [sem(f"c_in{r}") for r in range(GROUPS)]
        half, ysum, stored = sem("c_half"), sem("c_ysum"), sem("c_stored")
        with nc.Block() as block:
            @block.sync
            def _(sp):
                for g in range(GROUPS):
                    if g >= 4:
                        sp.wait_ge(ysum, g - 3)
                    sp.dma_start(yt[g % 4][:], ys[:, g]).then_inc(in_ready[g], 16)
                sp.wait_ge(stored, 16 * GROUPS)

            @block.vector
            def _(dve):
                for g in range(GROUPS):
                    dve.wait_ge(in_ready[g], 16)
                    dve.tensor_tensor(rs[:, g], rs[:, g], yt[g % 4][:, :, 0:D], ALU.add
                                      ).then_inc(half, 1)
                    dve.wait_ge(half, g + 1)
                    dve.tensor_tensor(rs[:, g], rs[:, g], yt[g % 4][:, :, D:2 * D], ALU.add
                                      ).then_inc(ysum, 1)

            @block.scalar
            def _(act):
                for g in range(GROUPS):
                    act.wait_ge(ysum, g + 1)
                    act.dma_start(out[:, g], rs[:, g]).then_inc(stored, 16)


INS = ["attn_x", "attn_Wq", "attn_bq", "attn_Wk", "attn_bk", "attn_Wv", "attn_bv", "attn_Wp",
       "attn_bp", "ffn_gate_w", "ffn_gate_b", "ffn_w1", "ffn_b1", "ffn_w3", "ffn_b3", "ffn_w2",
       "ffn_b2", "ffn_sw1", "ffn_sb1", "ffn_sw3", "ffn_sb3", "ffn_sw2", "ffn_sb2"]


def kernel(**inputs):
    import numpy as np
    import concourse.bacc as bacc
    from concourse.bass_utils import run_bass_kernel_spmd

    nc = bacc.Bacc("TRN2", target_bir_lowering=False, num_devices=1)
    arrays, args = {}, []
    for name in INS:
        a = np.ascontiguousarray(inputs["L0_" + name])
        arrays["in_" + name] = a
        args.append(nc.dram_tensor("in_" + name, a.shape, mybir.dt.from_np(a.dtype),
                                   kind="ExternalInput").ap())
    shape = [GROUPS, GT * P, D]
    args.append(nc.dram_tensor("out", shape, F32, kind="ExternalOutput").ap())
    xs = nc.dram_tensor("xs", [XS_ROWS, ROW], F32).ap()
    ys = nc.dram_tensor("ys", [TOKENS * K_TOP + PADS * P, D], F32).ap()
    resid = nc.dram_tensor("resid", shape, F32).ap()
    x3 = nc.dram_tensor("x3", shape, F32).ap()
    build(nc, *args, xs, ys, resid, x3)
    r = run_bass_kernel_spmd(nc, [arrays], core_ids=[0])
    return r.results[0]["out"]
```
